# Optimizing a Trainium2 kernel written in Bass

```python
import numpy as np
import jax
import jax.numpy as jnp

def _softmax(x, axis=-1):
    return jax.nn.softmax(x, axis=axis)

def _gelu(x):
    return jax.nn.gelu(x, approximate=True)

def _silu(x):
    return jax.nn.silu(x)

def _sigmoid(x):
    return jax.nn.sigmoid(x)

def _layernorm(x, axis=-1, eps=1e-05):
    m = jnp.mean(x, axis=axis, keepdims=True)
    v = jnp.var(x, axis=axis, keepdims=True)
    return (x - m) / jnp.sqrt(v + eps)

def _scatter_add(tgt, idx, src, axis=0):
    return tgt.at[idx].add(src)

def _segment_sum(src, seg, n):
    return jax.ops.segment_sum(src, seg, n)
kernel_name = 'mk_xattn_ffn_d4_seqx_r4_be12f2'

def setup_inputs(seed: int=0):
    np.random.seed(seed)
    _w = jnp.asarray

    def _rec_inputs():
        import jax
        import jax.numpy as jnp
        _rk = jax.random.key(seed)
        x = -0.0002928 + 1 * jax.random.normal(jax.random.fold_in(_rk, 1), (32, 128, 256), jnp.float32)
        _lenS = 128 - jax.random.randint(jax.random.fold_in(_rk, 7), (32,), 0, max(1, 128 // 4) + 1, jnp.int32)
        _lenS2 = 128 - jax.random.randint(jax.random.fold_in(_rk, 8), (32,), 0, max(1, 128 // 4) + 1, jnp.int32)
        _ctx_1024P = jax.random.normal(jax.random.fold_in(_rk, 11), (32, 16, 256), jnp.float32)
        _ctx_1024c = jax.random.dirichlet(jax.random.fold_in(_rk, 511), 0.3 * jnp.ones((16,), jnp.float32), (32, 128))
        _ctx_1024t = jnp.einsum('bsk,bkd->bsd', _ctx_1024c, _ctx_1024P)
        _ctx_1024t = _ctx_1024t * jax.lax.rsqrt(jnp.mean(jnp.square(_ctx_1024t)) + 1e-12) * 0.953939
        ctx_1024 = -1.52775e-05 + 0.999936 * (_ctx_1024t + 0.3 * jax.random.normal(jax.random.fold_in(_rk, 611), (32, 128, 256), jnp.float32))
        _validS = jnp.arange(128)[None, :] < _lenS[:, None]
        _validS2 = jnp.arange(128)[None, :] < _lenS2[:, None]
        _causal = jnp.tril(jnp.ones((128, 128), dtype=bool))
        mask_Bx1xSxS_ik0 = jnp.where(jnp.broadcast_to(_validS[:, None, None, :], (32, 1, 128, 128)), 0, 1).astype(jnp.int32)
        mask_Bx1x1xS2_if1 = jnp.where(jnp.ones((32, 1, 1, 128), dtype=bool), 1, 0).astype(jnp.int32)
        mask_1x1xSxS2_bk0 = jnp.logical_not(jnp.broadcast_to(_validS2[0:1, None, None, :], (1, 1, 128, 128)))
        return (x, ctx_1024, mask_Bx1xSxS_ik0, mask_Bx1x1xS2_if1, mask_1x1xSxS2_bk0)
    x, ctx_1024, mask_Bx1xSxS_ik0, mask_Bx1x1xS2_if1, mask_1x1xSxS2_bk0 = _rec_inputs()

    def _L0_xattn_setup():
        import jax, jax.numpy as jnp
        import numpy as np
        B, TQ, TK, DM, H, FF, STRIDE = (4, 256, 2048, 256, 16, 1024, 16)
        DH = DM // H
        J = TK // STRIDE
        NEG = -1000000000.0

        def _layer_norm(x, g, b, eps=1e-06):
            m = x.mean(-1, keepdims=True)
            v = ((x - m) ** 2).mean(-1, keepdims=True)
            return g * (x - m) / jnp.sqrt(v + eps) + b

        def _full_attn(q, k, v, mask, wq, bq, wk, bk, wv, bv, wo, bo):
            b_, tq, _ = q.shape
            tk = k.shape[1]
            Q = (q @ wq + bq).reshape(b_, tq, H, DH)
            K = (k @ wk + bk).reshape(b_, tk, H, DH)
            V = (v @ wv + bv).reshape(b_, tk, H, DH)
            scores = jnp.einsum('bqhd,bkhd->bhqk', Q, K) / np.sqrt(DH).astype(np.float32)
            scores = jnp.where(mask == 0, NEG, scores)
            attn = jax.nn.softmax(scores, axis=-1)
            out = jnp.einsum('bhqk,bkhd->bqhd', attn, V).reshape(b_, tq, DM)
            return out @ wo + bo

        def _hepos_attn(q, k, v, src_mask, wq, bq, wk, bk, wv, bv, wo, bo):
            b_, tq, _ = q.shape
            tk = k.shape[1]
            Q = (q @ wq + bq).reshape(b_, tq, H, DH)
            K = (k @ wk + bk).reshape(b_, tk, H, DH)
            V = (v @ wv + bv).reshape(b_, tk, H, DH)
            idx = jnp.arange(H)[:, None] + STRIDE * jnp.arange(J)[None, :]
            hsel = jnp.arange(H)[:, None]
            Kh = K[:, idx, hsel, :]
            Vh = V[:, idx, hsel, :]
            scores = jnp.einsum('bqhd,bhjd->bhqj', Q, Kh) / np.sqrt(DH).astype(np.float32)
            mask_h = src_mask[:, 0, 0, :][:, idx][:, :, None, :]
            scores = jnp.where(mask_h == 0, NEG, scores)
            attn = jax.nn.softmax(scores, axis=-1)
            out = jnp.einsum('bhqj,bhjd->bqhd', attn, Vh).reshape(b_, tq, DM)
            return out @ wo + bo
        key = jax.random.key(seed)
        ks = jax.random.split(key, 16)
        lin = lambda k, din, dout: jax.random.normal(k, (din, dout), jnp.float32) / np.sqrt(din).astype(np.float32)
        inp = {'x': jax.random.normal(ks[0], (B, TQ, DM), jnp.float32), 'enc': jax.random.normal(ks[1], (B, TK, DM), jnp.float32), 'trg_mask': jnp.broadcast_to(jnp.tril(jnp.ones((TQ, TQ), jnp.int32))[None, None], (B, 1, TQ, TQ)), 'src_mask': jnp.ones((B, 1, 1, TK), jnp.int32), 'sa_wq': lin(ks[2], DM, DM), 'sa_bq': jnp.zeros((DM,), jnp.float32), 'sa_wk': lin(ks[3], DM, DM), 'sa_bk': jnp.zeros((DM,), jnp.float32), 'sa_wv': lin(ks[4], DM, DM), 'sa_bv': jnp.zeros((DM,), jnp.float32), 'sa_wo': lin(ks[5], DM, DM), 'sa_bo': jnp.zeros((DM,), jnp.float32), 'ca_wq': lin(ks[6], DM, DM), 'ca_bq': jnp.zeros((DM,), jnp.float32), 'ca_wk': lin(ks[7], DM, DM), 'ca_bk': jnp.zeros((DM,), jnp.float32), 'ca_wv': lin(ks[8], DM, DM), 'ca_bv': jnp.zeros((DM,), jnp.float32), 'ca_wo': lin(ks[9], DM, DM), 'ca_bo': jnp.zeros((DM,), jnp.float32), 'ffn_w1': lin(ks[10], DM, FF), 'ffn_b1': jnp.zeros((FF,), jnp.float32), 'ffn_w2': lin(ks[11], FF, DM), 'ffn_b2': jnp.zeros((DM,), jnp.float32), 'ln1_g': jnp.ones((DM,), jnp.float32), 'ln1_b': jnp.zeros((DM,), jnp.float32), 'ln2_g': jnp.ones((DM,), jnp.float32), 'ln2_b': jnp.zeros((DM,), jnp.float32), 'ln3_g': jnp.ones((DM,), jnp.float32), 'ln3_b': jnp.zeros((DM,), jnp.float32)}
        return inp
    _L0_xattn_all = _L0_xattn_setup()
    _L0_xattn_in = {k: v for k, v in _L0_xattn_all.items() if k in ('sa_wq', 'sa_bq', 'sa_wk', 'sa_bk', 'sa_wv', 'sa_bv', 'sa_wo', 'sa_bo', 'ca_wq', 'ca_bq', 'ca_wk', 'ca_bk', 'ca_wv', 'ca_bv', 'ca_wo', 'ca_bo', 'ffn_w1', 'ffn_b1', 'ffn_w2', 'ffn_b2', 'ln1_g', 'ln1_b', 'ln2_g', 'ln2_b', 'ln3_g', 'ln3_b')}
    del _L0_xattn_all

    def _L0_ffn_setup():
        import jax, jax.numpy as jnp
        import numpy as np
        D = 256
        FF = 4 * D
        E = 8
        TOP_K = 2
        B, S = (4, 1024)
        key = jax.random.key(seed)
        ks = jax.random.split(key, 8)
        x = jax.random.normal(ks[0], (B, S, D), dtype=jnp.float32)
        Wg = jax.random.normal(ks[1], (D, E), dtype=jnp.float32) * 0.02
        bg = jnp.zeros((E,), dtype=jnp.float32)
        W1 = jax.random.normal(ks[2], (E, D, FF), dtype=jnp.float32) * 0.02
        b1 = jnp.zeros((E, FF), dtype=jnp.float32)
        W2 = jax.random.normal(ks[3], (E, FF, D), dtype=jnp.float32) * 0.02
        b2 = jnp.zeros((E, D), dtype=jnp.float32)
        return {'x': x, 'Wg': Wg, 'bg': bg, 'W1': W1, 'b1': b1, 'W2': W2, 'b2': b2}
    _L0_ffn_all = _L0_ffn_setup()
    _L0_ffn_in = {k: v for k, v in _L0_ffn_all.items() if k in ('Wg', 'bg', 'W1', 'b1', 'W2', 'b2')}
    del _L0_ffn_all

    def _L1_xattn_setup():
        import jax, jax.numpy as jnp
        import numpy as np
        D_MODEL = 256
        key = jax.random.key(seed)
        ks = jax.random.split(key, 11)
        B, Sq, Skv, D = (16, 512, 512, D_MODEL)
        s = 1.0 / np.sqrt(D)
        return {'q': jax.random.normal(ks[0], (B, Sq, D), jnp.float32), 'k': jax.random.normal(ks[1], (B, Skv, D), jnp.float32), 'v': jax.random.normal(ks[2], (B, Skv, D), jnp.float32), 'Wq': jax.random.normal(ks[3], (D, D), jnp.float32) * s, 'bq': jnp.zeros((D,), jnp.float32), 'Wk': jax.random.normal(ks[4], (D, D), jnp.float32) * s, 'bk': jnp.zeros((D,), jnp.float32), 'Wv': jax.random.normal(ks[5], (D, D), jnp.float32) * s, 'bv': jnp.zeros((D,), jnp.float32), 'Wo': jax.random.normal(ks[6], (D, D), jnp.float32) * s, 'bo': jnp.zeros((D,), jnp.float32)}
    _L1_xattn_all = _L1_xattn_setup()
    _L1_xattn_in = {k: v for k, v in _L1_xattn_all.items() if k in ('Wq', 'bq', 'Wk', 'bk', 'Wv', 'bv', 'Wo', 'bo')}
    del _L1_xattn_all

    def _L1_ffn_setup():
        import jax, jax.numpy as jnp
        import numpy as np
        BITS = 8
        LORA_RANK = 16
        LORA_ALPHA = 32
        SCALING = LORA_ALPHA / LORA_RANK

        def fake_quant_weight(w, bits=BITS):
            qmax = 2.0 ** (bits - 1) - 1
            scale = jnp.max(jnp.abs(w)) / qmax
            wq = jnp.clip(jnp.round(w / scale), -qmax - 1, qmax) * scale
            return w + jax.lax.stop_gradient(wq - w)

        def qat_lora_linear(x, W, b, A, B):
            Wq = fake_quant_weight(W)
            base = jnp.einsum('bsi,oi->bso', x, Wq) + b
            lora = jnp.einsum('bsr,or->bso', jnp.einsum('bsi,ri->bsr', x, A), B)
            return base + SCALING * lora
        key = jax.random.key(seed)
        ks = jax.random.split(key, 9)
        d, f = (256, 1024)
        s_in = 1.0 / np.sqrt(d)
        s_ff = 1.0 / np.sqrt(f)
        return {'hidden_states': jax.random.normal(ks[0], (4, 512, d), jnp.float32), 'W_fc': jax.random.normal(ks[1], (f, d), jnp.float32) * s_in, 'b_fc': jnp.zeros((f,), jnp.float32), 'A_fc': jax.random.normal(ks[2], (LORA_RANK, d), jnp.float32) * s_in, 'B_fc': jnp.zeros((f, LORA_RANK), jnp.float32), 'W_proj': jax.random.normal(ks[3], (d, f), jnp.float32) * s_ff, 'b_proj': jnp.zeros((d,), jnp.float32), 'A_proj': jax.random.normal(ks[4], (LORA_RANK, f), jnp.float32) * s_ff, 'B_proj': jnp.zeros((d, LORA_RANK), jnp.float32)}
    _L1_ffn_all = _L1_ffn_setup()
    _L1_ffn_in = {k: v for k, v in _L1_ffn_all.items() if k in ('W_fc', 'b_fc', 'A_fc', 'B_fc', 'W_proj', 'b_proj', 'A_proj', 'B_proj')}
    del _L1_ffn_all

    def _L2_xattn_setup():
        import jax, jax.numpy as jnp
        import numpy as np
        D_MODEL = 256
        NUM_HEADS = 16
        HEAD_DIM = D_MODEL // NUM_HEADS
        key = jax.random.key(seed)
        kq, kk, kv, k1, k2, k3, k4 = jax.random.split(key, 7)
        B, S = (4, 512)
        scale = 1.0 / np.sqrt(D_MODEL)
        return {'q': jax.random.normal(kq, (B, S, D_MODEL), jnp.float32), 'k': jax.random.normal(kk, (B, S, D_MODEL), jnp.float32), 'v': jax.random.normal(kv, (B, S, D_MODEL), jnp.float32), 'mask': jnp.tril(jnp.ones((S, S), jnp.bool_))[None, None, :, :], 'W_q': jax.random.normal(k1, (D_MODEL, D_MODEL), jnp.float32) * scale, 'W_k': jax.random.normal(k2, (D_MODEL, D_MODEL), jnp.float32) * scale, 'W_v': jax.random.normal(k3, (D_MODEL, D_MODEL), jnp.float32) * scale, 'W_o': jax.random.normal(k4, (D_MODEL, D_MODEL), jnp.float32) * scale}
    _L2_xattn_all = _L2_xattn_setup()
    _L2_xattn_in = {k: v for k, v in _L2_xattn_all.items() if k in ('W_q', 'W_k', 'W_v', 'W_o')}
    del _L2_xattn_all

    def _L2_ffn_setup():
        import jax, jax.numpy as jnp
        import numpy as np
        NUM_EXPERTS = 8
        CAPACITY = 160
        key = jax.random.key(seed)
        ks = jax.random.split(key, 5)
        D, E, F = (256, NUM_EXPERTS, 1024)
        inputs = jax.random.normal(ks[0], (2, 512, D), dtype=jnp.float32)
        gate_w = jax.random.normal(ks[1], (D, E), dtype=jnp.float32) * 0.02
        gate_b = jnp.zeros((E,), dtype=jnp.float32)
        w1 = jax.random.normal(ks[2], (E, D, F), dtype=jnp.float32) * 0.02
        b1 = jnp.zeros((E, F), dtype=jnp.float32)
        w2 = jax.random.normal(ks[3], (E, F, D), dtype=jnp.float32) * 0.02
        b2 = jnp.zeros((E, D), dtype=jnp.float32)
        return {'inputs': inputs, 'gate_w': gate_w, 'gate_b': gate_b, 'w1': w1, 'b1': b1, 'w2': w2, 'b2': b2}
    _L2_ffn_all = _L2_ffn_setup()
    _L2_ffn_in = {k: v for k, v in _L2_ffn_all.items() if k in ('gate_w', 'gate_b', 'w1', 'b1', 'w2', 'b2')}
    del _L2_ffn_all

    def _L3_xattn_setup():
        import jax, jax.numpy as jnp
        import numpy as np
        B, L, D, H = (4, 512, 256, 16)
        HD = D // H
        key = jax.random.key(seed)
        k1, k2, k3, k4 = jax.random.split(key, 4)
        return {'Q': jax.random.normal(k1, (B, L, D), dtype=jnp.float32), 'K': jax.random.normal(k2, (B, L, D), dtype=jnp.float32), 'V': jax.random.normal(k3, (B, L, D), dtype=jnp.float32), 'W_out': jax.random.normal(k4, (D, D), dtype=jnp.float32) * (1.0 / np.sqrt(D)), 'b_out': jnp.zeros((D,), dtype=jnp.float32)}
    _L3_xattn_all = _L3_xattn_setup()
    _L3_xattn_in = {k: v for k, v in _L3_xattn_all.items() if k in ('W_out', 'b_out')}
    del _L3_xattn_all

    def _L3_ffn_setup():
        import jax, jax.numpy as jnp
        import numpy as np
        E = 64
        K = 6
        CAP = 128
        ROUTE_SCALE = 1.0
        key = jax.random.key(seed)
        ks = jax.random.split(key, 9)
        B, S, D, I = (2, 256, 256, 176)
        SI = 2 * I
        s = 0.02
        return {'x': jax.random.normal(ks[0], (B, S, D), jnp.float32), 'gate_w': jax.random.normal(ks[1], (E, D), jnp.float32) * s, 'gate_b': jnp.zeros((E,), jnp.float32), 'w1': jax.random.normal(ks[2], (E, I, D), jnp.float32) * s, 'w2': jax.random.normal(ks[3], (E, D, I), jnp.float32) * s, 'w3': jax.random.normal(ks[4], (E, I, D), jnp.float32) * s, 'ws1': jax.random.normal(ks[5], (SI, D), jnp.float32) * s, 'ws2': jax.random.normal(ks[6], (D, SI), jnp.float32) * s, 'ws3': jax.random.normal(ks[7], (SI, D), jnp.float32) * s}
    _L3_ffn_all = _L3_ffn_setup()
    _L3_ffn_in = {k: v for k, v in _L3_ffn_all.items() if k in ('gate_w', 'gate_b', 'w1', 'w2', 'w3', 'ws1', 'ws2', 'ws3')}
    del _L3_ffn_all
    return {'x': x, 'ctx_1024': ctx_1024, 'mask_Bx1xSxS_ik0': mask_Bx1xSxS_ik0, 'mask_Bx1x1xS2_if1': mask_Bx1x1xS2_if1, 'mask_1x1xSxS2_bk0': mask_1x1xSxS2_bk0, 'L0_xattn_sa_wq': _L0_xattn_in['sa_wq'], 'L0_xattn_sa_bq': _L0_xattn_in['sa_bq'], 'L0_xattn_sa_wk': _L0_xattn_in['sa_wk'], 'L0_xattn_sa_bk': _L0_xattn_in['sa_bk'], 'L0_xattn_sa_wv': _L0_xattn_in['sa_wv'], 'L0_xattn_sa_bv': _L0_xattn_in['sa_bv'], 'L0_xattn_sa_wo': _L0_xattn_in['sa_wo'], 'L0_xattn_sa_bo': _L0_xattn_in['sa_bo'], 'L0_xattn_ca_wq': _L0_xattn_in['ca_wq'], 'L0_xattn_ca_bq': _L0_xattn_in['ca_bq'], 'L0_xattn_ca_wk': _L0_xattn_in['ca_wk'], 'L0_xattn_ca_bk': _L0_xattn_in['ca_bk'], 'L0_xattn_ca_wv': _L0_xattn_in['ca_wv'], 'L0_xattn_ca_bv': _L0_xattn_in['ca_bv'], 'L0_xattn_ca_wo': _L0_xattn_in['ca_wo'], 'L0_xattn_ca_bo': _L0_xattn_in['ca_bo'], 'L0_xattn_ffn_w1': _L0_xattn_in['ffn_w1'], 'L0_xattn_ffn_b1': _L0_xattn_in['ffn_b1'], 'L0_xattn_ffn_w2': _L0_xattn_in['ffn_w2'], 'L0_xattn_ffn_b2': _L0_xattn_in['ffn_b2'], 'L0_xattn_ln1_g': _L0_xattn_in['ln1_g'], 'L0_xattn_ln1_b': _L0_xattn_in['ln1_b'], 'L0_xattn_ln2_g': _L0_xattn_in['ln2_g'], 'L0_xattn_ln2_b': _L0_xattn_in['ln2_b'], 'L0_xattn_ln3_g': _L0_xattn_in['ln3_g'], 'L0_xattn_ln3_b': _L0_xattn_in['ln3_b'], 'L0_ffn_Wg': _L0_ffn_in['Wg'], 'L0_ffn_bg': _L0_ffn_in['bg'], 'L0_ffn_W1': _L0_ffn_in['W1'], 'L0_ffn_b1': _L0_ffn_in['b1'], 'L0_ffn_W2': _L0_ffn_in['W2'], 'L0_ffn_b2': _L0_ffn_in['b2'], 'L1_xattn_Wq': _L1_xattn_in['Wq'], 'L1_xattn_bq': _L1_xattn_in['bq'], 'L1_xattn_Wk': _L1_xattn_in['Wk'], 'L1_xattn_bk': _L1_xattn_in['bk'], 'L1_xattn_Wv': _L1_xattn_in['Wv'], 'L1_xattn_bv': _L1_xattn_in['bv'], 'L1_xattn_Wo': _L1_xattn_in['Wo'], 'L1_xattn_bo': _L1_xattn_in['bo'], 'L1_ffn_W_fc': _L1_ffn_in['W_fc'], 'L1_ffn_b_fc': _L1_ffn_in['b_fc'], 'L1_ffn_A_fc': _L1_ffn_in['A_fc'], 'L1_ffn_B_fc': _L1_ffn_in['B_fc'], 'L1_ffn_W_proj': _L1_ffn_in['W_proj'], 'L1_ffn_b_proj': _L1_ffn_in['b_proj'], 'L1_ffn_A_proj': _L1_ffn_in['A_proj'], 'L1_ffn_B_proj': _L1_ffn_in['B_proj'], 'L2_xattn_W_q': _L2_xattn_in['W_q'], 'L2_xattn_W_k': _L2_xattn_in['W_k'], 'L2_xattn_W_v': _L2_xattn_in['W_v'], 'L2_xattn_W_o': _L2_xattn_in['W_o'], 'L2_ffn_gate_w': _L2_ffn_in['gate_w'], 'L2_ffn_gate_b': _L2_ffn_in['gate_b'], 'L2_ffn_w1': _L2_ffn_in['w1'], 'L2_ffn_b1': _L2_ffn_in['b1'], 'L2_ffn_w2': _L2_ffn_in['w2'], 'L2_ffn_b2': _L2_ffn_in['b2'], 'L3_xattn_W_out': _L3_xattn_in['W_out'], 'L3_xattn_b_out': _L3_xattn_in['b_out'], 'L3_ffn_gate_w': _L3_ffn_in['gate_w'], 'L3_ffn_gate_b': _L3_ffn_in['gate_b'], 'L3_ffn_w1': _L3_ffn_in['w1'], 'L3_ffn_w2': _L3_ffn_in['w2'], 'L3_ffn_w3': _L3_ffn_in['w3'], 'L3_ffn_ws1': _L3_ffn_in['ws1'], 'L3_ffn_ws2': _L3_ffn_in['ws2'], 'L3_ffn_ws3': _L3_ffn_in['ws3']}

def reference(x, ctx_1024, mask_Bx1xSxS_ik0, mask_Bx1x1xS2_if1, mask_1x1xSxS2_bk0, L0_xattn_sa_wq, L0_xattn_sa_bq, L0_xattn_sa_wk, L0_xattn_sa_bk, L0_xattn_sa_wv, L0_xattn_sa_bv, L0_xattn_sa_wo, L0_xattn_sa_bo, L0_xattn_ca_wq, L0_xattn_ca_bq, L0_xattn_ca_wk, L0_xattn_ca_bk, L0_xattn_ca_wv, L0_xattn_ca_bv, L0_xattn_ca_wo, L0_xattn_ca_bo, L0_xattn_ffn_w1, L0_xattn_ffn_b1, L0_xattn_ffn_w2, L0_xattn_ffn_b2, L0_xattn_ln1_g, L0_xattn_ln1_b, L0_xattn_ln2_g, L0_xattn_ln2_b, L0_xattn_ln3_g, L0_xattn_ln3_b, L0_ffn_Wg, L0_ffn_bg, L0_ffn_W1, L0_ffn_b1, L0_ffn_W2, L0_ffn_b2, L1_xattn_Wq, L1_xattn_bq, L1_xattn_Wk, L1_xattn_bk, L1_xattn_Wv, L1_xattn_bv, L1_xattn_Wo, L1_xattn_bo, L1_ffn_W_fc, L1_ffn_b_fc, L1_ffn_A_fc, L1_ffn_B_fc, L1_ffn_W_proj, L1_ffn_b_proj, L1_ffn_A_proj, L1_ffn_B_proj, L2_xattn_W_q, L2_xattn_W_k, L2_xattn_W_v, L2_xattn_W_o, L2_ffn_gate_w, L2_ffn_gate_b, L2_ffn_w1, L2_ffn_b1, L2_ffn_w2, L2_ffn_b2, L3_xattn_W_out, L3_xattn_b_out, L3_ffn_gate_w, L3_ffn_gate_b, L3_ffn_w1, L3_ffn_w2, L3_ffn_w3, L3_ffn_ws1, L3_ffn_ws2, L3_ffn_ws3):
    import jax
    import jax.numpy as jnp

    def _L0_xattn_ref(x, enc, trg_mask, src_mask, sa_wq, sa_bq, sa_wk, sa_bk, sa_wv, sa_bv, sa_wo, sa_bo, ca_wq, ca_bq, ca_wk, ca_bk, ca_wv, ca_bv, ca_wo, ca_bo, ffn_w1, ffn_b1, ffn_w2, ffn_b2, ln1_g, ln1_b, ln2_g, ln2_b, ln3_g, ln3_b):
        import jax, jax.numpy as jnp
        import numpy as np
        B, TQ, TK, DM, H, FF, STRIDE = (4, 256, 2048, 256, 16, 1024, 16)
        DH = DM // H
        J = TK // STRIDE
        NEG = -1000000000.0

        def _layer_norm(x, g, b, eps=1e-06):
            m = x.mean(-1, keepdims=True)
            v = ((x - m) ** 2).mean(-1, keepdims=True)
            return g * (x - m) / jnp.sqrt(v + eps) + b

        def _full_attn(q, k, v, mask, wq, bq, wk, bk, wv, bv, wo, bo):
            b_, tq, _ = q.shape
            tk = k.shape[1]
            Q = (q @ wq + bq).reshape(b_, tq, H, DH)
            K = (k @ wk + bk).reshape(b_, tk, H, DH)
            V = (v @ wv + bv).reshape(b_, tk, H, DH)
            scores = jnp.einsum('bqhd,bkhd->bhqk', Q, K) / np.sqrt(DH).astype(np.float32)
            scores = jnp.where(mask == 0, NEG, scores)
            attn = jax.nn.softmax(scores, axis=-1)
            out = jnp.einsum('bhqk,bkhd->bqhd', attn, V).reshape(b_, tq, DM)
            return out @ wo + bo

        def _hepos_attn(q, k, v, src_mask, wq, bq, wk, bk, wv, bv, wo, bo):
            b_, tq, _ = q.shape
            tk = k.shape[1]
            Q = (q @ wq + bq).reshape(b_, tq, H, DH)
            K = (k @ wk + bk).reshape(b_, tk, H, DH)
            V = (v @ wv + bv).reshape(b_, tk, H, DH)
            idx = jnp.arange(H)[:, None] + STRIDE * jnp.arange(J)[None, :]
            hsel = jnp.arange(H)[:, None]
            Kh = K[:, idx, hsel, :]
            Vh = V[:, idx, hsel, :]
            scores = jnp.einsum('bqhd,bhjd->bhqj', Q, Kh) / np.sqrt(DH).astype(np.float32)
            mask_h = src_mask[:, 0, 0, :][:, idx][:, :, None, :]
            scores = jnp.where(mask_h == 0, NEG, scores)
            attn = jax.nn.softmax(scores, axis=-1)
            out = jnp.einsum('bhqj,bhjd->bqhd', attn, Vh).reshape(b_, tq, DM)
            return out @ wo + bo
        x = _layer_norm(x + _full_attn(x, x, x, trg_mask, sa_wq, sa_bq, sa_wk, sa_bk, sa_wv, sa_bv, sa_wo, sa_bo), ln1_g, ln1_b)
        x = _layer_norm(x + _hepos_attn(x, enc, enc, src_mask, ca_wq, ca_bq, ca_wk, ca_bk, ca_wv, ca_bv, ca_wo, ca_bo), ln2_g, ln2_b)
        ff = jax.nn.relu(x @ ffn_w1 + ffn_b1) @ ffn_w2 + ffn_b2
        x = _layer_norm(x + ff, ln3_g, ln3_b)
        return x

    def _L0_ffn_ref(x, Wg, bg, W1, b1, W2, b2):
        import jax, jax.numpy as jnp
        import numpy as np
        D = 256
        FF = 4 * D
        E = 8
        TOP_K = 2
        B, S = (4, 1024)
        b, s, d = x.shape
        xt = x.reshape(b * s, d)
        gate = jax.nn.softmax(xt @ Wg + bg, axis=-1)
        _, idx = jax.lax.top_k(gate, TOP_K)
        sel = jax.nn.one_hot(idx, E, dtype=jnp.float32).sum(axis=1) > 0
        sel = sel.astype(x.dtype)
        out = jnp.zeros_like(xt)
        for e in range(E):
            h = jax.nn.relu(xt @ W1[e] + b1[e])
            y = h @ W2[e] + b2[e]
            out = out + sel[:, e:e + 1] * y
        return out.reshape(b, s, d)

    def _L1_xattn_ref(q, k, v, Wq, bq, Wk, bk, Wv, bv, Wo, bo):
        import jax, jax.numpy as jnp
        import numpy as np
        D_MODEL = 256
        D = q.shape[-1]
        query = q @ Wq + bq
        key_p = k @ Wk + bk
        value = v @ Wv + bv
        scores = jnp.einsum('bqd,bkd->bqk', query / jnp.sqrt(jnp.float32(D)), key_p)
        attn = jax.nn.softmax(scores, axis=-1)
        out = jnp.einsum('bqk,bkd->bqd', attn, value)
        return out @ Wo + bo

    def _L1_ffn_ref(hidden_states, W_fc, b_fc, A_fc, B_fc, W_proj, b_proj, A_proj, B_proj):
        import jax, jax.numpy as jnp
        import numpy as np
        BITS = 8
        LORA_RANK = 16
        LORA_ALPHA = 32
        SCALING = LORA_ALPHA / LORA_RANK

        def fake_quant_weight(w, bits=BITS):
            qmax = 2.0 ** (bits - 1) - 1
            scale = jnp.max(jnp.abs(w)) / qmax
            wq = jnp.clip(jnp.round(w / scale), -qmax - 1, qmax) * scale
            return w + jax.lax.stop_gradient(wq - w)

        def qat_lora_linear(x, W, b, A, B):
            Wq = fake_quant_weight(W)
            base = jnp.einsum('bsi,oi->bso', x, Wq) + b
            lora = jnp.einsum('bsr,or->bso', jnp.einsum('bsi,ri->bsr', x, A), B)
            return base + SCALING * lora
        h = qat_lora_linear(hidden_states, W_fc, b_fc, A_fc, B_fc)
        h = jax.nn.gelu(h, approximate=False)
        h = qat_lora_linear(h, W_proj, b_proj, A_proj, B_proj)
        return h

    def _L2_xattn_ref(q, k, v, mask, W_q, W_k, W_v, W_o):
        import jax, jax.numpy as jnp
        import numpy as np
        D_MODEL = 256
        NUM_HEADS = 16
        HEAD_DIM = D_MODEL // NUM_HEADS
        B, S, _ = q.shape
        H, Dh = (NUM_HEADS, HEAD_DIM)

        def proj(x, W):
            return (x @ W.T).reshape(B, -1, H, Dh).transpose(0, 2, 1, 3)
        Q, K, V = (proj(q, W_q), proj(k, W_k), proj(v, W_v))
        scores = jnp.einsum('bhqd,bhkd->bhqk', Q, K) / np.sqrt(Dh)
        scores = jnp.where(mask, scores, -1000000000.0)
        attn = jax.nn.softmax(scores, axis=-1)
        out = jnp.einsum('bhqk,bhkd->bhqd', attn, V)
        out = out.transpose(0, 2, 1, 3).reshape(B, S, D_MODEL)
        return out @ W_o.T

    def _L2_ffn_ref(inputs, gate_w, gate_b, w1, b1, w2, b2):
        import jax, jax.numpy as jnp
        import numpy as np
        NUM_EXPERTS = 8
        CAPACITY = 160
        D = inputs.shape[-1]
        tokens = inputs.reshape(-1, D)
        logits = tokens @ gate_w + gate_b
        probs = jax.nn.softmax(logits, axis=-1)
        expert_idx = jnp.argmax(probs, axis=-1)
        mask1 = jax.nn.one_hot(expert_idx, NUM_EXPERTS, dtype=jnp.float32)
        pos = jnp.sum(jnp.cumsum(mask1, axis=0) * mask1, axis=-1) - 1.0
        pos = pos.astype(jnp.int32)
        keep = (pos < CAPACITY).astype(jnp.float32)
        gate_prob = jnp.sum(probs * mask1, axis=-1)
        pos_oh = jax.nn.one_hot(pos, CAPACITY, dtype=jnp.float32)
        sec_mask = mask1[:, :, None] * pos_oh[:, None, :] * keep[:, None, None]
        combine_weights = sec_mask * gate_prob[:, None, None]
        dispatch = jnp.einsum('nec,nd->ecd', sec_mask, tokens)
        h = jax.nn.gelu(jnp.einsum('ecd,edf->ecf', dispatch, w1) + b1[:, None, :])
        expert_out = jnp.einsum('ecf,efd->ecd', h, w2) + b2[:, None, :]
        out = jnp.einsum('nec,ecd->nd', combine_weights, expert_out)
        return out.reshape(inputs.shape)

    def _L3_xattn_ref(Q, K, V, W_out, b_out):
        import jax, jax.numpy as jnp
        import numpy as np
        B, L, D, H = (4, 512, 256, 16)
        HD = D // H
        b, l, d = Q.shape
        h, hd = (H, d // H)
        q = Q.reshape(b, l, h, hd)
        k = K.reshape(b, l, h, hd)
        v = V.reshape(b, l, h, hd)
        energy = jnp.einsum('nqhd,nkhd->nhqk', q, k)
        attn = jax.nn.softmax(energy / jnp.sqrt(jnp.float32(d)), axis=-1)
        out = jnp.einsum('nhql,nlhd->nqhd', attn, v).reshape(b, l, d)
        return out @ W_out.T + b_out

    def _L3_ffn_ref(x, gate_w, gate_b, w1, w2, w3, ws1, ws2, ws3):
        import jax, jax.numpy as jnp
        import numpy as np
        E = 64
        K = 6
        CAP = 128
        ROUTE_SCALE = 1.0
        shape = x.shape
        D = shape[-1]
        xf = x.reshape(-1, D)
        T = xf.shape[0]
        scores = jax.nn.softmax(xf @ gate_w.T, axis=-1)
        _, idx = jax.lax.top_k(scores + gate_b, K)
        weights = jnp.take_along_axis(scores, idx, axis=1) * ROUTE_SCALE
        flat_e = idx.reshape(-1)
        order = jnp.argsort(flat_e)
        se = flat_e[order]
        counts = jnp.bincount(flat_e, length=E)
        starts = jnp.cumsum(counts) - counts
        pos = jnp.arange(T * K) - starts[se]
        tok = order // K
        xb = jnp.zeros((E, CAP, D), xf.dtype).at[se, pos].set(xf[tok], mode='drop')
        h = jax.nn.silu(jnp.einsum('ecd,eid->eci', xb, w1)) * jnp.einsum('ecd,eid->eci', xb, w3)
        yb = jnp.einsum('eci,edi->ecd', h, w2)
        valid = (pos < CAP).astype(xf.dtype)
        contrib = yb[se, jnp.minimum(pos, CAP - 1)]
        wf = weights.reshape(-1)[order] * valid
        y = jnp.zeros_like(xf).at[tok].add(contrib * wf[:, None])
        z = jax.nn.silu(xf @ ws1.T) * (xf @ ws3.T) @ ws2.T
        return (y + z).reshape(shape)
    x = x + _L0_xattn_ref(_layernorm(x, axis=-1), ctx_1024, mask_Bx1xSxS_ik0, mask_Bx1x1xS2_if1, L0_xattn_sa_wq, L0_xattn_sa_bq, L0_xattn_sa_wk, L0_xattn_sa_bk, L0_xattn_sa_wv, L0_xattn_sa_bv, L0_xattn_sa_wo, L0_xattn_sa_bo, L0_xattn_ca_wq, L0_xattn_ca_bq, L0_xattn_ca_wk, L0_xattn_ca_bk, L0_xattn_ca_wv, L0_xattn_ca_bv, L0_xattn_ca_wo, L0_xattn_ca_bo, L0_xattn_ffn_w1, L0_xattn_ffn_b1, L0_xattn_ffn_w2, L0_xattn_ffn_b2, L0_xattn_ln1_g, L0_xattn_ln1_b, L0_xattn_ln2_g, L0_xattn_ln2_b, L0_xattn_ln3_g, L0_xattn_ln3_b)
    x = x + _L0_ffn_ref(_layernorm(x, axis=-1), L0_ffn_Wg, L0_ffn_bg, L0_ffn_W1, L0_ffn_b1, L0_ffn_W2, L0_ffn_b2)
    x = x + _L1_xattn_ref(_layernorm(x, axis=-1), ctx_1024, ctx_1024, L1_xattn_Wq, L1_xattn_bq, L1_xattn_Wk, L1_xattn_bk, L1_xattn_Wv, L1_xattn_bv, L1_xattn_Wo, L1_xattn_bo)
    x = x + _L1_ffn_ref(_layernorm(x, axis=-1), L1_ffn_W_fc, L1_ffn_b_fc, L1_ffn_A_fc, L1_ffn_B_fc, L1_ffn_W_proj, L1_ffn_b_proj, L1_ffn_A_proj, L1_ffn_B_proj)
    x = x + _L2_xattn_ref(_layernorm(x, axis=-1), ctx_1024, ctx_1024, mask_1x1xSxS2_bk0, L2_xattn_W_q, L2_xattn_W_k, L2_xattn_W_v, L2_xattn_W_o)
    x = x + _L2_ffn_ref(_layernorm(x, axis=-1), L2_ffn_gate_w, L2_ffn_gate_b, L2_ffn_w1, L2_ffn_b1, L2_ffn_w2, L2_ffn_b2)
    x = x + _L3_xattn_ref(_layernorm(x, axis=-1), ctx_1024, ctx_1024, L3_xattn_W_out, L3_xattn_b_out)
    x = x + _L3_ffn_ref(_layernorm(x, axis=-1), L3_ffn_gate_w, L3_ffn_gate_b, L3_ffn_w1, L3_ffn_w2, L3_ffn_w3, L3_ffn_ws1, L3_ffn_ws2, L3_ffn_ws3)
    return x

_drawn_inputs = setup_inputs


def setup_inputs(seed=0):
    import zlib

    import numpy as np

    out = dict(_drawn_inputs(seed))
    spreads = {'L0_xattn_sa_bq': (0.0, 0.414),
     'L0_xattn_sa_bk': (0.0, 0.8),
     'L0_xattn_sa_bv': (0.0, 0.1),
     'L0_xattn_sa_bo': (0.0, 0.1),
     'L0_xattn_ca_bq': (0.0, 0.621),
     'L0_xattn_ca_bk': (0.0, 0.8),
     'L0_xattn_ca_bv': (0.0, 0.1),
     'L0_xattn_ca_bo': (0.0, 0.1),
     'L0_xattn_ffn_b1': (0.0, 0.1),
     'L0_xattn_ffn_b2': (0.0, 0.1),
     'L0_xattn_ln1_g': (1.0, 0.2),
     'L0_xattn_ln1_b': (0.0, 0.1),
     'L0_xattn_ln2_g': (1.0, 0.2),
     'L0_xattn_ln2_b': (0.0, 0.1),
     'L0_xattn_ln3_g': (1.0, 0.2),
     'L0_xattn_ln3_b': (0.0, 0.1),
     'L0_ffn_bg': (0.0, 0.1),
     'L0_ffn_b1': (0.0, 0.1),
     'L0_ffn_b2': (0.0, 0.1),
     'L1_xattn_bq': (0.0, 0.698),
     'L1_xattn_bk': (0.0, 0.8),
     'L1_xattn_bv': (0.0, 0.1),
     'L1_xattn_bo': (0.0, 0.1),
     'L1_ffn_b_fc': (0.0, 0.1),
     'L1_ffn_B_fc': (0.0, 0.1),
     'L1_ffn_b_proj': (0.0, 0.1),
     'L1_ffn_B_proj': (0.0, 0.1),
     'L2_ffn_gate_b': (0.0, 0.8),
     'L2_ffn_b1': (0.0, 0.8),
     'L2_ffn_b2': (0.0, 0.8),
     'L3_xattn_b_out': (0.0, 0.1),
     'L3_ffn_gate_b': (0.0, 0.8)}
    factors = {'L2_ffn_gate_w': 8.0,
     'L2_ffn_w1': 8.0,
     'L2_ffn_w2': 8.0,
     'L3_ffn_gate_w': 8.0,
     'L3_ffn_w1': 8.0,
     'L3_ffn_w2': 8.0,
     'L3_ffn_w3': 8.0,
     'L3_ffn_ws1': 6.686,
     'L3_ffn_ws2': 6.656,
     'L3_ffn_ws3': 6.68}
    for name, (base, spread) in spreads.items():
        noise = np.random.default_rng([zlib.crc32(name.encode()), seed]).standard_normal(out[name].shape)
        drawn = base * np.exp(spread * noise) if base else spread * noise
        out[name] = jnp.asarray(drawn.astype(out[name].dtype))
    for name, factor in factors.items():
        out[name] = (out[name] * factor).astype(out[name].dtype)
    return out
```

```python
from contextlib import ExitStack

import numpy as np
import concourse.bass as bass
from concourse import mybir

F32 = mybir.dt.float32
BF16 = mybir.dt.bfloat16
I32 = mybir.dt.int32
U32 = mybir.dt.uint32
U8 = mybir.dt.uint8
ACT = mybir.ActivationFunctionType
ALU = mybir.AluOpType
AX = mybir.AxisListType

P = 128
D = 256
C = D // P
H = 16
DH = D // H
HC = P // DH
TG = 4
GT = TG * P
QH = 4
POOL_DMA_SEMS = 3 * (2 + 3) + 1
MASKED = -float(2 ** 30)


def ge(eng, sem, value):
    if isinstance(value, (int, np.integer)) and value <= 0:
        return
    eng.wait_ge(sem, value)


class Shared:
    pass


class Memory:

    def __init__(self, nc, ctx, phase):
        self.nc, self.ctx, self.phase, self.sems = nc, ctx, phase, []
        ctx.callback(self.clear)

    def sb(self, name, shape, dt=F32):
        return self.ctx.enter_context(self.nc.sbuf_tensor(f"{self.phase}_{name}", shape, dt))

    def bank(self, name, dt=F32):
        width = 512 if dt == F32 else 1024
        return self.ctx.enter_context(self.nc.psum_tensor(f"{self.phase}_{name}", [P, width], dt))

    def sem(self, name):
        self.sems.append(self.ctx.enter_context(self.nc.semaphore(f"{self.phase}_{name}")))
        return self.sems[-1]

    def clear(self):
        numbers = sorted(s.num for s in self.sems)
        with self.nc.Block() as block:
            @block.gpsimd
            def _(pool):
                first = 0
                for i in range(1, len(numbers) + 1):
                    if i == len(numbers) or numbers[i] != numbers[i - 1] + 1:
                        pool.sem_clear(range(numbers[first], numbers[i - 1] + 1))
                        first = i


def bcast(ap, axis, count):
    ap = ap.unsqueeze(axis)
    shape = list(ap.shape)
    shape[axis] = count
    return ap.broadcast_to(shape)


def column(vector):
    return vector.rearrange("(c p) -> p c", p=P)


def rows(vector, partitions=P):
    return vector.partition_broadcast(partitions)


class Evacuations:

    def __init__(self, ops, before, job_base, bases):
        self.names, self.jobs = [x[:2] for x in ops], [x[2] for x in ops]
        self.names_before, self.before = [x[:2] for x in before], [x[2] for x in before]
        self.job_base, self.bases = job_base, bases

    def filled(self, j):
        return self.job_base + j + 1

    def emptied(self, j):
        if j >= 0:
            e = self.jobs[j]
            return e, self.bases[e] + self.jobs[:j + 1].count(e)
        e = self.before[j]
        later = self.before[j + 1:] if j < -1 else []
        return e, self.bases[e] - later.count(e)

    def place(self, name):
        here = [i for i, x in enumerate(self.names) if name in (x, x[0])]
        there = [i - len(self.before) for i, x in enumerate(self.names_before) if name in (x, x[0])]
        return (here or there)[-1]

    def place_before(self, name):
        return [i - len(self.before) for i, x in enumerate(self.names_before) if name in (x, x[0])][-1]


def settle(eng, sh):
    eng.sem_inc(sh.settled, 1)


def build_constants(nc, sh, ctx):
    m = Memory(nc, ctx, "const")
    sh.ident = m.sb("ident", [P, P])
    sh.ident_bf = m.sb("ident_bf", [P, P], BF16)
    sh.power = m.sb("power", [P, TG])
    made, copied = m.sem("made"), m.sem("copied")
    loaded = m.sem("loaded")
    sh.settled = m.sem("settled")
    sh.pool_dma_sems = [ctx.enter_context(nc.semaphore(f"pool_dma{i}")) for i in range(POOL_DMA_SEMS)]
    with nc.Block() as block:
        @block.gpsimd
        def _(pool):
            nc.gpsimd.memset(sh.ident[:], 0.0).then_inc(made, 1)
            pool.wait_ge(made, 1)
            nc.gpsimd.memset(sh.power[:], -0.5)
            nc.gpsimd.affine_select(out=sh.ident[:], in_=sh.ident[:], compare_op=ALU.not_equal, fill=1.0,
                                    base=0, pattern=[[-1, P]], channel_multiplier=1).then_inc(made, 1)

        @block.vector
        def _(dve):
            dve.wait_ge(made, 2)
            nc.vector.tensor_copy(sh.ident_bf[:], sh.ident[:]).then_inc(copied, 1)

        @block.sync
        def _(sp):
            sp.dma_start(sh.X[:, :, :], sh.x_dram.rearrange("b t d -> t b d")).then_inc(loaded, 16)
            sp.wait_ge(loaded, 16)


def attention_heads(nc, sh, name, G, cfg):
    with ExitStack() as ctx:
        m = Memory(nc, ctx, name)
        project = cfg["wq"] is not None
        from_ctx = cfg["ctx"]
        mask = cfg["mask"]

        wq = m.sb("wq", [P, C, D]) if project else None
        wk = m.sb("wk", [P, C, D]) if project else None
        wv = m.sb("wv", [P, C, D]) if project else None
        wo = m.sb("wo", [P, C, D])
        bq = m.sb("bq", [P, C]) if cfg["bq"] is not None else None
        bk = m.sb("bk", [P, C]) if cfg["bk"] is not None else None
        bv = m.sb("bv", [P, D]) if cfg["bv"] is not None else None
        bo = m.sb("bo", [P, D]) if cfg["bo"] is not None else None
        stats = m.sb("stats", [P, TG, 6])
        moments = m.sb("moments", [P, TG, 2])
        veps = m.sb("veps", [P, TG])
        rstd = m.sb("rstd", [P, TG])
        ln = m.sb("ln", [P, 2, TG, D])
        lnT = m.sb("lnT", [P, C, GT])
        ctxT = m.sb("ctxT", [P, C, GT]) if from_ctx and project else None
        qT = m.sb("qT", [P, 2, C, GT])
        kT = m.sb("kT", [P, C, GT]) if project else None
        kblk = [m.sb(f"kblk{i}", [P, C, HC, GT]) for i in range(2)]
        vraw = m.sb("vraw", [P, TG, D]) if not project else None
        vaug = [m.sb(f"vaug{i}", [P, TG, H, DH + 1]) for i in range(2)]
        shifted = m.sb("shifted", [P, 4, QH, P])
        rowmax = m.sb("rowmax", [P, 4, QH])
        e = m.sb("e", [P, 4, QH, P])
        eT = m.sb("eT", [P, 4, QH, P])
        recip = m.sb("recip", [P, 2, H])
        o = m.sb("o", [P, 2, D])
        oT = m.sb("oT", [P, 2, C, P])
        res = m.sb("res", [P, 2, D]) if bo is not None else None
        if mask is not None:
            mask_in = m.sb("mask_in", [P, TG, P], I32) if mask == "full" else m.sb("mask_in", [P, P], U8)
            mask_add = m.sb("mask_add", [P, 2, TG, P], BF16)
            mask_best = m.sb("mask_best", [P, 2, TG])
            expscale = m.sb("expscale", [P, 2, TG])

        sbank = [m.bank(f"s{i}") for i in range(2)]
        tbank = [m.bank(f"t{i}") for i in range(2)]
        vbank = [m.bank(f"v{i}") for i in range(2)]
        jbank = [m.bank(f"j{i}") for i in range(2)]

        w_in = m.sem("w_in")
        zeroed = m.sem("zeroed")
        ctx_in, mask_dma, v_in = m.sem("ctx_in"), m.sem("mask_dma"), m.sem("v_in")
        bn_done, stats_done, veps_done, rstd_done = m.sem("bn"), m.sem("stats"), m.sem("veps"), m.sem("rstd")
        ln_done, best_done, mask_done = m.sem("ln"), m.sem("best"), m.sem("mask")
        job_done = m.sem("job")
        out_of = {"A": m.sem("act_job"), "V": m.sem("dve_job")}
        kblk_done = [[m.sem(f"kblk{i}_{c}") for c in range(C)] for i in range(2)]
        vaug_done = m.sem("vaug")
        s_done, max_done, sub_done, exp_done = m.sem("s"), m.sem("max"), m.sem("sub"), m.sem("exp")
        t_done, eT_done, av_done = m.sem("t"), m.sem("eT"), m.sem("av")
        recip_done, o_done, res_done = m.sem("recip"), m.sem("o"), m.sem("res")

        if project:
            proj = [("lnT", 0, "A"), ("lnT", 1, "A"), ("q", 0, "V"), ("q", 1, "V"),
                    ("k", 0, "A"), ("k", 1, "A"), ("v", 0, "V"), ("v", 1, "V")]
            proj_steps = [13, 14, 15, 16, 17, 18, 20, 21]
        else:
            proj = [("lnT", 0, "A"), ("lnT", 1, "A")]
            proj_steps = [14, 16]

        def schedule(with_proj):
            ops = []
            for step in range(26):
                if step < TG * 4:
                    ops.append(("S", step))
                if 0 <= step - 3 < TG * 4:
                    ops.append(("T", step - 3))
                if 0 <= step - 5 < TG * 4:
                    ops.append(("AV", step - 5))
                    if (step - 5) % 4 == 3:
                        ops.append(("NORM", (step - 5) // 4))
                if step % 4 == 2 and 0 <= (step - 10) // 4 < TG:
                    ops.append(("oT", (step - 10) // 4, "A"))
                if step % 4 == 0 and 0 <= (step - 12) // 4 < TG:
                    ops.append(("out", (step - 12) // 4, "V"))
                if with_proj:
                    if step == 5:
                        ops.append(("STATS", 0))
                    if step == 9:
                        ops.append(("LN", 0))
                    ops += [p for p, at in zip(proj, proj_steps) if at == step]
            return ops

        prologue = [("STATS", 0), ("LN", 0)] + proj
        middle, last = schedule(True), schedule(False)
        jobs_of = lambda ops: [x for x in ops if len(x) == 3]
        JM = jobs_of(middle)
        count = lambda jobs, who: sum(x[2] == who for x in jobs)

        def counts(g, ops):
            jp = jobs_of(prologue)
            if isinstance(g, int) and g < 0:
                return Evacuations(jp, [], 0, {"A": 0, "V": 0})
            before = jp if isinstance(g, int) and g == 0 else JM
            return Evacuations(jobs_of(ops), before, len(jp) + g * len(JM),
                               {w: count(jp, w) + g * count(JM, w) for w in "AV"})

        def run(eng, emit):
            emit(-1, 1, prologue)
            emit(0, 0, middle)
            with eng.Fori(0, (G - 2) // 2) as t:
                emit(t * 2 + 1, 1, middle)
                emit(t * 2 + 2, 0, middle)
            emit(G - 1, 1, last)

        def kblk_count(g, par):
            return 8 * HC * (g + 2) if par == 0 else 8 * HC * (g + 1)

        def bank_free(eng, ev, j):
            if not ev.before and j < 2:
                return
            who, n = ev.emptied(j - 2)
            ge(eng, out_of[who], n)

        n_weights = 16 * sum(x is not None for x in (wq, wk, wv, wo, bq, bk, bv, bo))
        block = ctx.enter_context(nc.Block())

        @block.sync
        def _(sp):
            for dst, src in ((wq, cfg["wq"]), (wk, cfg["wk"]), (wv, cfg["wv"]), (wo, cfg["wo"])):
                if dst is not None:
                    sp.dma_start(dst[:, :, :], src.rearrange("(c p) n -> p c n", p=P)).then_inc(w_in, 16)
            for dst, src in ((bq, cfg["bq"]), (bk, cfg["bk"])):
                if dst is not None:
                    sp.dma_start(dst[:, :], column(src), allow_slow_non_contiguous=True).then_inc(w_in, 16)
            for dst, src in ((bv, cfg["bv"]), (bo, cfg["bo"])):
                if dst is not None:
                    sp.dma_start(dst[:, :], rows(src)).then_inc(w_in, 16)
            if mask == "shared":
                sp.dma_start(mask_in[:, :], cfg["mask_dram"]).then_inc(mask_dma, 16)
            sp.wait_ge(zeroed, 3)

            def emit(g, par, ops):
                ev = counts(g, ops)
                n = g + 1
                np_ = (1 - par)
                j = -1
                for op in ops:
                    if len(op) == 3:
                        j += 1
                    if op[0] == "STATS":
                        if mask == "full":
                            ge(sp, mask_done, n)
                            sp.dma_start(mask_in[:, :, :], cfg["mask_dram"][bass.ds(n * TG, TG), :, :]
                                         .rearrange("b q k -> q b k")).then_inc(mask_dma, 16)
                        if from_ctx and project:
                            if ev.before:
                                sp.wait_ge(job_done, ev.filled(ev.place_before("v")))
                            for c in range(C):
                                sp.dma_start(ctxT[:, c, :], sh.ctxT_dram[c * P:(c + 1) * P, bass.ds(n * GT, GT)])\
                                  .then_inc(ctx_in, 16)
                        if not project:
                            ge(sp, s_done, (n - 1) * 16)
                            for c in range(C):
                                for r in range(HC):
                                    sp.dma_start(kblk[np_][DH * r:DH * r + DH, c, r, :],
                                                 sh.ctxT_dram[c * P + DH * r:c * P + DH * r + DH, bass.ds(n * GT, GT)])\
                                      .then_inc(kblk_done[np_][c], 16)
                            ge(sp, vaug_done, n)
                            sp.dma_start(vraw[:, :, :], sh.ctx_dram[bass.ds(n * TG, TG), :, :]
                                         .rearrange("b t d -> t b d")).then_inc(v_in, 16)
                    if op[0] == "k":
                        who, cnt = ev.emptied(j)
                        sp.wait_ge(out_of[who], cnt)
                        c = op[1]
                        for r in range(HC):
                            sp.dma_start(kblk[np_][DH * r:DH * r + DH, c, r, :], kT[DH * r:DH * r + DH, c, :])\
                              .then_inc(kblk_done[np_][c], 16)

            run(sp, emit)

        @block.gpsimd
        def _(pool):
            for kb in kblk:
                nc.gpsimd.memset(kb[:, :, :, :], 0.0).then_inc(zeroed, 1)
            for va in vaug:
                last_set = nc.gpsimd.memset(va[:, :, :, DH:DH + 1], 1.0)
            last_set.then_inc(zeroed, 1)

            def emit(g, par, ops):
                n = g + 1
                for op in ops:
                    if op[0] == "STATS":
                        pool.wait_ge(stats_done, n + 1)
                        settle(pool, sh)
                        nc.gpsimd.tensor_scalar(veps[:, :], moments[:, :, 1], cfg["eps"], None, ALU.add)\
                          .then_inc(veps_done, 1)
                        pool.wait_ge(veps_done, n + 1)
                        nc.gpsimd.tensor_tensor(rstd[:, :], veps[:, :], sh.power[:, :], ALU.pow).then_inc(rstd_done, 1)
                        if not project:
                            pool.wait_ge(v_in, 16 * (n + 1))
                            ge(pool, av_done, (n - 1) * 16)
                            settle(pool, sh)
                            for b in range(TG):
                                cp = nc.gpsimd.tensor_copy(vaug[1 - par][:, b, :, 0:DH],
                                                           vraw[:, b, :].rearrange("p (h d) -> p h d", h=H))
                            cp.then_inc(vaug_done, 1)

            run(pool, emit)

        @block.vector
        def _(dve):
            if mask == "shared":
                dve.wait_ge(mask_dma, 16)
                for q in range(2):
                    last_m = nc.vector.tensor_scalar(mask_add[:, q, :, :], bcast(mask_in[:, :], 1, TG), 0.0, MASKED,
                                                     ALU.is_equal, ALU.mult)
                last_m.then_inc(best_done, 1)
                dve.wait_ge(best_done, 1)
                nc.vector.tensor_reduce(mask_best[:, :, :], mask_add[:, :, :, :], AX.X, ALU.max).then_inc(best_done, 1)
                dve.wait_ge(best_done, 2)
                nc.vector.tensor_scalar(expscale[:, :, :], mask_best[:, :, :], 0.0, cfg["scale"], ALU.is_equal,
                                        ALU.mult).then_inc(mask_done, 1)
            dve.wait_ge(w_in, n_weights)

            def emit(g, par, ops):
                ev = counts(g, ops)
                n = g + 1
                np_ = 1 - par
                j = -1
                for op in ops:
                    if len(op) == 3:
                        j += 1
                    if op[0] == "STATS":
                        if not (isinstance(g, int) and g < 0):
                            dve.wait_ge(ln_done, n)
                        for b in range(TG):
                            bn = nc.vector.bn_stats(stats[:, b, :], cfg["src"][:, bass.ds(n * TG + b, 1), :]
                                                    .rearrange("p o d -> p (o d)"))
                        bn.then_inc(bn_done, 1)
                        dve.wait_ge(bn_done, n + 1)
                        settle(dve, sh)
                        for b in range(TG):
                            bn = nc.vector.bn_aggr(moments[:, b, :], stats[:, b, :])
                        bn.then_inc(stats_done, 1)
                        if mask == "full":
                            dve.wait_ge(mask_dma, 16 * (n + 1))
                            nc.vector.tensor_scalar(mask_add[:, np_, :, :], mask_in[:, :, :], 0, MASKED,
                                                    ALU.is_equal, ALU.mult).then_inc(best_done, 1)
                            dve.wait_ge(best_done, 2 * n + 1)
                            nc.vector.tensor_reduce(mask_best[:, np_, :], mask_add[:, np_, :, :], AX.X, ALU.max)\
                              .then_inc(best_done, 1)
                            dve.wait_ge(best_done, 2 * n + 2)
                            nc.vector.tensor_scalar(expscale[:, np_, :], mask_best[:, np_, :], 0.0, cfg["scale"],
                                                    ALU.is_equal, ALU.mult).then_inc(mask_done, 1)
                    if op[0] == "LN":
                        dve.wait_ge(rstd_done, n + 1)
                        for b in range(TG):
                            lnop = nc.vector.tensor_scalar(ln[:, np_, b, :], cfg["src"][:, bass.ds(n * TG + b, 1), :]
                                                           .rearrange("p o d -> p (o d)"), moments[:, b, 0:1],
                                                           rstd[:, b:b + 1], ALU.subtract, ALU.mult)
                        lnop.then_inc(ln_done, 1)
                    if op[0] == "q":
                        dve.wait_ge(job_done, ev.filled(j))
                        if bq is not None:
                            nc.vector.tensor_scalar(qT[:, np_, op[1], :], jbank[j % 2][:, :], bq[:, op[1]:op[1] + 1], None,
                                                    ALU.add).then_inc(out_of["V"], 1)
                        else:
                            nc.vector.tensor_copy(qT[:, np_, op[1], :], jbank[j % 2][:, :]).then_inc(out_of["V"], 1)
                    if op[0] == "v":
                        dve.wait_ge(job_done, ev.filled(j))
                        b0 = 2 * op[1]
                        dst = vaug[np_][:, b0:b0 + 2, :, 0:DH]
                        src = jbank[j % 2][:, :].rearrange("p (b h d) -> p b h d", b=2, h=H)
                        if bv is not None:
                            nc.vector.tensor_tensor(dst, src, bcast(bv[:, :].rearrange("p (h d) -> p h d", h=H), 1, 2),
                                                    ALU.add).then_inc(out_of["V"], 1)
                        else:
                            nc.vector.tensor_copy(dst, src).then_inc(out_of["V"], 1)
                    if op[0] == "S":
                        u = op[1]
                        U = g * 16 + u
                        s4 = sbank[u % 2][:, :].rearrange("p (h k) -> p h k", h=QH)
                        dve.wait_ge(s_done, U + 1)
                        nc.vector.tensor_reduce(rowmax[:, u % 4, :], s4, AX.X, ALU.max).then_inc(max_done, 1)
                        dve.wait_ge(max_done, U + 1)
                        ge(dve, exp_done, U - 3)
                        nc.vector.tensor_tensor(shifted[:, u % 4, :, :], s4, bcast(rowmax[:, u % 4, :], 2, P),
                                                ALU.subtract).then_inc(sub_done, 1)
                    if op[0] == "NORM":
                        b = op[1]
                        av = vbank[b % 2][:, 0:H * (DH + 1)].rearrange("p (h d) -> p h d", h=H)
                        dve.wait_ge(av_done, g * 16 + 4 * b + 4)
                        nc.vector.reciprocal(recip[:, b % 2, :], av[:, :, DH]).then_inc(recip_done, 1)
                        dve.wait_ge(recip_done, g * TG + b + 1)
                        nc.vector.tensor_tensor(o[:, b % 2, :].rearrange("p (h d) -> p h d", h=H), av[:, :, 0:DH],
                                                bcast(recip[:, b % 2, :], 2, DH), ALU.mult).then_inc(o_done, 1)
                    if op[0] == "out":
                        b = op[1]
                        dve.wait_ge(job_done, ev.filled(j))
                        dst = cfg["dst"][:, bass.ds(g * TG + b, 1), :].rearrange("p o d -> p (o d)")
                        base = ln[:, par, b, :] if cfg["base"] == "ln" else dst
                        if bo is not None:
                            nc.vector.tensor_tensor(res[:, b % 2, :], jbank[j % 2][:, 0:D], bo[:, :], ALU.add)\
                              .then_inc(res_done, 1)
                            dve.wait_ge(res_done, g * TG + b + 1)
                            nc.vector.tensor_tensor(dst, res[:, b % 2, :], base, ALU.add).then_inc(out_of["V"], 1)
                        else:
                            nc.vector.tensor_tensor(dst, jbank[j % 2][:, 0:D], base, ALU.add).then_inc(out_of["V"], 1)

            run(dve, emit)

        @block.scalar
        def _(act):
            act.wait_ge(w_in, n_weights)

            def emit(g, par, ops):
                ev = counts(g, ops)
                n = g + 1
                np_ = 1 - par
                j = -1
                for op in ops:
                    if len(op) == 3:
                        j += 1
                    if op[0] == "lnT":
                        act.wait_ge(job_done, ev.filled(j))
                        dst = lnT[:, op[1], :] if project else qT[:, np_, op[1], :]
                        nc.scalar.activation(dst, jbank[j % 2][:, :], ACT.Identity).then_inc(out_of["A"], 1)
                    if op[0] == "k":
                        act.wait_ge(job_done, ev.filled(j))
                        if not (isinstance(n, int) and n == 0):
                            act.wait_ge(kblk_done[par][op[1]], kblk_count(g, par))
                        bias = bk[:, op[1]:op[1] + 1] if bk is not None else 0.0
                        nc.scalar.activation(kT[:, op[1], :], jbank[j % 2][:, :], ACT.Identity, bias=bias)\
                          .then_inc(out_of["A"], 1)
                    if op[0] == "S":
                        u = op[1]
                        U = g * 16 + u
                        act.wait_ge(sub_done, U + 1)
                        ge(act, t_done, U - 3)
                        if mask is not None:
                            if u == 0:
                                act.wait_ge(mask_done, g + 1 if mask == "full" else 1)
                            scale = expscale[:, par, u // 4:u // 4 + 1]
                        else:
                            scale = cfg["scale"]
                        nc.scalar.activation(e[:, u % 4, :, :], shifted[:, u % 4, :, :], ACT.Exp, scale=scale)\
                          .then_inc(exp_done, 1)
                    if op[0] == "T":
                        u = op[1]
                        U = g * 16 + u
                        act.wait_ge(t_done, U + 1)
                        ge(act, av_done, U - 3)
                        nc.scalar.activation(eT[:, u % 4, :, :].rearrange("p h k -> p (h k)"), tbank[u % 2][:, :],
                                             ACT.Identity).then_inc(eT_done, 1)
                    if op[0] == "oT":
                        act.wait_ge(job_done, ev.filled(j))
                        nc.scalar.activation(oT[:, op[1] % 2, :, :].rearrange("p c t -> p (c t)"), jbank[j % 2][:, 0:D],
                                             ACT.Identity).then_inc(out_of["A"], 1)

            run(act, emit)

        @block.tensor
        def _(pe):
            pe.wait_ge(w_in, n_weights)
            pe.wait_ge(zeroed, 3)

            def emit(g, par, ops):
                ev = counts(g, ops)
                n = g + 1
                np_ = 1 - par
                j = -1
                for op in ops:
                    if len(op) == 3:
                        j += 1
                        bank = jbank[j % 2]
                        bank_free(pe, ev, j)
                    if op[0] == "lnT":
                        pe.wait_ge(ln_done, n + 1)
                        for b in range(TG):
                            last_mm = nc.tensor.transpose(bank[:, b * P:(b + 1) * P], ln[:, np_, b, op[1] * P:(op[1] + 1) * P],
                                                          sh.ident[:, :])
                        last_mm.then_inc(job_done, 1)
                    if op[0] in ("q", "k"):
                        w, x = (wq, lnT) if op[0] == "q" else (wk, ctxT if from_ctx else lnT)
                        if op[0] == "q" and op[1] == 0:
                            who, cnt = ev.emptied(j - 1)
                            pe.wait_ge(out_of[who], cnt)
                        if op[0] == "k" and op[1] == 0 and from_ctx:
                            pe.wait_ge(ctx_in, 16 * C * (n + 1))
                        for c in range(C):
                            last_mm = nc.tensor.matmul(bank[:, :], w[:, c, op[1] * P:(op[1] + 1) * P], x[:, c, :],
                                                       start=(c == 0), stop=(c == C - 1))
                        last_mm.then_inc(job_done, 1)
                    if op[0] == "v":
                        x = ctxT if from_ctx else lnT
                        for i in range(2):
                            b = 2 * op[1] + i
                            for c in range(C):
                                last_mm = nc.tensor.matmul(bank[:, i * D:(i + 1) * D], x[:, c, b * P:(b + 1) * P], wv[:, c, :],
                                                           start=(c == 0), stop=(c == C - 1))
                        last_mm.then_inc(job_done, 1)
                    if op[0] == "S":
                        u = op[1]
                        U = g * 16 + u
                        b, c, h0 = u // 4, (u % 4) // 2, QH * (u % 2)
                        if u == 0:
                            who, cnt = ev.emptied(ev.place_before("q" if project else "lnT"))
                            pe.wait_ge(out_of[who], cnt)
                            pe.wait_ge(kblk_done[par][0], kblk_count(g, par))
                            if mask is not None:
                                pe.wait_ge(mask_done, g + 1 if mask == "full" else 1)
                        if u == 2:
                            pe.wait_ge(kblk_done[par][1], kblk_count(g, par))
                        ge(pe, sub_done, U - 1)
                        bank = sbank[u % 2]
                        if mask is not None:
                            nc.tensor.matmul(bank[:, :].rearrange("p (h k) -> p h k", h=QH), sh.ident_bf[:, :],
                                             bcast(mask_add[:, par, b, :], 1, QH), start=True, stop=False)
                        nc.tensor.matmul(bank[:, :].rearrange("p (h k) -> p h k", h=QH), qT[:, par, c, b * P:(b + 1) * P],
                                         kblk[par][:, c, h0:h0 + QH, b * P:(b + 1) * P],
                                         start=(mask is None), stop=True).then_inc(s_done, 1)
                    if op[0] == "T":
                        u = op[1]
                        U = g * 16 + u
                        pe.wait_ge(exp_done, U + 1)
                        ge(pe, eT_done, U - 1)
                        for h in range(QH):
                            last_mm = nc.tensor.transpose(tbank[u % 2][:, h * P:(h + 1) * P], e[:, u % 4, h, :], sh.ident[:, :])
                        last_mm.then_inc(t_done, 1)
                    if op[0] == "AV":
                        u = op[1]
                        U = g * 16 + u
                        b = u // 4
                        if u == 0:
                            if project:
                                who, cnt = ev.emptied(ev.place_before("v"))
                                pe.wait_ge(out_of[who], cnt)
                            else:
                                pe.wait_ge(vaug_done, g + 1)
                        pe.wait_ge(eT_done, U + 1)
                        if u % 4 == 0:
                            ge(pe, o_done, g * TG + b - 1)
                        for h in range(QH):
                            hh = QH * (u % 4) + h
                            last_mm = nc.tensor.matmul(vbank[b % 2][:, hh * (DH + 1):(hh + 1) * (DH + 1)], eT[:, u % 4, h, :],
                                                       vaug[par][:, b, hh, :], start=True, stop=True)
                        last_mm.then_inc(av_done, 1)
                    if op[0] == "oT":
                        b = op[1]
                        pe.wait_ge(o_done, g * TG + b + 1)
                        for c in range(C):
                            last_mm = nc.tensor.transpose(bank[:, c * P:(c + 1) * P], o[:, b % 2, c * P:(c + 1) * P], sh.ident[:, :])
                        last_mm.then_inc(job_done, 1)
                    if op[0] == "out":
                        b = op[1]
                        who, cnt = ev.emptied(ev.place(("oT", b)))
                        pe.wait_ge(out_of[who], cnt)
                        for c in range(C):
                            last_mm = nc.tensor.matmul(bank[:, 0:D], oT[:, b % 2, c, :], wo[:, c, :],
                                                       start=(c == 0), stop=(c == C - 1))
                        last_mm.then_inc(job_done, 1)

            run(pe, emit)


class Chain:

    def __init__(self, eng, sem, start, per):
        self.eng, self.sem, self.start, self.per = eng, sem, start, per

    def group(self, g):
        self.base, self.k = (0 if isinstance(g, int) and g < 0 else self.start + g * self.per), 0

    def link(self, ins):
        self.k += 1
        ins.then_inc(self.sem, 1)
        self.eng.wait_ge(self.sem, self.base + self.k)


def run_groups(eng, emit, G, prologue, middle, last):
    emit(-1, 1, prologue)
    emit(0, 0, middle)
    with eng.Fori(0, (G - 2) // 2) as t:
        emit(t * 2 + 1, 1, middle)
        emit(t * 2 + 2, 0, middle)
    emit(G - 1, 1, last)


def tile_of(stream, t):
    return stream[:, bass.ds(t, 1), :].rearrange("p o d -> p (o d)")


def ffn(nc, sh, name, G, cfg):
    with ExitStack() as ctx:
        m = Memory(nc, ctx, name)
        affine, post = cfg["affine"], cfg["post"]
        F = cfg["F"]
        NF = F // P
        resident = cfg.get("resident")
        w1 = resident[0] if resident else m.sb("w1", [P, C, F])
        w2 = resident[1] if resident else m.sb("w2", [P, NF, D])
        b1 = m.sb("b1", [P, NF])
        b2 = m.sb("b2", [P, D])
        vec = {}
        for k, src in (("g", affine and affine[0]), ("b", affine and affine[1]),
                       ("pg", post and post[0]), ("pb", post and post[1])):
            if src is not None:
                vec[k] = (m.sb(k, [P, D]), src)
        stats = m.sb("stats", [P, TG, 6])
        moments = m.sb("moments", [P, TG, 2])
        veps, rstd = m.sb("veps", [P, TG]), m.sb("rstd", [P, TG])
        pmoments = m.sb("pmoments", [P, TG, 2])
        pveps, prstd = m.sb("pveps", [P, TG]), m.sb("prstd", [P, TG])
        ln = m.sb("ln", [P, 2, TG, D])
        lnT = m.sb("lnT", [P, 2, C, GT])
        hT = m.sb("hT", [P, 4, GT])
        y = m.sb("y", [P, TG, D])

        hbank = [m.bank(f"h{i}") for i in range(2)]
        ybank = [m.bank(f"y{i}") for i in range(TG)]
        tbank = [m.bank(f"t{i}") for i in range(C)]

        w_in = m.sem("w_in")
        stats_done, veps_done, rstd_done, ln_done = m.sem("stats"), m.sem("veps"), m.sem("rstd"), m.sem("ln")
        pstats_done, pveps_done, prstd_done = m.sem("pstats"), m.sem("pveps"), m.sem("prstd")
        chain_sem = m.sem("chain")
        t_done, lnT_done = m.sem("t"), m.sem("lnT")
        h_done, act_done, y_done, out_done = m.sem("h"), m.sem("act"), m.sem("y"), m.sem("out")

        def schedule(with_next):
            ops = []
            for s in range(NF + 2):
                if s < NF:
                    ops.append(("H", s))
                if s >= 2:
                    ops.append(("Y", s - 2))
                if with_next:
                    ops += {1: [("STATS",)], 4: [("LN",)], 6: [("lnT", 0), ("lnT", 1)]}.get(s, [])
            return ops + [("OUT",)]

        prologue = [("STATS",), ("LN",), ("lnT", 0), ("lnT", 1)]
        middle, last = schedule(True), schedule(False)
        loads = (0 if resident else 2) + 2 + len(vec)
        block = ctx.enter_context(nc.Block())

        @block.sync
        def _(sp):
            if not resident:
                sp.dma_start(w1[:, :, :], cfg["w1"].rearrange("(c p) n -> p c n", p=P)).then_inc(w_in, 16)
                sp.dma_start(w2[:, :, :], cfg["w2"].rearrange("(c p) n -> p c n", p=P)).then_inc(w_in, 16)
            sp.dma_start(b1[:, :], column(cfg["b1"]), allow_slow_non_contiguous=True).then_inc(w_in, 16)
            sp.dma_start(b2[:, :], rows(cfg["b2"])).then_inc(w_in, 16)
            for dst, src in vec.values():
                sp.dma_start(dst[:, :], rows(src)).then_inc(w_in, 16)

        @block.gpsimd
        def _(pool):
            def emit(g, par, ops):
                n = g + 1
                for op in ops:
                    if op[0] == "STATS":
                        pool.wait_ge(stats_done, n + 1)
                        settle(pool, sh)
                        nc.gpsimd.tensor_scalar(veps[:, :], moments[:, :, 1], cfg["eps"], None, ALU.add)\
                          .then_inc(veps_done, 1)
                        pool.wait_ge(veps_done, n + 1)
                        nc.gpsimd.tensor_tensor(rstd[:, :], veps[:, :], sh.power[:, :], ALU.pow).then_inc(rstd_done, 1)
                    if op[0] == "OUT" and post:
                        pool.wait_ge(pstats_done, g + 1)
                        settle(pool, sh)
                        nc.gpsimd.tensor_scalar(pveps[:, :], pmoments[:, :, 1], post[2], None, ALU.add)\
                          .then_inc(pveps_done, 1)
                        pool.wait_ge(pveps_done, g + 1)
                        nc.gpsimd.tensor_tensor(prstd[:, :], pveps[:, :], sh.power[:, :], ALU.pow).then_inc(prstd_done, 1)

            run_groups(pool, emit, G, prologue, middle, last)

        @block.vector
        def _(dve):
            dve.wait_ge(w_in, 16 * loads)
            ln_links = 1 + (2 if affine else 0)
            out_links = 1 + (1 + 1 + 3 if post else 0)
            chain = Chain(dve, chain_sem, ln_links, ln_links + out_links)

            def emit(g, par, ops):
                n = g + 1
                np_ = 1 - par
                chain.group(g)
                for op in ops:
                    if op[0] == "STATS":
                        for b in range(TG):
                            bn = nc.vector.bn_stats(stats[:, b, :], tile_of(cfg["src"], n * TG + b))
                        chain.link(bn)
                        settle(dve, sh)
                        for b in range(TG):
                            bn = nc.vector.bn_aggr(moments[:, b, :], stats[:, b, :])
                        bn.then_inc(stats_done, 1)
                    if op[0] == "LN":
                        dve.wait_ge(rstd_done, n + 1)
                        for b in range(TG):
                            lnop = nc.vector.tensor_scalar(ln[:, np_, b, :], tile_of(cfg["src"], n * TG + b),
                                                           moments[:, b, 0:1], rstd[:, b:b + 1], ALU.subtract, ALU.mult)
                        if affine:
                            chain.link(lnop)
                            x4 = ln[:, np_, :, :]
                            chain.link(nc.vector.tensor_tensor(x4, x4, bcast(vec["g"][0][:, :], 1, TG), ALU.mult))
                            lnop = nc.vector.tensor_tensor(x4, x4, bcast(vec["b"][0][:, :], 1, TG), ALU.add)
                        lnop.then_inc(ln_done, 1)
                    if op[0] == "OUT":
                        dve.wait_ge(y_done, (g + 1) * NF)
                        for b in range(TG):
                            add = nc.vector.tensor_tensor(y[:, b, :], ybank[b][:, 0:D], b2[:, :], ALU.add)
                        add.then_inc(out_done, 1)
                        dve.wait_ge(out_done, g + 1)
                        base = ln[:, par, :, :] if affine else cfg["dst"][:, bass.ds(g * TG, TG), :]
                        if not post:
                            dst = cfg["dst"][:, bass.ds(g * TG, TG), :]
                            chain.link(nc.vector.tensor_tensor(dst, y[:, :, :], base, ALU.add))
                        else:
                            chain.link(nc.vector.tensor_tensor(y[:, :, :], y[:, :, :], base, ALU.add))
                            for b in range(TG):
                                bn = nc.vector.bn_stats(stats[:, b, :], y[:, b, :])
                            chain.link(bn)
                            settle(dve, sh)
                            for b in range(TG):
                                bn = nc.vector.bn_aggr(pmoments[:, b, :], stats[:, b, :])
                            bn.then_inc(pstats_done, 1)
                            dve.wait_ge(prstd_done, g + 1)
                            for b in range(TG):
                                lnop = nc.vector.tensor_scalar(y[:, b, :], y[:, b, :], pmoments[:, b, 0:1],
                                                               prstd[:, b:b + 1], ALU.subtract, ALU.mult)
                            chain.link(lnop)
                            chain.link(nc.vector.tensor_tensor(y[:, :, :], y[:, :, :], bcast(vec["pg"][0][:, :], 1, TG), ALU.mult))
                            chain.link(nc.vector.tensor_tensor(y[:, :, :], y[:, :, :], bcast(vec["pb"][0][:, :], 1, TG), ALU.add))
                            dst = cfg["dst"][:, bass.ds(g * TG, TG), :]
                            chain.link(nc.vector.tensor_tensor(dst, dst, y[:, :, :], ALU.add))

            run_groups(dve, emit, G, prologue, middle, last)

        @block.scalar
        def _(act):
            act.wait_ge(w_in, 16 * loads)

            def emit(g, par, ops):
                n = g + 1
                for op in ops:
                    if op[0] == "lnT":
                        act.wait_ge(t_done, n * C + op[1] + 1)
                        nc.scalar.activation(lnT[:, 1 - par, op[1], :], tbank[op[1]][:, :], ACT.Identity).then_inc(lnT_done, 1)
                    if op[0] == "H":
                        U = g * NF + op[1]
                        act.wait_ge(h_done, U + 1)
                        ge(act, y_done, U - 3)
                        nc.scalar.activation(hT[:, op[1] % 4, :], hbank[op[1] % 2][:, :], cfg["act"],
                                             bias=b1[:, op[1]:op[1] + 1]).then_inc(act_done, 1)

            run_groups(act, emit, G, prologue, middle, last)

        @block.tensor
        def _(pe):
            pe.wait_ge(w_in, 16 * loads)

            def emit(g, par, ops):
                n = g + 1
                for op in ops:
                    if op[0] == "lnT":
                        c = op[1]
                        pe.wait_ge(ln_done, n + 1)
                        ge(pe, lnT_done, n * C - C + c + 1 if not isinstance(n, int) or n > 0 else 0)
                        for b in range(TG):
                            tr = nc.tensor.transpose(tbank[c][:, b * P:(b + 1) * P], ln[:, 1 - par, b, c * P:(c + 1) * P],
                                                     sh.ident[:, :])
                        tr.then_inc(t_done, 1)
                    if op[0] == "H":
                        f = op[1]
                        U = g * NF + f
                        if f == 0:
                            pe.wait_ge(lnT_done, C * (g + 1))
                        ge(pe, act_done, U - 1)
                        for c in range(C):
                            mm = nc.tensor.matmul(hbank[f % 2][:, :], w1[:, c, f * P:(f + 1) * P], lnT[:, par, c, :],
                                                  start=(c == 0), stop=(c == C - 1))
                        mm.then_inc(h_done, 1)
                    if op[0] == "Y":
                        f = op[1]
                        pe.wait_ge(act_done, g * NF + f + 1)
                        if f == 0:
                            ge(pe, out_done, g)
                        for b in range(TG):
                            mm = nc.tensor.matmul(ybank[b][:, 0:D], hT[:, f % 4, b * P:(b + 1) * P], w2[:, f, :],
                                                  start=(f == 0), stop=(f == NF - 1))
                        mm.then_inc(y_done, 1)

            run_groups(pe, emit, G, prologue, middle, last)


def attention_narrow(nc, sh, name, G, cfg):
    with ExitStack() as ctx:
        m = Memory(nc, ctx, name)
        strided = cfg["kind"] == "strided"
        affine = cfg["affine"]
        KW = P + H if strided else P
        SLOTS = KW // H
        wq, wk, wv, wo = (m.sb(w, [P, C, D]) for w in ("wq", "wk", "wv", "wo"))
        bq, bk = m.sb("bq", [P, C]), m.sb("bk", [P, C])
        bv, bo = m.sb("bv", [P, D]), m.sb("bo", [P, D])
        if affine:
            ga, be = m.sb("ga", [P, D]), m.sb("be", [P, D])
        stats, moments = m.sb("stats", [P, TG, 6]), m.sb("moments", [P, TG, 2])
        veps, rstd = m.sb("veps", [P, TG]), m.sb("rstd", [P, TG])
        ln = m.sb("ln", [P, 2, TG, D])
        lnT = m.sb("lnT", [P, C, GT])
        ctxT = m.sb("ctxT", [P, 2, C, GT])
        qT = m.sb("qT", [P, 2, C, GT])
        k = m.sb("k", [P, 2, C, TG, KW])
        vt = m.sb("vt", [P, TG, D])
        v = m.sb("v", [P, 2, TG, D])
        if strided:
            head_of = m.sb("head_of", [P, C, H])
            key_of = m.sb("key_of", [P, H])
            xt = m.sb("xt", [H, TG, D])
            vx = m.sb("vx", [H, 2, TG, D])
            mask_in = m.sb("mask_in", [P, TG, P], I32)
            keep = m.sb("keep", [P, 2, TG, KW])
            fill = m.sb("fill", [P, 2, TG, KW])
            pxT = m.sb("pxT", [H, TG, P])
        sc = m.sb("sc", [P, TG, KW])
        p = m.sb("p", [P, TG, KW])
        NMAX = H if strided else 1
        best, total, recip = (m.sb(x, [P, TG, NMAX]) for x in ("best", "total", "recip"))
        pT = m.sb("pT", [P, TG, P])
        o = m.sb("o", [P, TG, D])
        oT = m.sb("oT", [P, 2, 2, C, P])
        res = m.sb("res", [P, TG, D])

        jbank = [m.bank(f"j{i}") for i in range(2)]
        sbank = [m.bank(f"s{i}") for i in range(2)]
        vbank = [m.bank(f"v{i}") for i in range(2)]
        tbank = m.bank("t")
        xbank = m.bank("x")

        w_in, ctx_in, mask_in_done = m.sem("w_in"), m.sem("ctx_in"), m.sem("mask_in")
        heads_made, heads_step = m.sem("heads_made"), m.sem("heads_step")
        stats_done, veps_done, rstd_done, ln_done = m.sem("stats"), m.sem("veps"), m.sem("rstd"), m.sem("ln")
        mask_done = m.sem("mask")
        job_done = m.sem("job")
        out_of = {"A": m.sem("act_job"), "V": m.sem("dve_job")}
        s_done, sc_done, exp_done, total_done = m.sem("s"), m.sem("sc"), m.sem("exp"), m.sem("total")
        pt_done, pT_done, av_done, o_done = m.sem("pt"), m.sem("pT"), m.sem("av"), m.sem("o")
        ot_done, oT_done, out_done, res_done = m.sem("ot"), m.sem("oT"), m.sem("out"), m.sem("res")
        chain_sem = m.sem("chain")

        proj = [("lnT", 0, "A"), ("lnT", 1, "A"), ("q", 0, "A"), ("q", 1, "A"),
                ("k", 0, "V"), ("k", 1, "V"), ("v", 0, "V"), ("v", 1, "V")]
        if strided:
            proj += [("x", 0, "V"), ("x", 1, "V")]
        J = dict(((x[0], x[1]), x) for x in proj)
        prologue = [("STATS",), ("LN",)] + proj
        last = [("S",), ("SOFT",), ("PT",), ("AV",), ("NORM",), ("OT",), ("OUT",)]
        middle = [("S",), ("SOFT",), ("STATS",), ("LN",), J["lnT", 0], J["lnT", 1], J["q", 0], ("PT",), J["q", 1],
                  J["k", 0], ("AV",), J["k", 1], ("NORM",), J["v", 0], ("OT",), J["v", 1]] \
            + ([J["x", 0]] if strided else []) + [("OUT",)] + ([J["x", 1]] if strided else [])
        jobs_of = lambda ops: [x for x in ops if len(x) == 3]
        per = {w: sum(x[2] == w for x in proj) for w in "AV"}

        def counts(g, ops):
            n = g + 1
            before = [] if isinstance(g, int) and g < 0 else proj
            return Evacuations(jobs_of(ops), before, n * len(proj), {w: n * per[w] for w in "AV"})

        next_links = 1 + (2 if affine else 0) + (4 if strided else 0)
        own_links = 5 if strided else 2
        loads = 8 + (2 if affine else 0)
        block = ctx.enter_context(nc.Block())

        @block.sync
        def _(sp):
            for dst, src in ((wq, "wq"), (wk, "wk"), (wv, "wv"), (wo, "wo")):
                sp.dma_start(dst[:, :, :], cfg[src].rearrange("(c p) n -> p c n", p=P)).then_inc(w_in, 16)
            for dst, src in ((bq, "bq"), (bk, "bk")):
                sp.dma_start(dst[:, :], column(cfg[src]), allow_slow_non_contiguous=True).then_inc(w_in, 16)
            for dst, src in ((bv, cfg["bv"]), (bo, cfg["bo"])) + (((ga, affine[0]), (be, affine[1])) if affine else ()):
                sp.dma_start(dst[:, :], rows(src)).then_inc(w_in, 16)

            def emit(g, par, ops):
                n = g + 1
                for op in ops:
                    if op[0] == "STATS":
                        if not (isinstance(n, int) and n < 2):
                            sp.wait_ge(job_done, (n - 1) * len(proj))
                        if not (isinstance(n, int) and n < 1):
                            sp.wait_ge(ctx_in, 16 * C * n)
                        for c in range(C):
                            sp.dma_start(ctxT[:, 1 - par, c, :], sh.ctxT_dram[c * P:(c + 1) * P, bass.ds(n * GT, GT)])\
                              .then_inc(ctx_in, 16)
                        if strided:
                            ge(sp, mask_done, n)
                            sp.dma_start(mask_in[:, :, :], cfg["mask_dram"][bass.ds(n * TG, TG), :]
                                         .partition_broadcast(P)).then_inc(mask_in_done, 16)

            run_groups(sp, emit, G, prologue, middle, last)

        @block.gpsimd
        def _(pool):
            if strided:
                nc.gpsimd.memset(head_of[:, :, :], 1.0).then_inc(heads_step, 1)
                pool.wait_ge(heads_step, 1)
                nc.gpsimd.affine_select(out=head_of[:, :, :], in_=head_of[:, :, :], compare_op=ALU.is_ge, fill=0.0,
                                        base=0, pattern=[[P, C], [-DH, H]], channel_multiplier=1).then_inc(heads_step, 1)
                pool.wait_ge(heads_step, 2)
                nc.gpsimd.affine_select(out=head_of[:, :, :], in_=head_of[:, :, :], compare_op=ALU.is_ge, fill=0.0,
                                        base=DH - 1, pattern=[[-P, C], [DH, H]], channel_multiplier=-1)\
                  .then_inc(heads_step, 1)
                nc.gpsimd.memset(key_of[:, :], 0.0).then_inc(heads_step, 1)
                for i in range(P // H):
                    pool.wait_ge(heads_step, 4 + i)
                    nc.gpsimd.affine_select(out=key_of[:, :], in_=key_of[:, :], compare_op=ALU.not_equal, fill=1.0,
                                            base=-H * i, pattern=[[-1, H]], channel_multiplier=1).then_inc(heads_step, 1)

            def emit(g, par, ops):
                n = g + 1
                for op in ops:
                    if op[0] == "STATS":
                        pool.wait_ge(stats_done, n + 1)
                        settle(pool, sh)
                        nc.gpsimd.tensor_scalar(veps[:, :], moments[:, :, 1], cfg["eps"], None, ALU.add)\
                          .then_inc(veps_done, 1)
                        pool.wait_ge(veps_done, n + 1)
                        nc.gpsimd.tensor_tensor(rstd[:, :], veps[:, :], sh.power[:, :], ALU.pow).then_inc(rstd_done, 1)

            run_groups(pool, emit, G, prologue, middle, last)

        @block.vector
        def _(dve):
            dve.wait_ge(w_in, 16 * loads)
            if strided:
                dve.wait_ge(heads_step, 4 + P // H)
            chain = Chain(dve, chain_sem, next_links, next_links + own_links)

            def emit(g, par, ops):
                n = g + 1
                np_ = 1 - par
                ev = counts(g, ops)
                j = -1
                chain.group(g)
                for op in ops:
                    if len(op) == 3:
                        j += 1
                        if op[2] == "V":
                            dve.wait_ge(job_done, ev.filled(j))
                    if op[0] == "STATS":
                        for b in range(TG):
                            bn = nc.vector.bn_stats(stats[:, b, :], tile_of(cfg["src"], n * TG + b))
                        chain.link(bn)
                        settle(dve, sh)
                        for b in range(TG):
                            bn = nc.vector.bn_aggr(moments[:, b, :], stats[:, b, :])
                        bn.then_inc(stats_done, 1)
                        if strided:
                            dve.wait_ge(mask_in_done, 16 * (n + 1))
                            last_key = bcast(mask_in[:, :, P - 1], 2, H)
                            nc.vector.tensor_scalar(keep[:, np_, :, 0:P], mask_in[:, :, :], 0, cfg["scale"],
                                                    ALU.not_equal, ALU.mult)
                            nc.vector.tensor_scalar(fill[:, np_, :, 0:P], mask_in[:, :, :], 0, cfg["masked"],
                                                    ALU.is_equal, ALU.mult)
                            nc.vector.tensor_scalar(fill[:, np_, :, P:KW], last_key, 0, cfg["masked"],
                                                    ALU.is_equal, ALU.mult)
                            nc.vector.tensor_scalar(keep[:, np_, :, P:KW], last_key, 0, cfg["scale"],
                                                    ALU.not_equal, ALU.mult).then_inc(mask_done, 1)
                    if op[0] == "LN":
                        dve.wait_ge(rstd_done, n + 1)
                        for b in range(TG):
                            lnop = nc.vector.tensor_scalar(ln[:, np_, b, :], tile_of(cfg["src"], n * TG + b),
                                                           moments[:, b, 0:1], rstd[:, b:b + 1], ALU.subtract, ALU.mult)
                        if affine:
                            chain.link(lnop)
                            x4 = ln[:, np_, :, :]
                            chain.link(nc.vector.tensor_tensor(x4, x4, bcast(ga[:, :], 1, TG), ALU.mult))
                            lnop = nc.vector.tensor_tensor(x4, x4, bcast(be[:, :], 1, TG), ALU.add)
                        lnop.then_inc(ln_done, 1)
                    if op[0] == "k":
                        c = op[1]
                        bank = jbank[j % 2][:, :]
                        if strided:
                            for b in range(TG):
                                nc.vector.scalar_tensor_tensor(
                                    out=k[:, np_, c, b, 0:P].rearrange("p (i h) -> p i h", h=H),
                                    in0=bank[:, b * P:(b + 1) * P].rearrange("p (i h) -> p i h", h=H),
                                    scalar=bk[:, c:c + 1], in1=bcast(head_of[:, c, :], 1, P // H), op0=ALU.add, op1=ALU.mult)
                            nc.vector.scalar_tensor_tensor(
                                out=k[:, np_, c, :, P:KW],
                                in0=bcast(bank.rearrange("p (b k) -> p b k", b=TG)[:, :, P - 1], 2, H),
                                scalar=bk[:, c:c + 1], in1=bcast(head_of[:, c, :], 1, TG), op0=ALU.add, op1=ALU.mult)\
                              .then_inc(out_of["V"], 1)
                        else:
                            nc.vector.tensor_scalar(k[:, np_, c, :, :].rearrange("p b k -> p (b k)"), bank,
                                                    bk[:, c:c + 1], None, ALU.add).then_inc(out_of["V"], 1)
                    if op[0] == "v":
                        b0 = 2 * op[1]
                        bank = jbank[j % 2][:, :].rearrange("p (b d) -> p b d", b=2)
                        if strided:
                            chain.link(nc.vector.tensor_tensor(vt[:, b0:b0 + 2, :], bank, bcast(bv[:, :], 1, 2), ALU.add))
                            nc.vector.tensor_tensor(v[:, np_, b0:b0 + 2, :].rearrange("p b (h d) -> p b h d", h=H),
                                                    vt[:, b0:b0 + 2, :].rearrange("p b (h d) -> p b h d", h=H),
                                                    bcast(bcast(key_of[:, :], 1, 2), 3, DH), ALU.mult)\
                              .then_inc(out_of["V"], 1)
                        else:
                            nc.vector.tensor_tensor(v[:, np_, b0:b0 + 2, :], bank, bcast(bv[:, :], 1, 2), ALU.add)\
                              .then_inc(out_of["V"], 1)
                    if op[0] == "x":
                        b0 = 2 * op[1]
                        bank = jbank[j % 2][0:H, :].rearrange("p (b d) -> p b d", b=2)
                        chain.link(nc.vector.tensor_tensor(xt[:, b0:b0 + 2, :], bank, bcast(bv[0:H, :], 1, 2), ALU.add))
                        nc.vector.tensor_tensor(vx[:, np_, b0:b0 + 2, :].rearrange("p b (h d) -> p b h d", h=H),
                                                xt[:, b0:b0 + 2, :].rearrange("p b (h d) -> p b h d", h=H),
                                                bcast(bcast(key_of[0:H, :], 1, 2), 3, DH), ALU.mult)\
                          .then_inc(out_of["V"], 1)
                    if op[0] == "SOFT":
                        dve.wait_ge(s_done, g + 1)
                        by_head = lambda t: t[:, :, :].rearrange("p b (i h) -> p b h i", h=NMAX) if strided else t[:, :, :]
                        if strided:
                            for i in range(2):
                                mul = nc.vector.tensor_tensor(
                                    sc[:, 2 * i:2 * i + 2, :], sbank[i][:, 0:2 * KW].rearrange("p (b k) -> p b k", b=2),
                                    keep[:, par, 2 * i:2 * i + 2, :], ALU.mult)
                            mul.then_inc(sc_done, 1)
                            dve.wait_ge(sc_done, g + 1)
                            chain.link(nc.vector.tensor_tensor(sc[:, :, :], sc[:, :, :], fill[:, par, :, :], ALU.add))
                            chain.link(nc.vector.tensor_reduce(best[:, :, :], by_head(sc), AX.X, ALU.max))
                            chain.link(nc.vector.tensor_tensor(
                                sc[:, :, :].rearrange("p b (i h) -> p b i h", h=H),
                                sc[:, :, :].rearrange("p b (i h) -> p b i h", h=H),
                                bcast(best[:, :, :], 2, SLOTS), ALU.subtract))
                        else:
                            s4 = sbank[0][:, :].rearrange("p (b k) -> p b k", b=TG)
                            chain.link(nc.vector.tensor_reduce(best[:, :, 0], s4, AX.X, ALU.max))
                            nc.vector.tensor_tensor(sc[:, :, :], s4, bcast(best[:, :, 0], 2, P), ALU.subtract)\
                              .then_inc(sc_done, 1)
                            dve.wait_ge(sc_done, g + 1)
                        if strided:
                            dve.wait_ge(exp_done, g + 1)
                            chain.link(nc.vector.tensor_scalar(p[:, :, P:KW], p[:, :, P:KW], float(cfg["repeats"]), None,
                                                               ALU.mult))
                            chain.link(nc.vector.tensor_reduce(total[:, :, :], by_head(p), AX.X, ALU.add))
                        else:
                            dve.wait_ge(exp_done, g + 1)
                            chain.link(nc.vector.tensor_reduce(total[:, :, 0], p[:, :, :], AX.X, ALU.add))
                        nc.vector.reciprocal(recip[:, :, :], total[:, :, :]).then_inc(total_done, 1)
                    if op[0] == "NORM":
                        dve.wait_ge(av_done, g + 1)
                        dve.wait_ge(total_done, g + 1)
                        for i in range(2):
                            if strided:
                                for b in range(2):
                                    mul = nc.vector.tensor_tensor(
                                        o[:, 2 * i + b, :].rearrange("p (h d) -> p h d", h=H),
                                        vbank[i][:, b * D:(b + 1) * D].rearrange("p (h d) -> p h d", h=H),
                                        bcast(recip[:, 2 * i + b, :], 2, DH), ALU.mult)
                            else:
                                mul = nc.vector.tensor_tensor(
                                    o[:, 2 * i:2 * i + 2, :], vbank[i][:, :].rearrange("p (b d) -> p b d", b=2),
                                    bcast(recip[:, 2 * i:2 * i + 2, 0], 2, D), ALU.mult)
                        mul.then_inc(o_done, 1)
                    if op[0] == "OUT":
                        dve.wait_ge(out_done, g + 1)
                        for i in range(2):
                            add = nc.vector.tensor_tensor(res[:, 2 * i:2 * i + 2, :],
                                                          vbank[i][:, :].rearrange("p (b d) -> p b d", b=2),
                                                          bcast(bo[:, :], 1, 2), ALU.add)
                        add.then_inc(res_done, 1)
                        dve.wait_ge(res_done, g + 1)
                        dst = cfg["dst"][:, bass.ds(g * TG, TG), :]
                        base = ln[:, par, :, :] if affine else dst
                        nc.vector.tensor_tensor(dst, res[:, :, :], base, ALU.add)

            run_groups(dve, emit, G, prologue, middle, last)

        @block.scalar
        def _(act):
            act.wait_ge(w_in, 16 * loads)

            def emit(g, par, ops):
                n = g + 1
                ev = counts(g, ops)
                j = -1
                for op in ops:
                    if len(op) == 3:
                        j += 1
                        if op[2] == "A":
                            act.wait_ge(job_done, ev.filled(j))
                    if op[0] == "lnT":
                        nc.scalar.activation(lnT[:, op[1], :], jbank[j % 2][:, :], ACT.Identity).then_inc(out_of["A"], 1)
                    if op[0] == "q":
                        nc.scalar.activation(qT[:, 1 - par, op[1], :], jbank[j % 2][:, :], ACT.Identity,
                                             bias=bq[:, op[1]:op[1] + 1]).then_inc(out_of["A"], 1)
                    if op[0] == "SOFT":
                        if strided:
                            act.wait_ge(chain_sem, next_links + g * (next_links + own_links) + 3)
                            nc.scalar.activation(p[:, :, :], sc[:, :, :], ACT.Exp).then_inc(exp_done, 1)
                        else:
                            act.wait_ge(sc_done, g + 1)
                            nc.scalar.activation(p[:, :, :], sc[:, :, :], ACT.Exp, scale=cfg["scale"]).then_inc(exp_done, 1)
                    if op[0] == "PT":
                        act.wait_ge(pt_done, g + 1)
                        pe_copy = nc.scalar.activation(pT[:, :, :].rearrange("p b q -> p (b q)"), tbank[:, :], ACT.Identity)
                        if strided:
                            pe_copy = nc.scalar.activation(pxT[:, :, :].rearrange("p b q -> p (b q)"), xbank[0:H, :],
                                                           ACT.Identity)
                        pe_copy.then_inc(pT_done, 1)
                    if op[0] == "OT":
                        act.wait_ge(ot_done, g + 1)
                        for i in range(2):
                            cp = nc.scalar.activation(oT[:, i, :, :, :].rearrange("p b c t -> p (b c t)"), sbank[i][:, :],
                                                      ACT.Identity)
                        cp.then_inc(oT_done, 1)

            run_groups(act, emit, G, prologue, middle, last)

        @block.tensor
        def _(pe):
            pe.wait_ge(w_in, 16 * loads)

            def emit(g, par, ops):
                n = g + 1
                np_ = 1 - par
                ev = counts(g, ops)
                j = -1
                for op in ops:
                    if len(op) == 3:
                        j += 1
                        bank = jbank[j % 2]
                        if ev.before or j >= 2:
                            who, cnt = ev.emptied(j - 2)
                            pe.wait_ge(out_of[who], cnt)
                    if op[0] == "lnT":
                        pe.wait_ge(ln_done, n + 1)
                        for b in range(TG):
                            mm = nc.tensor.transpose(bank[:, b * P:(b + 1) * P], ln[:, np_, b, op[1] * P:(op[1] + 1) * P],
                                                     sh.ident[:, :])
                        mm.then_inc(job_done, 1)
                    if op[0] in ("q", "k"):
                        w, x = (wq, lnT) if op[0] == "q" else (wk, ctxT[:, np_, :, :])
                        if op == ("q", 0, "A"):
                            who, cnt = ev.emptied(ev.place(("lnT", 1)))
                            pe.wait_ge(out_of[who], cnt)
                        if op[0] == "k" and op[1] == 0:
                            pe.wait_ge(ctx_in, 16 * C * (n + 1))
                        for c in range(C):
                            mm = nc.tensor.matmul(bank[:, :], w[:, c, op[1] * P:(op[1] + 1) * P], x[:, c, :],
                                                  start=(c == 0), stop=(c == C - 1))
                        mm.then_inc(job_done, 1)
                    if op[0] == "v":
                        for i in range(2):
                            b = 2 * op[1] + i
                            for c in range(C):
                                mm = nc.tensor.matmul(bank[:, i * D:(i + 1) * D], ctxT[:, np_, c, b * P:(b + 1) * P],
                                                      wv[:, c, :], start=(c == 0), stop=(c == C - 1))
                        mm.then_inc(job_done, 1)
                    if op[0] == "x":
                        for i in range(2):
                            b = 2 * op[1] + i
                            for c in range(C):
                                last_key = ctxT[:, np_, c, (b + 1) * P - 1:(b + 1) * P].broadcast_to([P, H])
                                mm = nc.tensor.matmul(bank[0:H, i * D:(i + 1) * D], last_key, wv[:, c, :],
                                                      start=(c == 0), stop=(c == C - 1))
                        mm.then_inc(job_done, 1)
                    if op[0] == "S":
                        for who in ("A", "V"):
                            pe.wait_ge(out_of[who], (g + 1) * per[who])
                        ge(pe, oT_done, g)
                        for b in range(TG):
                            out = sbank[b // 2][:, (b % 2) * KW:(b % 2 + 1) * KW] if strided else sbank[0][:, b * P:(b + 1) * P]
                            for c in range(C):
                                mm = nc.tensor.matmul(out, qT[:, par, c, b * P:(b + 1) * P], k[:, par, c, b, :],
                                                      start=(c == 0), stop=(c == C - 1))
                        mm.then_inc(s_done, 1)
                    if op[0] == "PT":
                        pe.wait_ge(total_done, g + 1)
                        ge(pe, pT_done, g)
                        for b in range(TG):
                            mm = nc.tensor.transpose(tbank[:, b * P:(b + 1) * P], p[:, b, 0:P], sh.ident[:, :])
                            if strided:
                                mm = nc.tensor.transpose(xbank[0:H, b * P:(b + 1) * P], p[:, b, P:KW], sh.ident[:, :])
                        mm.then_inc(pt_done, 1)
                    if op[0] == "AV":
                        pe.wait_ge(pT_done, g + 1)
                        ge(pe, res_done, g)
                        for b in range(TG):
                            out = vbank[b // 2][:, (b % 2) * D:(b % 2 + 1) * D]
                            mm = nc.tensor.matmul(out, pT[:, b, :], v[:, par, b, :], start=True, stop=not strided)
                            if strided:
                                mm = nc.tensor.matmul(out, pxT[:, b, :], vx[:, par, b, :], start=False, stop=True)
                        mm.then_inc(av_done, 1)
                    if op[0] == "OT":
                        pe.wait_ge(o_done, g + 1)
                        for b in range(TG):
                            for c in range(C):
                                at = ((b % 2) * C + c) * P
                                mm = nc.tensor.transpose(sbank[b // 2][:, at:at + P], o[:, b, c * P:(c + 1) * P], sh.ident[:, :])
                        mm.then_inc(ot_done, 1)
                    if op[0] == "OUT":
                        pe.wait_ge(oT_done, g + 1)
                        for b in range(TG):
                            for c in range(C):
                                mm = nc.tensor.matmul(vbank[b // 2][:, (b % 2) * D:(b % 2 + 1) * D], oT[:, b // 2, b % 2, c, :],
                                                      wo[:, c, :], start=(c == 0), stop=(c == C - 1))
                        mm.then_inc(out_done, 1)

            run_groups(pe, emit, G, prologue, middle, last)


def quantised_weights(nc, name, weights, steps):
    QMAX, SCALING = steps
    ROUND = 1.5 * 2.0 ** 23
    with ExitStack() as ctx:
        m = Memory(nc, ctx, name)
        N = len(weights)
        rank = weights[0][2].shape[0]
        w = [m.sb(f"w{i}", list(x[0].shape)) for i, x in enumerate(weights)]
        t = [m.sb(f"t{i}", list(x[0].shape)) for i, x in enumerate(weights)]
        a = [m.sb(f"a{i}", [rank, x[2].shape[1]]) for i, x in enumerate(weights)]
        b = [m.sb(f"b{i}", [rank, x[3].shape[1]]) for i, x in enumerate(weights)]
        most, most_all, scale, inverse = (m.sb(x, [P, N]) for x in ("most", "most_all", "scale", "inverse"))
        banks = [m.bank(f"bank{i}") for i in range(8)]
        w_in, most_done, all_done, low_done = m.sem("w_in"), m.sem("most"), m.sem("all"), m.sem("low")
        chain_sem = m.sem("chain")
        flat = lambda x: x[:, :, :].rearrange("p c n -> p (c n)")

        def low_rank_pieces():
            at = 0
            for i, x in enumerate(weights):
                _, chunks, cols = x[0].shape
                for c in range(chunks):
                    for n0 in range(0, cols, 512):
                        width = min(512, cols - n0)
                        yield i, c, n0, width, at // 512, at % 512
                        at += width

        block = ctx.enter_context(nc.Block())

        @block.sync
        def _(sp):
            for i, (_, wT, A, BT) in enumerate(weights):
                sp.dma_start(w[i][:, :, :], wT.rearrange("(c p) n -> p c n", p=P)).then_inc(w_in, 16)
                sp.dma_start(a[i][:, :], A).then_inc(w_in, 16)
                sp.dma_start(b[i][:, :], BT).then_inc(w_in, 16)

        @block.gpsimd
        def _(pool):
            pool.wait_ge(most_done, 1)
            nc.gpsimd.partition_all_reduce(most_all[:, :], most[:, :], P, bass.bass_isa.ReduceOp.max).then_inc(all_done, 1)

        @block.tensor
        def _(pe):
            pe.wait_ge(w_in, 48 * N)
            for i, c, n0, width, bank, at in low_rank_pieces():
                mm = nc.tensor.matmul(banks[bank][:, at:at + width], a[i][:, c * P:(c + 1) * P], b[i][:, n0:n0 + width],
                                      start=True, stop=True)
            mm.then_inc(low_done, 1)

        @block.vector
        def _(dve):
            chain = Chain(dve, chain_sem, 0, 0)
            chain.group(-1)
            dve.wait_ge(w_in, 48 * N)
            for i in range(N):
                red = nc.vector.tensor_reduce(most[:, i:i + 1], w[i][:, :, :], AX.XY, ALU.max, apply_absolute_value=True)
            red.then_inc(most_done, 1)
            dve.wait_ge(all_done, 1)
            chain.link(nc.vector.tensor_scalar(scale[:, :], most_all[:, :], 1.0 / QMAX, None, ALU.mult))
            chain.link(nc.vector.reciprocal(inverse[:, :], scale[:, :]))
            for i in range(N):
                chain.link(nc.vector.tensor_scalar(flat(t[i]), flat(w[i]), inverse[:, i:i + 1], None, ALU.mult))
                chain.link(nc.vector.tensor_scalar(flat(t[i]), flat(t[i]), ROUND, ROUND, ALU.add, ALU.subtract))
                chain.link(nc.vector.tensor_scalar(flat(t[i]), flat(t[i]), -QMAX - 1, QMAX, ALU.max, ALU.min))
                chain.link(nc.vector.scalar_tensor_tensor(out=flat(t[i]), in0=flat(t[i]), scalar=scale[:, i:i + 1],
                                                          in1=flat(w[i]), op0=ALU.mult, op1=ALU.subtract))
                chain.link(nc.vector.tensor_tensor(flat(t[i]), flat(t[i]), flat(w[i]), ALU.add))
            dve.wait_ge(low_done, 1)
            for i, c, n0, width, bank, at in low_rank_pieces():
                nc.vector.scalar_tensor_tensor(out=weights[i][0][:, c, n0:n0 + width], in0=banks[bank][:, at:at + width],
                                               scalar=SCALING, in1=t[i][:, c, n0:n0 + width], op0=ALU.mult, op1=ALU.add)


def ffn_quantised(nc, sh, name, G, cfg):
    F = cfg["F"]
    with ExitStack() as ctx:
        m = Memory(nc, ctx, name + "_w")
        w1, w2 = m.sb("w1", [P, C, F]), m.sb("w2", [P, F // P, D])
        quantised_weights(nc, name + "_quant", [(w1, cfg["w1T"], cfg["A1"], cfg["B1T"]), (w2, cfg["w2T"], cfg["A2"], cfg["B2T"])],
                          (127.0, 2.0))
        ffn(nc, sh, name, G, dict(cfg, resident=(w1, w2), affine=None, post=None))

FAR = 1.0e6


class Steps:

    def __init__(self, eng, sem, per):
        self.eng, self.sem, self.per, self.k = eng, sem, per, per

    def at(self, index):
        assert self.k == self.per, (self.k, self.per)
        self.base, self.k = index * self.per, 0

    def link(self, ins):
        self.k += 1
        ins.then_inc(self.sem, 1)
        self.eng.wait_ge(self.sem, self.base + self.k)


def zero_rows(nc, sh, ctx):
    spare = sh.token_rows.shape[0] - sh.NT * P
    m = Memory(nc, ctx, "rows")
    zero = m.sb("zero", [P, D])
    set_, done = m.sem("set"), m.sem("done")
    with nc.Block() as block:
        @block.vector
        def _(dve):
            nc.vector.memset(zero[:, :], 0.0).then_inc(set_, 1)

        @block.sync
        def _(sp):
            sp.wait_ge(set_, 1)
            for table in (sh.token_rows, sh.sum_rows):
                sp.dma_start(table[sh.NT * P:, :].rearrange("(r p) d -> p r d", p=P), bcast(zero[:, :], 1, spare // P))\
                  .then_inc(done, 16)
            sp.wait_ge(done, 32)


def route(nc, sh, name, G, cfg):
    E, K, CAP = cfg["E"], cfg["K"], cfg["CAP"]
    table = cfg["table"]
    NS = table.shape[0]
    with ExitStack() as ctx:
        m = Memory(nc, ctx, name)
        wg = m.sb("wg", [P, C, E])
        bias = m.sb("bias", [P, E]) if cfg["bg"] is not None else None
        sbias = m.sb("sbias", [P, E]) if cfg["sb"] is not None else None
        b2 = m.sb("b2", [E, D]) if cfg["b2"] is not None else None
        expert_no = m.sb("expert_no", [P, E])
        token_no = m.sb("token_no", [P, G * TG], I32)
        before = m.sb("before", [P, P], BF16)
        ones = m.sb("ones", [P, P], BF16)
        initial = m.sb("initial", [P, NS // P, 2], I32)
        stats, moments = m.sb("stats", [P, TG, 6]), m.sb("moments", [P, TG, 2])
        veps, rstd = m.sb("veps", [P, TG]), m.sb("rstd", [P, TG])
        ln = m.sb("ln", [P, 2, TG, D])
        lnT = m.sb("lnT", [P, C, GT])
        logit, prob = m.sb("logit", [P, TG, E]), m.sb("prob", [P, TG, E])
        choice = m.sb("choice", [P, TG, E]) if sbias is not None else prob
        top, total, inv = m.sb("top", [P, TG]), m.sb("total", [P, TG]), m.sb("inv", [P, TG])
        best = m.sb("best", [P, TG, 8])
        best_at = m.sb("best_at", [P, TG, 8], U32)
        at_f = m.sb("at_f", [P, TG, K])
        hot = m.sb("hot", [P, TG * K, E])
        work = m.sb("work", [P, TG * K, E])
        taken = m.sb("taken", [P, 2, TG, E], BF16)
        taken_sum = m.sb("taken_sum", [P, E])
        so_far = m.sb("so_far", [P, 2, E], BF16)
        place = m.sb("place", [P, TG, K])
        weight = m.sb("weight", [P, TG, K])
        slot_f, over = m.sb("slot_f", [P, TG, K]), m.sb("over", [P, TG, K])
        slot = m.sb("slot", [P, 2, TG * K], U32)
        pay = m.sb("pay", [P, 2, TG * K, 2], I32)
        kept = m.sb("kept", [P, TG, K])
        wsum, wT = m.sb("wsum", [P, TG, E]), m.sb("wT", [E, TG, P])
        if CAP is None:
            all_at, all_place = m.sb("all_at", [P, G * TG, K]), m.sb("all_place", [P, G * TG, K])

        tb = [m.bank(f"t{i}") for i in range(C)]
        lbank, pbank, wbank = m.bank("l"), m.bank("p"), m.bank("w")
        bbank = [m.bank(f"b{i}") for i in range(2)]

        w_in, const, const_step = m.sem("w_in"), m.sem("const"), m.sem("const_step")
        table_set = m.sem("table_set")
        pay_out = [sh.pool_dma_sems.pop() for _ in range(2)]
        rows_out = [m.sem(f"rows_out{i}") for i in range(2)]
        stats_done, veps_done, rstd_done, ln_done = m.sem("stats"), m.sem("veps"), m.sem("rstd"), m.sem("ln")
        t_done, lnT_done, l_done = m.sem("t"), m.sem("lnT"), m.sem("l")
        logit_done, exp_done, taken_done, p_done = m.sem("logit"), m.sem("exp"), m.sem("taken"), m.sem("p")
        slot_done, wsum_done, wt_done, wT_done = m.sem("slot"), m.sem("wsum"), m.sem("wt"), m.sem("wT")
        b_done, x_done, x_out = m.sem("b"), m.sem("x"), m.sem("x_out")
        front_sem, back_sem, so_far_done = m.sem("front"), m.sem("back"), m.sem("so_far")

        prologue = [("STATS",), ("LN",), ("T",), ("LG",)]
        bias2 = b2 is not None
        middle = [("SOFT",), ("STATS",), ("PICK",), ("LN",), ("T",), ("PLACE",), ("LG",)] + [("BIAS2",)] * bias2
        last = [("SOFT",), ("PICK",), ("PLACE",)] + [("BIAS2",)] * bias2
        loads = 1 + sum(x is not None for x in (bias, sbias, b2))
        trash0 = sh.NT * P
        block_context = ExitStack()
        block = block_context.enter_context(nc.Block())

        @block.sync
        def _(sp):
            sp.dma_start(wg[:, :, :], cfg["wg"].rearrange("(c p) e -> p c e", p=P)).then_inc(w_in, 16)
            for dst, src in ((bias, cfg["bg"]), (sbias, cfg["sb"])):
                if dst is not None:
                    sp.dma_start(dst[:, :], rows(src)).then_inc(w_in, 16)
            if bias2:
                sp.dma_start(b2[:, :], cfg["b2"]).then_inc(w_in, 16)
            sp.wait_ge(const, 2)
            sp.dma_start(table.rearrange("(p r) c -> p r c", p=P), initial[:, :, :]).then_inc(table_set, 16)

            def emit(g, par, ops):
                n = g + 1
                for op in ops:
                    if op[0] == "T":
                        sp.wait_ge(ln_done, n + 1)
                        sp.dma_start(sh.token_rows[bass.ds(n * GT, GT), :].rearrange("(b t) d -> t b d", t=P),
                                     ln[:, 1 - par, :, :]).then_inc(rows_out[1 - par], 16)
                    if op[0] == "BIAS2":
                        sp.wait_ge(x_done, g + 1)
                        sp.dma_start(sh.sum_rows[bass.ds(g * GT, GT), :].rearrange("(b t) d -> t b d", t=P),
                                     cfg["src"][:, bass.ds(g * TG, TG), :]).then_inc(x_out, 16)

            run_groups(sp, emit, G, prologue, middle, last)
            for sem in rows_out:
                sp.wait_ge(sem, 16 * (G // 2))
            ge(sp, x_out, 16 * G * bias2)

        @block.gpsimd
        def _(pool):
            nc.gpsimd.iota(expert_no[:, :], [[1, E]], base=0, channel_multiplier=0,
                           allow_small_or_imprecise_dtypes=True)
            nc.gpsimd.iota(token_no[:, :], [[P, G * TG]], base=0, channel_multiplier=1)
            nc.gpsimd.memset(ones[:, :], 1.0)
            nc.gpsimd.memset(before[:, :], 1.0).then_inc(const_step, 1)
            pool.wait_ge(const_step, 1)
            nc.gpsimd.affine_select(out=before[:, :], in_=before[:, :], compare_op=ALU.is_gt, fill=0.0, base=0,
                                    pattern=[[1, P]], channel_multiplier=-1).then_inc(const, 1)
            nc.gpsimd.memset(initial[:, :, 1], 0).then_inc(const_step, 1)
            pool.wait_ge(const_step, 2)
            nc.gpsimd.iota(initial[:, :, 0], cfg["trash"][0], base=trash0, channel_multiplier=cfg["trash"][1])\
              .then_inc(const, 1)

            def emit(g, par, ops):
                n = g + 1
                for op in ops:
                    if op[0] == "STATS":
                        pool.wait_ge(stats_done, n + 1)
                        settle(pool, sh)
                        nc.gpsimd.tensor_scalar(veps[:, :], moments[:, :, 1], cfg["eps"], None, ALU.add)\
                          .then_inc(veps_done, 1)
                        pool.wait_ge(veps_done, n + 1)
                        nc.gpsimd.tensor_tensor(rstd[:, :], veps[:, :], sh.power[:, :], ALU.pow).then_inc(rstd_done, 1)
                    if op[0] == "PLACE" and CAP is not None:
                        pool.wait_ge(slot_done, g + 1)
                        settle(pool, sh)
                        if isinstance(g, int) and g == 0:
                            pool.wait_ge(table_set, 16)
                        for i in range(TG * K):
                            nc.gpsimd.indirect_dma_start(
                                table, bass.IndirectOffsetOnAxis(ap=slot[:, par, i:i + 1], axis=0), pay[:, par, i, :], None,
                                bounds_check=NS - 1, oob_is_err=False).then_inc(pay_out[par], 16)

            run_groups(pool, emit, G, prologue, middle, last)
            if CAP is not None:
                for sem in pay_out:
                    pool.wait_ge(sem, 8 * G * TG * K)

        @block.vector
        def _(dve):
            dve.wait_ge(w_in, 16 * loads)
            dve.wait_ge(const, 2)
            nc.vector.memset(so_far[:, 0, :], 0.0).then_inc(so_far_done, 1)
            front = Steps(dve, front_sem, 1)
            per = 11 + (bias is not None) + (sbias is not None) + 2 * (cfg["weight"] == "score")
            per += 3 * (CAP is not None) + 2 * (bias2 and cfg["weight"] != "one")
            back = Steps(dve, back_sem, per)

            def emit(g, par, ops):
                n = g + 1
                by_k = lambda t: t[:, :, :].rearrange("p (b k) e -> p b k e", b=TG)
                for op in ops:
                    if op[0] == "STATS":
                        front.at(n)
                        for b in range(TG):
                            bn = nc.vector.bn_stats(stats[:, b, :], tile_of(cfg["src"], n * TG + b))
                        front.link(bn)
                        settle(dve, sh)
                        for b in range(TG):
                            bn = nc.vector.bn_aggr(moments[:, b, :], stats[:, b, :])
                        bn.then_inc(stats_done, 1)
                    if op[0] == "LN":
                        dve.wait_ge(rstd_done, n + 1)
                        ge(dve, rows_out[1 - par], 8 * n if par == 1 else 8 * (n - 1))
                        for b in range(TG):
                            lnop = nc.vector.tensor_scalar(ln[:, 1 - par, b, :], tile_of(cfg["src"], n * TG + b),
                                                           moments[:, b, 0:1], rstd[:, b:b + 1], ALU.subtract, ALU.mult)
                        lnop.then_inc(ln_done, 1)
                    if op[0] == "SOFT":
                        back.at(g)
                        dve.wait_ge(l_done, g + 1)
                        logits = lbank[:, 0:TG * E].rearrange("p (b e) -> p b e", b=TG)
                        if bias is not None:
                            back.link(nc.vector.tensor_tensor(logit[:, :, :], logits, bcast(bias[:, :], 1, TG), ALU.add))
                            logits = logit[:, :, :]
                        back.link(nc.vector.tensor_reduce(top[:, :], logits, AX.X, ALU.max))
                        nc.vector.tensor_tensor(logit[:, :, :], logits, bcast(top[:, :], 2, E), ALU.subtract)\
                          .then_inc(logit_done, 1)
                    if op[0] == "PICK":
                        dve.wait_ge(exp_done, g + 1)
                        back.link(nc.vector.tensor_reduce(total[:, :], prob[:, :, :], AX.X, ALU.add))
                        back.link(nc.vector.reciprocal(inv[:, :], total[:, :]))
                        back.link(nc.vector.tensor_tensor(prob[:, :, :], prob[:, :, :], bcast(inv[:, :], 2, E), ALU.mult))
                        if sbias is not None:
                            back.link(nc.vector.tensor_tensor(choice[:, :, :], prob[:, :, :], bcast(sbias[:, :], 1, TG),
                                                              ALU.add))
                        settle(dve, sh)
                        for b in range(TG):
                            mx = nc.vector.max(best[:, b, :], choice[:, b, :])
                        back.link(mx)
                        settle(dve, sh)
                        for b in range(TG):
                            mx = nc.vector.max_index(best_at[:, b, :], best[:, b, :], choice[:, b, :])
                        back.link(mx)
                        settle(dve, sh)
                        back.link(nc.vector.tensor_copy(at_f[:, :, :], best_at[:, :, 0:K]))
                        back.link(nc.vector.tensor_tensor(hot[:, :, :], bcast(expert_no[:, :], 1, TG * K),
                                                          bcast(at_f[:, :, :].rearrange("p b k -> p (b k)"), 2, E),
                                                          ALU.is_equal))
                        with nc.allow_low_precision(reason="zeroes and ones"):
                            nc.vector.tensor_reduce(taken[:, par, :, :], by_k(hot).rearrange("p b k e -> p b e k"), AX.X,
                                                    ALU.add).then_inc(taken_done, 1)
                        dve.wait_ge(taken_done, g + 1)
                        back.link(nc.vector.tensor_reduce(taken_sum[:, :], taken[:, par, :, :].rearrange("p b e -> p e b"),
                                                          AX.X, ALU.add))
                        dve.wait_ge(so_far_done, g + 1)
                        nc.vector.tensor_tensor(so_far[:, 1 - par, :], so_far[:, par, :], taken_sum[:, :], ALU.add)\
                          .then_inc(so_far_done, 1)
                        if cfg["weight"] == "score":
                            back.link(nc.vector.tensor_tensor(by_k(work), by_k(hot), bcast(prob[:, :, :], 2, K), ALU.mult))
                            back.link(nc.vector.tensor_reduce(weight[:, :, :], by_k(work), AX.X, ALU.add))
                    if op[0] == "PLACE":
                        dve.wait_ge(p_done, g + 1)
                        places = pbank[:, 0:TG * E].rearrange("p (b e) -> p b e", b=TG)
                        back.link(nc.vector.tensor_tensor(by_k(work), by_k(hot), bcast(places, 2, K), ALU.mult))
                        back.link(nc.vector.tensor_reduce(place[:, :, :], by_k(work), AX.X, ALU.add))
                        if CAP is None:
                            nc.vector.tensor_copy(all_at[:, bass.ds(g * TG, TG), :], at_f[:, :, :])
                            nc.vector.tensor_copy(all_place[:, bass.ds(g * TG, TG), :], place[:, :, :]).then_inc(slot_done, 1)
                        else:
                            back.link(nc.vector.tensor_scalar(over[:, :, :], place[:, :, :], float(CAP), FAR, ALU.is_ge,
                                                              ALU.mult))
                            back.link(nc.vector.tensor_scalar(slot_f[:, :, :], place[:, :, :], float(E), None, ALU.mult))
                            back.link(nc.vector.tensor_tensor(slot_f[:, :, :], slot_f[:, :, :], at_f[:, :, :], ALU.add))
                            ge(dve, pay_out[par], 8 * TG * K * (g if par == 0 else g - 1))
                            nc.vector.tensor_tensor(slot[:, par, :].rearrange("p (b k) -> p b k", b=TG), slot_f[:, :, :],
                                                    over[:, :, :], ALU.add)
                            pay4 = pay[:, par, :, :].rearrange("p (b k) c -> p b k c", b=TG)
                            nc.vector.tensor_copy(pay4[:, :, :, 0], bcast(token_no[:, bass.ds(g * TG, TG)], 2, K))
                            w = best[:, :, 0:K] if cfg["weight"] == "best" else weight[:, :, :]
                            nc.vector.tensor_copy(pay4[:, :, :, 1].bitcast(F32), w).then_inc(slot_done, 1)
                        if bias2 and cfg["weight"] == "one":
                            nc.vector.tensor_copy(wsum[:, :, :], taken[:, par, :, :]).then_inc(wsum_done, 1)
                        if bias2 and cfg["weight"] == "best":
                            back.link(nc.vector.tensor_scalar(kept[:, :, :], place[:, :, :], float(CAP), None, ALU.is_lt))
                            back.link(nc.vector.tensor_tensor(kept[:, :, :], kept[:, :, :], best[:, :, 0:K], ALU.mult))
                            nc.vector.tensor_tensor(wsum[:, :, :], hot[:, :, :], bcast(kept[:, :, 0], 2, E), ALU.mult)\
                              .then_inc(wsum_done, 1)
                    if op[0] == "BIAS2":
                        dve.wait_ge(b_done, g + 1)
                        for i in range(2):
                            dst = cfg["src"][:, bass.ds(g * TG + 2 * i, 2), :]
                            add = nc.vector.tensor_tensor(dst, bbank[i][:, :].rearrange("p (b d) -> p b d", b=2), dst, ALU.add)
                        add.then_inc(x_done, 1)

            run_groups(dve, emit, G, prologue, middle, last)

        @block.scalar
        def _(act):
            def emit(g, par, ops):
                n = g + 1
                for op in ops:
                    if op[0] == "T":
                        for c in range(C):
                            act.wait_ge(t_done, n * C + c + 1)
                            nc.scalar.activation(lnT[:, c, :], tb[c][:, :], ACT.Identity).then_inc(lnT_done, 1)
                    if op[0] == "SOFT":
                        act.wait_ge(logit_done, g + 1)
                        nc.scalar.activation(prob[:, :, :], logit[:, :, :], ACT.Exp).then_inc(exp_done, 1)
                    if op[0] == "BIAS2":
                        act.wait_ge(wt_done, g + 1)
                        nc.scalar.activation(wT[:, :, :].rearrange("e b t -> e (b t)"), wbank[0:E, :], ACT.Identity)\
                          .then_inc(wT_done, 1)

            run_groups(act, emit, G, prologue, middle, last)

        @block.tensor
        def _(pe):
            pe.wait_ge(w_in, 16 * loads)
            pe.wait_ge(const, 2)

            def emit(g, par, ops):
                n = g + 1
                for op in ops:
                    if op[0] == "T":
                        pe.wait_ge(ln_done, n + 1)
                        ge(pe, lnT_done, n * C)
                        for c in range(C):
                            for b in range(TG):
                                mm = nc.tensor.transpose(tb[c][:, b * P:(b + 1) * P], ln[:, 1 - par, b, c * P:(c + 1) * P],
                                                         sh.ident[:, :])
                            mm.then_inc(t_done, 1)
                    if op[0] == "LG":
                        pe.wait_ge(lnT_done, (n + 1) * C)
                        ge(pe, logit_done, n)
                        for b in range(TG):
                            for c in range(C):
                                mm = nc.tensor.matmul(lbank[:, b * E:(b + 1) * E], lnT[:, c, b * P:(b + 1) * P], wg[:, c, :],
                                                      start=(c == 0), stop=(c == C - 1))
                        mm.then_inc(l_done, 1)
                    if op[0] == "PLACE":
                        pe.wait_ge(taken_done, g + 1)
                        pe.wait_ge(so_far_done, g + 1)
                        for b in range(TG):
                            out = pbank[:, b * E:(b + 1) * E]
                            nc.tensor.matmul(out, before[:, :], taken[:, par, b, :], start=True, stop=False)
                            for a in range(b):
                                nc.tensor.matmul(out, ones[:, :], taken[:, par, a, :], start=False, stop=False)
                            mm = nc.tensor.matmul(out, ones[:, :], so_far[:, par, :], start=False, stop=True)
                        mm.then_inc(p_done, 1)
                    if op[0] == "BIAS2":
                        pe.wait_ge(wsum_done, g + 1)
                        ge(pe, wT_done, g)
                        for b in range(TG):
                            mm = nc.tensor.transpose(wbank[0:E, b * P:(b + 1) * P], wsum[:, b, :], sh.ident[:, :])
                        mm.then_inc(wt_done, 1)
                        pe.wait_ge(wT_done, g + 1)
                        ge(pe, x_done, g)
                        for b in range(TG):
                            mm = nc.tensor.matmul(bbank[b // 2][:, (b % 2) * D:(b % 2 + 1) * D], wT[:, b, :], b2[:, :],
                                                  start=True, stop=True)
                        mm.then_inc(b_done, 1)

            run_groups(pe, emit, G, prologue, middle, last)

        block_context.close()
        if CAP is None:
            place_in_tiles(nc, sh, m, cfg, all_at, all_place, so_far, ones, expert_no, token_no,
                           table_set)


def place_in_tiles(nc, sh, m, cfg, all_at, all_place, so_far, ones, expert_no, token_no, table_set):
    E, K, table, tile_expert = cfg["E"], cfg["K"], cfg["table"], cfg["tile_expert"]
    TILES = table.shape[0] // P
    NK = sh.NT * K
    WHOLE = 1.5 * 2.0 ** 23
    DOWN = 0.5 - 1.0 / (2 * P)
    filled, ends = m.sb("filled", [P, E]), m.sb("ends", [P, E + 1])
    hot = m.sb("all_hot", [P, NK, E])
    start, full, row = (m.sb(x, [P, NK]) for x in ("start", "full", "row"))
    slot = m.sb("all_slot", [P, NK], U32)
    pay = m.sb("all_pay", [P, NK, 2], I32)
    tile_no = m.sb("tile_no", [P, TILES])
    after = m.sb("after", [P, TILES, E - 1])
    expert = m.sb("expert", [P, TILES])
    bank = m.bank("count")
    count_done, no_done, slots_done, out = m.sem("count"), m.sem("tile_no"), m.sem("all_slots"), sh.pool_dma_sems.pop()
    step = m.sem("place_step")
    with nc.Block() as block:
        @block.tensor
        def _(pe):
            nc.tensor.matmul(bank[:, 0:E], ones[:, :], so_far[:, 0, :], start=True, stop=True).then_inc(count_done, 1)

        @block.gpsimd
        def _(pool):
            nc.gpsimd.iota(tile_no[:, :], [[1, TILES]], base=0, channel_multiplier=0, allow_small_or_imprecise_dtypes=True)\
              .then_inc(no_done, 1)
            pool.wait_ge(slots_done, 1)
            pool.wait_ge(table_set, 16)
            for i in range(NK):
                nc.gpsimd.indirect_dma_start(table, bass.IndirectOffsetOnAxis(ap=slot[:, i:i + 1], axis=0), pay[:, i, :],
                                             None, bounds_check=table.shape[0] - 1, oob_is_err=False).then_inc(out, 16)
            pool.wait_ge(out, 16 * NK)

        @block.vector
        def _(dve):
            steps = Steps(dve, step, 14 + E)
            steps.at(0)
            dve.wait_ge(count_done, 1)
            steps.link(nc.vector.tensor_scalar(filled[:, :], bank[:, 0:E], P - 1.0, 1.0 / P, ALU.add, ALU.mult))
            steps.link(nc.vector.tensor_scalar(filled[:, :], filled[:, :], -DOWN, WHOLE, ALU.add, ALU.add))
            steps.link(nc.vector.tensor_scalar(filled[:, :], filled[:, :], WHOLE, None, ALU.subtract))
            steps.link(nc.vector.memset(ends[:, 0:1], 0.0))
            for e in range(E):
                steps.link(nc.vector.tensor_tensor(ends[:, e + 1:e + 2], ends[:, e:e + 1], filled[:, e:e + 1], ALU.add))
            flat = lambda t: t[:, :, :].rearrange("p b k -> p (b k)")
            steps.link(nc.vector.tensor_tensor(hot[:, :, :], bcast(expert_no[:, :], 1, NK), bcast(flat(all_at), 2, E),
                                               ALU.is_equal))
            steps.link(nc.vector.tensor_tensor(hot[:, :, :], hot[:, :, :], bcast(ends[:, 0:E], 1, NK), ALU.mult))
            steps.link(nc.vector.tensor_reduce(start[:, :], hot[:, :, :], AX.X, ALU.add))
            steps.link(nc.vector.tensor_scalar(full[:, :], flat(all_place), 1.0 / P, -DOWN, ALU.mult, ALU.add))
            steps.link(nc.vector.tensor_scalar(full[:, :], full[:, :], WHOLE, WHOLE, ALU.add, ALU.subtract))
            steps.link(nc.vector.scalar_tensor_tensor(out=row[:, :], in0=full[:, :], scalar=-float(P), in1=flat(all_place),
                                                      op0=ALU.mult, op1=ALU.add))
            steps.link(nc.vector.tensor_tensor(start[:, :], start[:, :], full[:, :], ALU.add))
            nc.vector.scalar_tensor_tensor(out=slot[:, :], in0=row[:, :], scalar=float(TILES), in1=start[:, :],
                                           op0=ALU.mult, op1=ALU.add)
            steps.link(nc.vector.memset(pay[:, :, 1], 0))
            nc.vector.tensor_copy(pay[:, :, 0].rearrange("p (t k) -> p t k", k=K), bcast(token_no[:, :], 2, K))\
              .then_inc(slots_done, 1)
            dve.wait_ge(no_done, 1)
            steps.link(nc.vector.tensor_tensor(after[:, :, :], bcast(tile_no[:, :], 2, E - 1),
                                               bcast(ends[:, 1:E], 1, TILES), ALU.is_ge))
            steps.link(nc.vector.tensor_reduce(expert[:, :], after[:, :, :], AX.X, ALU.add))
            nc.vector.tensor_copy(tile_expert[:, :], expert[:, :])


def experts(nc, sh, name, cfg):
    T, S, U, F = cfg["TILES"], cfg["S"], cfg["unroll"], cfg["F"]
    gated = cfg.get("w3T") is not None
    FW = F // 2 if gated else P
    NF = F // FW
    WIDTH = 2 * F if gated else F
    SLOTS = 4
    with ExitStack() as ctx:
        m = Memory(nc, ctx, name)
        if gated:
            w1 = m.sb("w1", [P, SLOTS, C, WIDTH])
            w2 = m.sb("w2", [FW, SLOTS, NF, D])
            sil = m.sb("sil", [S, 2, F])
        else:
            w1, w2, b1 = cfg["w1"], cfg["w2"], cfg["b1"]
        tab = m.sb("tab", [S, T, 2], I32)
        gather_at = m.sb("gather_at", [S, 2], U32)
        scatter_at = m.sb("scatter_at", [S, 2], U32)
        xg = m.sb("xg", [S, 2, D])
        xT = m.sb("xT", [P, 2, C, S])
        g = m.sb("g", [S, 2, F])
        hT = m.sb("hT", [FW, NF, S])
        y = m.sb("y", [S, 2, D])

        HB = -(-WIDTH // 512)
        hbank = [[m.bank(f"h{i}_{j}") for j in range(HB)] for i in range(2)]
        thbank = [m.bank(f"th{j}") for j in range(-(-NF * S // 512))]
        per_th = 512 // S if not gated else NF
        txbank, ybank = m.bank("txbank"), m.bank("ybank")

        tab_in = m.sem("tab_in")
        w_in = [m.sem(f"w_in{i}") for i in range(SLOTS)] if gated else None
        gather_at_done = m.sem("gather_at")
        gather_done = [sh.pool_dma_sems.pop() for _ in range(2)]
        scatter_done = sh.pool_dma_sems.pop()
        tx_done, xT_done, h_done, sil_done, g_done = m.sem("tx"), m.sem("xT"), m.sem("h"), m.sem("sil"), m.sem("g")
        th_done, hT_done, y_done, out_done = m.sem("th"), m.sem("hT"), m.sem("y"), m.sem("out")

        def run_tiles(emit, eng):
            ends = -(-3 // U)
            for u in range(U):
                emit(u, u)
            with eng.Fori(1, T // U - ends) as t:
                for u in range(U):
                    emit(t * U + u, u)
            for s in range(T - ends * U, T):
                emit(s, s % U)
            emit(T, 0)

        def exists(i):
            return not isinstance(i, (int, np.integer)) or 0 <= i < T

        def gathered(i, par):
            return 8 * i + 16 if par == 0 else 8 * i + 8

        block = ctx.enter_context(nc.Block())

        @block.sync
        def _(sp):
            for src, part in cfg["table"]:
                sp.dma_start(tab[:, part, :], src).then_inc(tab_in, 16)

            def load(i, u):
                if gated and exists(i):
                    ge(sp, y_done, i - SLOTS + 1)
                    for half, src in ((0, cfg["w1T"]), (1, cfg["w3T"])):
                        sp.dma_start(w1[:, u % SLOTS, :, half * F:(half + 1) * F],
                                     src[bass.ds(i, 1), :, :].rearrange("o (c p) n -> p (o c) n", p=P))\
                          .then_inc(w_in[u % SLOTS], 16)
                    sp.dma_start(w2[:, u % SLOTS, :, :],
                                 cfg["w2T"][bass.ds(i, 1), :, :].rearrange("o (c p) n -> p (o c) n", p=FW))\
                      .then_inc(w_in[u % SLOTS], 16)

            if gated:
                run_tiles(load, sp)

        @block.gpsimd
        def _(pool):
            def gather(i, par):
                if exists(i):
                    pool.wait_ge(gather_at_done, i + 1)
                    ge(pool, tx_done, i - 1)
                    settle(pool, sh)
                    nc.gpsimd.indirect_dma_start(xg[:, par, :], None, sh.token_rows,
                                                 bass.IndirectOffsetOnAxis(ap=gather_at[:, par:par + 1], axis=0))\
                      .then_inc(gather_done[par], 16)

            def step(s, u):
                gather(s + 2, u % 2)
                if exists(s - 1):
                    pool.wait_ge(out_done, s)
                    ge(pool, scatter_done, 16 * (s - 1))
                    settle(pool, sh)
                    par = (u + 1) % 2
                    nc.gpsimd.indirect_dma_start(sh.sum_rows, bass.IndirectOffsetOnAxis(ap=scatter_at[:, par:par + 1], axis=0),
                                                 y[:, par, :], None, compute_op=ALU.add).then_inc(scatter_done, 16)

            gather(0, 0)
            gather(1, 1)
            run_tiles(step, pool)
            pool.wait_ge(scatter_done, 16 * T)

        @block.vector
        def _(dve):
            dve.wait_ge(tab_in, 16 * len(cfg["table"]))

            def indices(i, par):
                if exists(i):
                    ge(dve, gather_done[par], gathered(i - 2, par))
                    nc.vector.tensor_copy(gather_at[:, par:par + 1], tab[:, bass.ds(i, 1), 0]).then_inc(gather_at_done, 1)

            def step(s, u):
                par = u % 2
                if exists(s):
                    dve.wait_ge(sil_done if gated else h_done, s + 1)
                    ge(dve, th_done, s - 1)
                    if gated:
                        gop = nc.vector.tensor_tensor(g[:, par, :], sil[:, par, :], hbank[par][0][0:S, F:2 * F], ALU.mult)
                    else:
                        for j in range(HB):
                            gop = nc.vector.tensor_copy(g[:, par, j * 512:(j + 1) * 512], hbank[par][j][0:S, :])
                    gop.then_inc(g_done, 1)
                if exists(s - 1):
                    i, ipar = s - 1, 1 - par
                    dve.wait_ge(y_done, i + 1)
                    ge(dve, scatter_done, 16 * (i - 1))
                    nc.vector.tensor_copy(scatter_at[:, ipar:ipar + 1], tab[:, bass.ds(i, 1), 0])
                    if cfg["weighted"]:
                        yop = nc.vector.tensor_scalar(y[:, ipar, :], ybank[0:S, 0:D],
                                                      tab[:, bass.ds(i, 1), 1].bitcast(F32), None, ALU.mult)
                    else:
                        yop = nc.vector.tensor_copy(y[:, ipar, :], ybank[0:S, 0:D])
                    yop.then_inc(out_done, 1)
                indices(s + 3, 1 - par)

            indices(0, 0)
            indices(1, 1)
            indices(2, 0)
            run_tiles(step, dve)

        @block.scalar
        def _(act):
            if not gated:
                act.wait_ge(*cfg["w_in"])

            def xT_out(i, par):
                if exists(i):
                    act.wait_ge(tx_done, i + 1)
                    ge(act, h_done, i - 1)
                    nc.scalar.activation(xT[:, par, :, :].rearrange("p c s -> p (c s)"), txbank[:, 0:C * S], ACT.Identity)\
                      .then_inc(xT_done, 1)

            def step(s, u):
                par = u % 2
                if exists(s - 1):
                    i = s - 1
                    act.wait_ge(th_done, i + 1)
                    ge(act, y_done, i)
                    if gated:
                        nc.scalar.activation(hT[:, :, :].rearrange("p f s -> p (f s)"), thbank[0][0:FW, 0:NF * S], ACT.Identity)\
                          .then_inc(hT_done, 1)
                    else:
                        e = cfg["expert"](act, i)
                        for f in range(NF):
                            at = (f % per_th) * S
                            nc.scalar.activation(hT[:, f, :], thbank[f // per_th][:, at:at + S], cfg["act"],
                                                 bias=b1[:, bass.ds(e * NF + f, 1)]).then_inc(hT_done, 1)
                xT_out(s + 1, 1 - par)
                if gated and exists(s):
                    act.wait_ge(h_done, s + 1)
                    ge(act, g_done, s - 1)
                    nc.scalar.activation(sil[:, par, :], hbank[par][0][0:S, 0:F], cfg["act"]).then_inc(sil_done, 1)

            xT_out(0, 0)
            run_tiles(step, act)

        @block.tensor
        def _(pe):
            if not gated:
                pe.wait_ge(*cfg["w_in"])

            def transpose_x(i, par):
                if exists(i):
                    pe.wait_ge(gather_done[par], gathered(i, par))
                    ge(pe, xT_done, i)
                    for c in range(C):
                        tr = nc.tensor.transpose(txbank[:, c * S:(c + 1) * S], xg[:, par, c * P:(c + 1) * P], sh.ident[0:S, 0:S])
                    tr.then_inc(tx_done, 1)

            def step(s, u):
                par = u % 2
                if exists(s - 1):
                    pe.wait_ge(g_done, s)
                    ge(pe, hT_done, (s - 1) * (1 if gated else NF))
                    for f in range(NF):
                        at = (f % per_th) * S
                        tr = nc.tensor.transpose(thbank[f // per_th][0:FW, at:at + S], g[:, 1 - par, f * FW:(f + 1) * FW],
                                                 sh.ident[0:S, 0:S])
                    tr.then_inc(th_done, 1)
                transpose_x(s + 1, 1 - par)
                if exists(s):
                    pe.wait_ge(xT_done, s + 1)
                    ge(pe, g_done, s - 1)
                    if gated:
                        k = u % SLOTS
                        pe.wait_ge(w_in[k], (s - k) * (48 // SLOTS) + 48)
                        for c in range(C):
                            mm = nc.tensor.matmul(hbank[par][0][0:S, 0:WIDTH], xT[:, par, c, :], w1[:, k, c, :],
                                                  start=(c == 0), stop=(c == C - 1))
                    else:
                        e = cfg["expert"](pe, s)
                        for j in range(HB):
                            for c in range(C):
                                mm = nc.tensor.matmul(hbank[par][j][0:S, :], xT[:, par, c, :],
                                                      w1[:, c, bass.ds(e * F + j * 512, 512)], start=(c == 0), stop=(c == C - 1))
                    mm.then_inc(h_done, 1)
                if exists(s - 1):
                    i = s - 1
                    ge(pe, out_done, i)
                    if not gated:
                        e = cfg["expert"](pe, i)
                    for f in range(NF):
                        if gated:
                            if f == 0:
                                pe.wait_ge(hT_done, i + 1)
                            rhs = w2[:, (u - 1) % SLOTS, f, :]
                        else:
                            pe.wait_ge(hT_done, i * NF + f + 1)
                            rhs = w2[:, f, bass.ds(e * D, D)]
                        mm = nc.tensor.matmul(ybank[0:S, 0:D], hT[:, f, :], rhs, start=(f == 0), stop=(f == NF - 1))
                    mm.then_inc(y_done, 1)

            transpose_x(0, 0)
            run_tiles(step, pe)


def resident_experts(nc, m, E, F, w1_dram, w2_dram, b1_dram):
    w1 = m.sb("w1", [P, C, E * F])
    w2 = m.sb("w2", [P, F // P, E * D])
    b1 = m.sb("b1", [P, E * (F // P)])
    w_in = m.sem("w_in")
    with nc.Block() as block:
        @block.sync
        def _(sp):
            sp.dma_start(b1[:, :], b1_dram.rearrange("e (f p) -> p (e f)", p=P), allow_slow_non_contiguous=True)\
              .then_inc(w_in, 16)
            for e in range(E):
                sp.dma_start(w1[:, :, e * F:(e + 1) * F], w1_dram[e].rearrange("(c p) f -> p c f", p=P)).then_inc(w_in, 16)
                sp.dma_start(w2[:, :, e * D:(e + 1) * D], w2_dram[e].rearrange("(f p) d -> p f d", p=P)).then_inc(w_in, 16)
    return w1, w2, b1, (w_in, 16 * (2 * E + 1))


def ffn_all_resident_routed(nc, sh, name, G, cfg):
    with ExitStack() as ctx:
        m = Memory(nc, ctx, name)
        T, S, F, E = cfg["TILES"], cfg["S"], cfg["F"], cfg["E"]
        tile_expert = m.sb("tile_expert", [P, T], I32)
        w1, w2, b1, w_in = resident_experts(nc, m, E, F, cfg["w1"], cfg["w2"], cfg["b1"])
        route(nc, sh, name + "_route", G, dict(cfg, tile_expert=tile_expert))
        if cfg["CAP"] is None:
            views = [(cfg["table"].rearrange("(r t) c -> r t c", t=T), slice(0, T))]
        else:
            HALVES = T // E
            parts = cfg["table"].rearrange("(h r e) c -> h r e c", r=S, e=E)
            views = [(parts[h], slice(h, T, HALVES)) for h in range(HALVES)]
            numbered = m.sem("numbered")
            with nc.Block() as block:
                @block.gpsimd
                def _(pool):
                    nc.gpsimd.iota(tile_expert[:, :].rearrange("p (e h) -> p e h", h=HALVES), [[1, E], [0, HALVES]], base=0,
                                   channel_multiplier=0).then_inc(numbered, 1)
                    pool.wait_ge(numbered, 1)

        def expert(eng, i):
            settle(eng, sh)
            return eng.value_load(tile_expert[0:1, bass.ds(i, 1)], min_val=0, max_val=E - 1)

        experts(nc, sh, name + "_tiles", dict(TILES=T, S=S, table=views, unroll=cfg["unroll"],
                                              weighted=cfg["weight"] != "one", F=F, w1=w1, w2=w2, b1=b1, w_in=w_in,
                                              act=cfg["act"], expert=expert))
        reload = m.sem("reload")
        with nc.Block() as block:
            @block.sync
            def _(sp):
                sp.dma_start(sh.X[:, :, :], sh.sum_rows[0:sh.NT * P, :].rearrange("(b t) d -> t b d", t=P)).then_inc(reload, 16)
                sp.wait_ge(reload, 16)


def shared_expert(nc, sh, name, G, cfg):
    with ExitStack() as ctx:
        m = Memory(nc, ctx, name)
        F = cfg["F"]
        NF = 4
        FW = F // NF
        w13 = [m.sb(x, [P, C, F]) for x in ("w1", "w3")]
        w2 = m.sb("w2", [FW, NF, D])
        stats, moments = m.sb("stats", [P, TG, 6]), m.sb("moments", [P, TG, 2])
        veps, rstd = m.sb("veps", [P, TG]), m.sb("rstd", [P, TG])
        ln = m.sb("ln", [P, 2, TG, D])
        lnT = m.sb("lnT", [P, 2, C, GT])
        sil = m.sb("sil", [FW, 2, GT])
        hT = m.sb("hT", [FW, 2, NF, GT])

        hbank = [[m.bank(f"h{i}_{j}") for j in range(2)] for i in range(2)]
        ybank = [m.bank(f"y{i}") for i in range(2)]
        tbank = [m.bank(f"t{i}") for i in range(C)]

        w_in = m.sem("w_in")
        stats_done, veps_done, rstd_done, ln_done = m.sem("stats"), m.sem("veps"), m.sem("rstd"), m.sem("ln")
        chain_sem = m.sem("chain")
        t_done, lnT_done = m.sem("t"), m.sem("lnT")
        h_done, sil_done, gate_done, y_done, out_done = m.sem("h"), m.sem("sil"), m.sem("gate"), m.sem("y"), m.sem("out")

        H_ = [("H", f) for f in range(NF)]
        prologue = [("STATS",), ("LN",), ("lnT", 0), ("lnT", 1)]
        middle = H_[:1] + [("STATS",)] + H_[1:3] + [("LN",)] + H_[3:] + [("lnT", 0), ("lnT", 1), ("OUT",)]
        last = H_ + [("OUT",)]
        block = ctx.enter_context(nc.Block())

        @block.sync
        def _(sp):
            for dst, src in zip(w13, (cfg["w1T"], cfg["w3T"])):
                sp.dma_start(dst[:, :, :], src.rearrange("(c p) n -> p c n", p=P)).then_inc(w_in, 16)
            sp.dma_start(w2[:, :, :], cfg["w2T"].rearrange("(c p) n -> p c n", p=FW)).then_inc(w_in, 16)

        @block.gpsimd
        def _(pool):
            def emit(g, par, ops):
                n = g + 1
                for op in ops:
                    if op[0] == "STATS":
                        pool.wait_ge(stats_done, n + 1)
                        settle(pool, sh)
                        nc.gpsimd.tensor_scalar(veps[:, :], moments[:, :, 1], cfg["eps"], None, ALU.add)\
                          .then_inc(veps_done, 1)
                        pool.wait_ge(veps_done, n + 1)
                        nc.gpsimd.tensor_tensor(rstd[:, :], veps[:, :], sh.power[:, :], ALU.pow).then_inc(rstd_done, 1)

            run_groups(pool, emit, G, prologue, middle, last)

        @block.vector
        def _(dve):
            chain = Chain(dve, chain_sem, 1, 1)

            def emit(g, par, ops):
                n = g + 1
                chain.group(g)
                for op in ops:
                    if op[0] == "STATS":
                        for b in range(TG):
                            bn = nc.vector.bn_stats(stats[:, b, :], tile_of(cfg["src"], n * TG + b))
                        chain.link(bn)
                        settle(dve, sh)
                        for b in range(TG):
                            bn = nc.vector.bn_aggr(moments[:, b, :], stats[:, b, :])
                        bn.then_inc(stats_done, 1)
                    if op[0] == "LN":
                        dve.wait_ge(rstd_done, n + 1)
                        for b in range(TG):
                            lnop = nc.vector.tensor_scalar(ln[:, 1 - par, b, :], tile_of(cfg["src"], n * TG + b),
                                                           moments[:, b, 0:1], rstd[:, b:b + 1], ALU.subtract, ALU.mult)
                        lnop.then_inc(ln_done, 1)
                    if op[0] == "H":
                        f = op[1]
                        dve.wait_ge(sil_done, g * NF + f + 1)
                        ge(dve, y_done, g - 1)
                        nc.vector.tensor_tensor(hT[:, par, f, :], sil[:, f % 2, :], hbank[f % 2][1][0:FW, :], ALU.mult)\
                          .then_inc(gate_done, 1)
                    if op[0] == "OUT":
                        dve.wait_ge(y_done, g + 1)
                        for i in range(2):
                            dst = cfg["dst"][:, bass.ds(g * TG + 2 * i, 2), :]
                            add = nc.vector.tensor_tensor(dst, ybank[i][:, :].rearrange("p (b d) -> p b d", b=2), dst, ALU.add)
                        add.then_inc(out_done, 1)

            run_groups(dve, emit, G, prologue, middle, last)

        @block.scalar
        def _(act):
            def emit(g, par, ops):
                n = g + 1
                for op in ops:
                    if op[0] == "lnT":
                        act.wait_ge(t_done, n * C + op[1] + 1)
                        nc.scalar.activation(lnT[:, 1 - par, op[1], :], tbank[op[1]][:, :], ACT.Identity).then_inc(lnT_done, 1)
                    if op[0] == "H":
                        U = g * NF + op[1]
                        act.wait_ge(h_done, U + 1)
                        ge(act, gate_done, U - 1)
                        nc.scalar.activation(sil[:, op[1] % 2, :], hbank[op[1] % 2][0][0:FW, :], cfg["act"]).then_inc(sil_done, 1)

            run_groups(act, emit, G, prologue, middle, last)

        @block.tensor
        def _(pe):
            def emit(g, par, ops):
                n = g + 1
                for op in ops:
                    if op[0] == "lnT":
                        c = op[1]
                        pe.wait_ge(ln_done, n + 1)
                        ge(pe, lnT_done, n * C - C + c + 1 if not isinstance(n, int) or n > 0 else 0)
                        for b in range(TG):
                            tr = nc.tensor.transpose(tbank[c][:, b * P:(b + 1) * P], ln[:, 1 - par, b, c * P:(c + 1) * P],
                                                     sh.ident[:, :])
                        tr.then_inc(t_done, 1)
                    if op[0] == "H":
                        f = op[1]
                        U = g * NF + f
                        if isinstance(g, int) and g == 0 and f == 0:
                            pe.wait_ge(w_in, 48)
                        if f == 0:
                            pe.wait_ge(lnT_done, C * (g + 1))
                        ge(pe, gate_done, U - 1)
                        for j in range(2):
                            for c in range(C):
                                mm = nc.tensor.matmul(hbank[f % 2][j][0:FW, :], w13[j][:, c, f * FW:(f + 1) * FW],
                                                      lnT[:, par, c, :], start=(c == 0), stop=(c == C - 1))
                        mm.then_inc(h_done, 1)
                    if op[0] == "OUT":
                        pe.wait_ge(gate_done, (g + 1) * NF)
                        ge(pe, out_done, g)
                        for b in range(TG):
                            for f in range(NF):
                                mm = nc.tensor.matmul(ybank[b // 2][:, (b % 2) * D:(b % 2 + 1) * D],
                                                      hT[:, par, f, b * P:(b + 1) * P], w2[:, f, :],
                                                      start=(f == 0), stop=(f == NF - 1))
                        mm.then_inc(y_done, 1)

            run_groups(pe, emit, G, prologue, middle, last)


def blocks_kernel(nc, a, out):
    B = a["x"].shape[0]
    G = B // TG
    F = a["L0_xattn_ffn_w1"].shape[1]
    EPS, EPS_L0 = 1e-5, 1e-6

    E0, K0 = a["L0_ffn_Wg"].shape[1], 2
    T0 = B * K0 + E0
    E2, CAP2, S2 = a["L2_ffn_gate_w"].shape[1], 160, 80
    E3, K3, CAP3 = a["L3_ffn_gate_wT"].shape[1], 6, 128
    spare = E2 * CAP2

    def part(prefix, *names):
        return {n.split("_")[-1].lower(): a[prefix + n] for n in names}

    with ExitStack() as ctx:
        sh = Shared()
        sh.NT = B
        sh.X = ctx.enter_context(nc.sbuf_tensor("X", [P, B, D], F32))
        sh.x_dram, sh.ctx_dram, sh.ctxT_dram = a["x"], a["ctx_1024"], a["ctxT"]
        sh.token_rows = nc.dram_tensor("token_rows", [B * P + spare, D], F32, kind="Internal").ap()
        sh.sum_rows = nc.dram_tensor("sum_rows", [B * P + spare, D], F32, kind="Internal").ap()
        table = lambda i, slots: nc.dram_tensor(f"table{i}", [slots, 2], I32, kind="Internal").ap()
        build_constants(nc, sh, ctx)
        zero_rows(nc, sh, ctx)

        with ExitStack() as inner:
            Y = inner.enter_context(nc.sbuf_tensor("Y", [P, B, D], F32))
            attention_heads(nc, sh, "l0sa", G, dict(
                part("L0_xattn_", "sa_wq", "sa_wk", "sa_wv", "sa_wo", "sa_bq", "sa_bk", "sa_bv", "sa_bo"),
                src=sh.X, dst=Y, base="ln", eps=EPS, ctx=False, mask="full",
                mask_dram=a["mask_Bx1xSxS_ik0"].rearrange("b o q k -> b (o q) k"), scale=DH ** -0.5))
            attention_narrow(nc, sh, "l0ca", G, dict(
                part("L0_xattn_", "ca_wq", "ca_wk", "ca_wv", "ca_wo", "ca_bq", "ca_bk", "ca_bv", "ca_bo"),
                kind="strided", src=Y, dst=Y, eps=EPS_L0, affine=(a["L0_xattn_ln1_g"], a["L0_xattn_ln1_b"]),
                repeats=P - P // H, masked=-1e9, mask_dram=a["mask_Bx1x1xS2_if1"].rearrange("b o q k -> b (o q k)"),
                scale=DH ** -0.5))
            ffn(nc, sh, "l0ff", G, dict(
                part("L0_xattn_", "ffn_w1", "ffn_w2", "ffn_b1", "ffn_b2"),
                src=Y, dst=sh.X, eps=EPS_L0, affine=(a["L0_xattn_ln2_g"], a["L0_xattn_ln2_b"]), F=F, act=ACT.Relu,
                post=(a["L0_xattn_ln3_g"], a["L0_xattn_ln3_b"], EPS_L0)))

        ffn_all_resident_routed(nc, sh, "l0moe", G, dict(
            part("L0_ffn_", "Wg", "bg", "W1", "b1", "W2", "b2"),
            src=sh.X, eps=EPS, E=E0, K=K0, CAP=None, sb=None, weight="one", table=table(0, T0 * P), trash=([[0, T0]], 1),
            TILES=T0, S=P, F=F, act=ACT.Relu, unroll=2))

        attention_narrow(nc, sh, "l1att", G, dict(
            part("L1_xattn_", "Wq", "Wk", "Wv", "Wo", "bq", "bk", "bv", "bo"),
            kind="single", src=sh.X, dst=sh.X, eps=EPS, affine=None, scale=D ** -0.5))
        ffn_quantised(nc, sh, "l1ff", G, dict(
            src=sh.X, dst=sh.X, eps=EPS, F=F, act=ACT.Gelu, w1T=a["L1_ffn_W_fcT"], w2T=a["L1_ffn_W_projT"],
            A1=a["L1_ffn_A_fc"], A2=a["L1_ffn_A_proj"], B1T=a["L1_ffn_B_fcT"], B2T=a["L1_ffn_B_projT"],
            b1=a["L1_ffn_b_fc"], b2=a["L1_ffn_b_proj"]))

        attention_heads(nc, sh, "l2att", G, dict(
            wq=a["L2_xattn_W_qT"], wk=a["L2_xattn_W_kT"], wv=a["L2_xattn_W_vT"], wo=a["L2_xattn_W_oT"],
            bq=None, bk=None, bv=None, bo=None, src=sh.X, dst=sh.X, base="dst", eps=EPS, ctx=True, mask="shared",
            mask_dram=a["mask_shared"], scale=DH ** -0.5))
        ffn_all_resident_routed(nc, sh, "l2moe", G, dict(
            part("L2_ffn_", "w1", "b1", "w2", "b2"), wg=a["L2_ffn_gate_w"], bg=a["L2_ffn_gate_b"],
            src=sh.X, eps=EPS, E=E2, K=1, CAP=CAP2, sb=None, weight="best", table=table(2, E2 * CAP2),
            trash=([[1, E2 * CAP2 // P]], E2 * CAP2 // P), TILES=E2 * CAP2 // S2, S=S2, F=F, act=ACT.Gelu_apprx_tanh,
            unroll=2))

        attention_heads(nc, sh, "l3att", G, dict(
            wq=None, wk=None, wv=None, wo=a["L3_xattn_W_outT"], bq=None, bk=None, bv=None, bo=a["L3_xattn_b_out"],
            src=sh.X, dst=sh.X, base="dst", eps=EPS, ctx=True, mask=None, scale=D ** -0.5))
        table3 = table(3, E3 * CAP3)
        route(nc, sh, "l3route", G, dict(
            src=sh.X, eps=EPS, E=E3, K=K3, CAP=CAP3, wg=a["L3_ffn_gate_wT"], bg=None, sb=a["L3_ffn_gate_b"],
            weight="score", b2=None, table=table3, trash=([[0, E3 * CAP3 // P]], 1)))
        shared_expert(nc, sh, "l3shared", G, dict(
            src=sh.X, dst=sh.X, eps=EPS, F=a["L3_ffn_ws1T"].shape[1], w1T=a["L3_ffn_ws1T"], w3T=a["L3_ffn_ws3T"],
            w2T=a["L3_ffn_ws2T"], act=ACT.Silu))
        x_stored = Memory(nc, ctx, "x").sem("stored")
        with nc.Block() as block:
            @block.sync
            def _(sp):
                sp.dma_start(sh.sum_rows[0:B * P, :].rearrange("(b t) d -> t b d", t=P), sh.X[:, :, :]).then_inc(x_stored, 16)
                sp.wait_ge(x_stored, 16)
        experts(nc, sh, "l3moe", dict(
            TILES=E3, S=CAP3, table=[(table3.rearrange("(r e) c -> r e c", e=E3), slice(0, E3))], unroll=4, weighted=True,
            F=a["L3_ffn_w1T"].shape[2], w1T=a["L3_ffn_w1T"], w2T=a["L3_ffn_w2T"], w3T=a["L3_ffn_w3T"], act=ACT.Silu))
        out_stored = Memory(nc, ctx, "out").sem("stored")
        with nc.Block() as block:
            @block.sync
            def _(sp):
                sp.dma_start(out.rearrange("b t d -> (b t) d"), sh.sum_rows[0:B * P, :]).then_inc(out_stored, 16)
                sp.wait_ge(out_stored, 16)


_TRANSPOSED = ["L1_ffn_W_fc", "L1_ffn_W_proj", "L1_ffn_B_fc", "L1_ffn_B_proj", "L2_xattn_W_q", "L2_xattn_W_k",
               "L2_xattn_W_v", "L2_xattn_W_o", "L3_xattn_W_out", "L3_ffn_gate_w", "L3_ffn_w1", "L3_ffn_w2",
               "L3_ffn_w3", "L3_ffn_ws1", "L3_ffn_ws2", "L3_ffn_ws3"]
_OUTS = [((32, 128, 256), "float32")]


def kernel(**inputs):
    import numpy as _np
    import concourse.bacc as _bacc
    from concourse import mybir as _mybir
    from concourse.bass_utils import run_bass_kernel_spmd as _run

    nc = _bacc.Bacc("TRN2", target_bir_lowering=False, num_devices=1)
    laid_out = {}
    for name, value in inputs.items():
        value = _np.asarray(value)
        if name == "mask_1x1xSxS2_bk0":
            laid_out["mask_shared"] = _np.ascontiguousarray(value).reshape(value.shape[2:])
        elif name in _TRANSPOSED:
            laid_out[name + "T"] = _np.swapaxes(value, -1, -2)
        else:
            laid_out[name] = value
    ctx = laid_out["ctx_1024"]
    laid_out["ctxT"] = ctx.transpose(2, 0, 1).reshape(ctx.shape[2], -1)
    arrays, args = {}, {}
    for name, value in laid_out.items():
        arrays[f"in_{name}_dram"] = _np.ascontiguousarray(value)
        args[name] = nc.dram_tensor(f"in_{name}_dram", value.shape, _mybir.dt.from_np(value.dtype), kind="ExternalInput").ap()
    outs = []
    for i, (shape, dtype) in enumerate(_OUTS):
        dt = _mybir.dt.from_np(_np.dtype(dtype))
        outs.append(nc.dram_tensor(f"out_{i}_dram", shape, dt, kind="ExternalOutput").ap())
    blocks_kernel(nc, args, *outs)
    r = _run(nc, [arrays], core_ids=[0])
    return r.results[0]["out_0_dram"]
```

```python
from contextlib import ExitStack

import numpy as np
import concourse.bass as bass
from concourse import mybir

F32 = mybir.dt.float32
BF16 = mybir.dt.bfloat16
I32 = mybir.dt.int32
U32 = mybir.dt.uint32
U8 = mybir.dt.uint8
ACT = mybir.ActivationFunctionType
ALU = mybir.AluOpType
AX = mybir.AxisListType

P = 128
D = 256
C = D // P
H = 16
DH = D // H
HC = P // DH
TG = 4
GT = TG * P
QH = 4
X_LOADS = 3
POOL_DMA_SEMS = 3 * (2 + 3) + 1
MASKED = -float(2 ** 30)


def ge(eng, sem, value):
    if isinstance(value, (int, np.integer)) and value <= 0:
        return
    eng.wait_ge(sem, value)


class Shared:
    pass


class Memory:

    used = []

    def __init__(self, nc, ctx, phase):
        self.nc, self.ctx, self.phase, self.sems = nc, ctx, phase, []
        ctx.callback(self.leave)

    def sb(self, name, shape, dt=F32):
        return self.ctx.enter_context(self.nc.sbuf_tensor(f"{self.phase}_{name}", shape, dt))

    def bank(self, name, dt=F32):
        width = 512 if dt == F32 else 1024
        return self.ctx.enter_context(self.nc.psum_tensor(f"{self.phase}_{name}", [P, width], dt))

    def sem(self, name):
        self.sems.append(self.ctx.enter_context(self.nc.semaphore(f"{self.phase}_{name}")))
        return self.sems[-1]

    def leave(self):
        self.used += [s.num for s in self.sems]


def clear_semaphores(nc, used):
    numbers = sorted(set(used))
    used.clear()
    with nc.Block() as block:
        @block.gpsimd
        def _(pool):
            first = 0
            for i in range(1, len(numbers) + 1):
                if i == len(numbers) or numbers[i] != numbers[i - 1] + 1:
                    pool.sem_clear(range(numbers[first], numbers[i - 1] + 1))
                    first = i


def bcast(ap, axis, count):
    ap = ap.unsqueeze(axis)
    shape = list(ap.shape)
    shape[axis] = count
    return ap.broadcast_to(shape)


def column(vector):
    return vector.rearrange("(c p) -> p c", p=P)


def rows(vector, partitions=P):
    return vector.partition_broadcast(partitions)


class Evacuations:

    def __init__(self, ops, before, job_base, bases):
        self.names, self.jobs = [x[:2] for x in ops], [x[2] for x in ops]
        self.names_before, self.before = [x[:2] for x in before], [x[2] for x in before]
        self.job_base, self.bases = job_base, bases

    def filled(self, j):
        return self.job_base + j + 1

    def emptied(self, j):
        if j >= 0:
            e = self.jobs[j]
            return e, self.bases[e] + self.jobs[:j + 1].count(e)
        e = self.before[j]
        later = self.before[j + 1:] if j < -1 else []
        return e, self.bases[e] - later.count(e)

    def place(self, name):
        here = [i for i, x in enumerate(self.names) if name in (x, x[0])]
        there = [i - len(self.before) for i, x in enumerate(self.names_before) if name in (x, x[0])]
        return (here or there)[-1]

    def place_before(self, name):
        return [i - len(self.before) for i, x in enumerate(self.names_before) if name in (x, x[0])][-1]


def settle(eng, sh):
    eng.sem_inc(sh.settled, 1)


def build_constants(nc, sh, ctx):
    m = Memory(nc, ctx, "const")
    sh.ident = m.sb("ident", [P, P])
    sh.ident_bf = m.sb("ident_bf", [P, P], BF16)
    sh.power = m.sb("power", [P, TG])
    made, copied = m.sem("made"), m.sem("copied")
    sh.x_in = [ctx.enter_context(nc.semaphore(f"x_in{i}")) for i in range(X_LOADS)]
    sh.settled = m.sem("settled")
    sh.pool_dma_sems = [ctx.enter_context(nc.semaphore(f"pool_dma{i}")) for i in range(POOL_DMA_SEMS)]
    with nc.Block() as block:
        @block.gpsimd
        def _(pool):
            nc.gpsimd.memset(sh.ident[:], 0.0).then_inc(made, 1)
            pool.wait_ge(made, 1)
            nc.gpsimd.memset(sh.power[:], -0.5)
            nc.gpsimd.affine_select(out=sh.ident[:], in_=sh.ident[:], compare_op=ALU.not_equal, fill=1.0,
                                    base=0, pattern=[[-1, P]], channel_multiplier=1).then_inc(made, 1)

        @block.vector
        def _(dve):
            dve.wait_ge(made, 2)
            nc.vector.tensor_copy(sh.ident_bf[:], sh.ident[:]).then_inc(copied, 1)

        @block.sync
        def _(sp):
            sp.dma_start(sh.X[:, :, :], sh.x_dram.rearrange("b t d -> t b d")).then_inc(sh.x_in[0], 16)


def attention_heads(nc, sh, name, G, cfg):
    with ExitStack() as ctx:
        m = Memory(nc, ctx, name)
        project = cfg["wq"] is not None
        from_ctx = cfg["ctx"]
        mask = cfg["mask"]

        wq = m.sb("wq", [P, C, D]) if project else None
        wk = m.sb("wk", [P, C, D]) if project else None
        wv = m.sb("wv", [P, C, D]) if project else None
        wo = m.sb("wo", [P, C, D])
        bq = m.sb("bq", [P, C]) if cfg["bq"] is not None else None
        bk = m.sb("bk", [P, C]) if cfg["bk"] is not None else None
        bv = m.sb("bv", [P, D]) if cfg["bv"] is not None else None
        bo = m.sb("bo", [P, D]) if cfg["bo"] is not None else None
        stats = m.sb("stats", [P, TG, 6])
        moments = m.sb("moments", [P, TG, 2])
        veps = m.sb("veps", [P, TG])
        rstd = m.sb("rstd", [P, TG])
        ln = m.sb("ln", [P, 2, TG, D])
        lnT = m.sb("lnT", [P, C, GT])
        ctxT = m.sb("ctxT", [P, C, GT]) if from_ctx and project else None
        qT = m.sb("qT", [P, 2, C, GT])
        kT = m.sb("kT", [P, C, GT]) if project else None
        kblk = [m.sb(f"kblk{i}", [P, C, HC, GT]) for i in range(2)]
        vraw = m.sb("vraw", [P, TG, D]) if not project else None
        vaug = [m.sb(f"vaug{i}", [P, TG, H, DH + 1]) for i in range(2)]
        shifted = m.sb("shifted", [P, 4, QH, P])
        rowmax = m.sb("rowmax", [P, 4, QH])
        e = m.sb("e", [P, 4, QH, P])
        eT = m.sb("eT", [P, 4, QH, P])
        recip = m.sb("recip", [P, 2, H])
        o = m.sb("o", [P, 2, D])
        oT = m.sb("oT", [P, 2, C, P])
        res = m.sb("res", [P, 2, D]) if bo is not None else None
        if mask is not None:
            mask_in = m.sb("mask_in", [P, TG, P], I32) if mask == "full" else m.sb("mask_in", [P, P], U8)
            mask_add = m.sb("mask_add", [P, 2, TG, P], BF16)
            mask_best = m.sb("mask_best", [P, 2, TG])
            expscale = m.sb("expscale", [P, 2, TG])

        sbank = [m.bank(f"s{i}") for i in range(2)]
        tbank = [m.bank(f"t{i}") for i in range(2)]
        vbank = [m.bank(f"v{i}") for i in range(2)]
        jbank = [m.bank(f"j{i}") for i in range(2)]

        w_in = m.sem("w_in")
        zeroed, zeroed_1 = m.sem("zeroed"), m.sem("zeroed_1")
        ctx_in, mask_dma, v_in = m.sem("ctx_in"), m.sem("mask_dma"), m.sem("v_in")
        bn_done, stats_done, veps_done, rstd_done = m.sem("bn"), m.sem("stats"), m.sem("veps"), m.sem("rstd")
        ln_done, best_done, mask_done = m.sem("ln"), m.sem("best"), m.sem("mask")
        job_done = m.sem("job")
        out_of = {"A": m.sem("act_job"), "V": m.sem("dve_job")}
        kblk_done = [[m.sem(f"kblk{i}_{c}") for c in range(C)] for i in range(2)]
        vaug_done = m.sem("vaug")
        s_done, max_done, sub_done, exp_done = m.sem("s"), m.sem("max"), m.sem("sub"), m.sem("exp")
        t_done, eT_done, av_done = m.sem("t"), m.sem("eT"), m.sem("av")
        recip_done, o_done, res_done = m.sem("recip"), m.sem("o"), m.sem("res")

        if project:
            proj = [("lnT", 0, "A", 0), ("lnT", 1, "A", 0), ("q", 0, "V", 0), ("q", 1, "V", 0),
                    ("k", 0, "A", 0), ("k", 1, "A", 0), ("v", 0, "V", 0), ("v", 1, "V", 0)]
            proj_steps = [10, 10, 11, 12, 12, 13, 14, 15]
        else:
            proj = [("lnT", 0, "A", 0), ("lnT", 1, "A", 0)]
            proj_steps = [10, 12]

        STEPS = TG * 4
        STAGES = [([("S", u, None) for u in range(STEPS)], 1, 0),
                  ([("T", u, None) for u in range(STEPS)], 1, 3),
                  ([("AV", u, None) for u in range(STEPS)], 1, 5),
                  ([("NORM", b, None) for b in range(TG)], 4, 8),
                  ([("oT", b, "A") for b in range(TG)], 4, 9),
                  ([("out", b, "V") for b in range(TG)], 4, 11)]
        middle = []
        for step in range(STEPS):
            for stage, every, start in STAGES:
                for i, op in enumerate(stage):
                    if (start + every * i) % STEPS == step:
                        middle.append((*op, -((start + every * i) // STEPS)))
            middle += {5: [("STATS", 0, None, 0)], 9: [("LN", 0, None, 0)]}.get(step, [])
            middle += [p for p, at in zip(proj, proj_steps) if at == step]
        front = ("STATS", "LN", "lnT", "q", "k", "v")
        prologue = [("STATS", 0, None, 0), ("LN", 0, None, 0)] + proj
        first = [x for x in middle if x[3] == 0]
        last = [x for x in middle if x[0] not in front]
        epilogue = [x for x in middle if x[3] == -1]
        jobs_of = lambda ops: [x for x in ops if x[2]]
        JM = jobs_of(middle)
        count = lambda jobs, who: sum(x[2] == who for x in jobs)

        def counts(g, ops):
            jp, jf, jl = jobs_of(prologue), jobs_of(first), jobs_of(last)
            if isinstance(g, int) and g < 0:
                return Evacuations(jp, [], 0, {"A": 0, "V": 0})
            if isinstance(g, int) and g == 0:
                return Evacuations(jobs_of(ops), jp, len(jp), {w: count(jp, w) for w in "AV"})
            before = jl if isinstance(g, int) and g == G else JM
            base = lambda size: size(jp) + size(jf) - size(JM) + (
                (G - 1) * size(JM) + size(jl) if before is jl else g * size(JM))
            return Evacuations(jobs_of(ops), before, base(len),
                               {w: base(lambda jobs: count(jobs, w)) for w in "AV"})

        def run(eng, emit):
            emit(-1, 1, prologue)
            emit(0, 0, first)
            with eng.Fori(0, (G - 2) // 2) as t:
                emit(t * 2 + 1, 1, middle)
                emit(t * 2 + 2, 0, middle)
            emit(G - 1, 1, last)
            emit(G, 0, epilogue)

        def kblk_count(g, par):
            return 8 * HC * (g + 2) if par == 0 else 8 * HC * (g + 1)

        def bank_free(eng, ev, j):
            if not ev.before and j < 2:
                return
            who, n = ev.emptied(j - 2)
            ge(eng, out_of[who], n)

        n_weights = 16 * sum(x is not None for x in (wq, wk, wv, wo, bq, bk, bv, bo))
        block = ctx.enter_context(nc.Block())

        @block.sync
        def _(sp):
            for dst, src in ((wq, cfg["wq"]), (wk, cfg["wk"]), (wv, cfg["wv"]), (wo, cfg["wo"])):
                if dst is not None:
                    sp.dma_start(dst[:, :, :], src.rearrange("(c p) n -> p c n", p=P)).then_inc(w_in, 16)
            for dst, src in ((bq, cfg["bq"]), (bk, cfg["bk"])):
                if dst is not None:
                    sp.dma_start(dst[:, :], column(src), allow_slow_non_contiguous=True).then_inc(w_in, 16)
            for dst, src in ((bv, cfg["bv"]), (bo, cfg["bo"])):
                if dst is not None:
                    sp.dma_start(dst[:, :], rows(src)).then_inc(w_in, 16)
            if mask == "shared":
                sp.dma_start(mask_in[:, :], cfg["mask_dram"]).then_inc(mask_dma, 16)
            sp.wait_ge(zeroed, 2)

            def emit(g0, par0, ops):
                ev = counts(g0, ops)
                n = g0 + 1
                np_ = 1 - par0
                j = -1
                for op in ops:
                    g, par = (g0, par0) if op[3] == 0 else (g0 - 1, 1 - par0)
                    if op[2]:
                        j += 1
                    if op[0] == "STATS":
                        if isinstance(g, int) and g == 0:
                            sp.wait_ge(zeroed_1, 1)
                        if mask == "full":
                            ge(sp, mask_done, n)
                            sp.dma_start(mask_in[:, :, :], cfg["mask_dram"][bass.ds(n * TG, TG), :, :]
                                         .rearrange("b q k -> q b k")).then_inc(mask_dma, 16)
                        if from_ctx and project:
                            if ev.before:
                                sp.wait_ge(job_done, ev.filled(ev.place_before("v")))
                            for c in range(C):
                                sp.dma_start(ctxT[:, c, :], sh.ctxT_dram[c * P:(c + 1) * P, bass.ds(n * GT, GT)])\
                                  .then_inc(ctx_in, 16)
                        if not project:
                            ge(sp, s_done, (n - 1) * 16)
                            for c in range(C):
                                for r in range(HC):
                                    sp.dma_start(kblk[np_][DH * r:DH * r + DH, c, r, :],
                                                 sh.ctxT_dram[c * P + DH * r:c * P + DH * r + DH, bass.ds(n * GT, GT)])\
                                      .then_inc(kblk_done[np_][c], 16)
                            ge(sp, vaug_done, n)
                            sp.dma_start(vraw[:, :, :], sh.ctx_dram[bass.ds(n * TG, TG), :, :]
                                         .rearrange("b t d -> t b d")).then_inc(v_in, 16)
                    if op[0] == "k":
                        who, cnt = ev.emptied(j)
                        sp.wait_ge(out_of[who], cnt)
                        c = op[1]
                        for r in range(HC):
                            sp.dma_start(kblk[np_][DH * r:DH * r + DH, c, r, :], kT[DH * r:DH * r + DH, c, :])\
                              .then_inc(kblk_done[np_][c], 16)

            run(sp, emit)

        @block.gpsimd
        def _(pool):
            for va in vaug:
                last_set = nc.gpsimd.memset(va[:, :, :, DH:DH + 1], 1.0)
            last_set.then_inc(zeroed, 1)

            def emit(g, par, ops):
                n = g + 1
                for op in ops:
                    if op[0] == "STATS":
                        pool.wait_ge(stats_done, n + 1)
                        settle(pool, sh)
                        nc.gpsimd.tensor_scalar(veps[:, :], moments[:, :, 1], cfg["eps"], None, ALU.add)\
                          .then_inc(veps_done, 1)
                        pool.wait_ge(veps_done, n + 1)
                        nc.gpsimd.tensor_tensor(rstd[:, :], veps[:, :], sh.power[:, :], ALU.pow).then_inc(rstd_done, 1)
                        if not project:
                            pool.wait_ge(v_in, 16 * (n + 1))
                            ge(pool, av_done, (n - 1) * 16)
                            settle(pool, sh)
                            for b in range(TG):
                                cp = nc.gpsimd.tensor_copy(vaug[1 - par][:, b, :, 0:DH],
                                                           vraw[:, b, :].rearrange("p (h d) -> p h d", h=H))
                            cp.then_inc(vaug_done, 1)

                        if isinstance(g, int) and g < 0:
                            nc.gpsimd.memset(kblk[1][:, :, :, :], 0.0).then_inc(zeroed_1, 1)

            run(pool, emit)

        @block.vector
        def _(dve):
            nc.vector.memset(kblk[0][:, :, :, :], 0.0).then_inc(zeroed, 1)
            if cfg.get("src_in"):
                dve.wait_ge(cfg["src_in"], 16)
            if mask == "shared":
                dve.wait_ge(mask_dma, 16)
                for q in range(2):
                    last_m = nc.vector.tensor_scalar(mask_add[:, q, :, :], bcast(mask_in[:, :], 1, TG), 0.0, MASKED,
                                                     ALU.is_equal, ALU.mult)
                last_m.then_inc(best_done, 1)
                dve.wait_ge(best_done, 1)
                nc.vector.tensor_reduce(mask_best[:, :, :], mask_add[:, :, :, :], AX.X, ALU.max).then_inc(best_done, 1)
                dve.wait_ge(best_done, 2)
                nc.vector.tensor_scalar(expscale[:, :, :], mask_best[:, :, :], 0.0, cfg["scale"], ALU.is_equal,
                                        ALU.mult).then_inc(mask_done, 1)

            def emit(g0, par0, ops):
                ev = counts(g0, ops)
                n = g0 + 1
                np_ = 1 - par0
                j = -1
                for op in ops:
                    g, par = (g0, par0) if op[3] == 0 else (g0 - 1, 1 - par0)
                    if op[2]:
                        j += 1
                    if op[0] == "STATS":
                        if not (isinstance(g, int) and g < 0):
                            dve.wait_ge(ln_done, n)
                        for b in range(TG):
                            bn = nc.vector.bn_stats(stats[:, b, :], cfg["src"][:, bass.ds(n * TG + b, 1), :]
                                                    .rearrange("p o d -> p (o d)"))
                        bn.then_inc(bn_done, 1)
                        dve.wait_ge(bn_done, n + 1)
                        settle(dve, sh)
                        for b in range(TG):
                            bn = nc.vector.bn_aggr(moments[:, b, :], stats[:, b, :])
                        bn.then_inc(stats_done, 1)
                        if mask == "full":
                            dve.wait_ge(mask_dma, 16 * (n + 1))
                            nc.vector.tensor_scalar(mask_add[:, np_, :, :], mask_in[:, :, :], 0, MASKED,
                                                    ALU.is_equal, ALU.mult).then_inc(best_done, 1)
                            dve.wait_ge(best_done, 2 * n + 1)
                            nc.vector.tensor_reduce(mask_best[:, np_, :], mask_add[:, np_, :, :], AX.X, ALU.max)\
                              .then_inc(best_done, 1)
                            dve.wait_ge(best_done, 2 * n + 2)
                            nc.vector.tensor_scalar(expscale[:, np_, :], mask_best[:, np_, :], 0.0, cfg["scale"],
                                                    ALU.is_equal, ALU.mult).then_inc(mask_done, 1)
                    if op[:2] == ("lnT", 1) and isinstance(g, int) and g < 0:
                        dve.wait_ge(w_in, n_weights)
                    if op[0] == "LN":
                        dve.wait_ge(rstd_done, n + 1)
                        for b in range(TG):
                            lnop = nc.vector.tensor_scalar(ln[:, np_, b, :], cfg["src"][:, bass.ds(n * TG + b, 1), :]
                                                           .rearrange("p o d -> p (o d)"), moments[:, b, 0:1],
                                                           rstd[:, b:b + 1], ALU.subtract, ALU.mult)
                        lnop.then_inc(ln_done, 1)
                    if op[0] == "q":
                        dve.wait_ge(job_done, ev.filled(j))
                        if bq is not None:
                            nc.vector.tensor_scalar(qT[:, np_, op[1], :], jbank[j % 2][:, :], bq[:, op[1]:op[1] + 1], None,
                                                    ALU.add).then_inc(out_of["V"], 1)
                        else:
                            nc.vector.tensor_copy(qT[:, np_, op[1], :], jbank[j % 2][:, :]).then_inc(out_of["V"], 1)
                    if op[0] == "v":
                        dve.wait_ge(job_done, ev.filled(j))
                        b0 = 2 * op[1]
                        dst = vaug[np_][:, b0:b0 + 2, :, 0:DH]
                        src = jbank[j % 2][:, :].rearrange("p (b h d) -> p b h d", b=2, h=H)
                        if bv is not None:
                            nc.vector.tensor_tensor(dst, src, bcast(bv[:, :].rearrange("p (h d) -> p h d", h=H), 1, 2),
                                                    ALU.add).then_inc(out_of["V"], 1)
                        else:
                            nc.vector.tensor_copy(dst, src).then_inc(out_of["V"], 1)
                    if op[0] == "S":
                        u = op[1]
                        U = g * 16 + u
                        s4 = sbank[u % 2][:, :].rearrange("p (h k) -> p h k", h=QH)
                        dve.wait_ge(s_done, U + 1)
                        nc.vector.tensor_reduce(rowmax[:, u % 4, :], s4, AX.X, ALU.max).then_inc(max_done, 1)
                        dve.wait_ge(max_done, U + 1)
                        ge(dve, exp_done, U - 3)
                        nc.vector.tensor_tensor(shifted[:, u % 4, :, :], s4, bcast(rowmax[:, u % 4, :], 2, P),
                                                ALU.subtract).then_inc(sub_done, 1)
                    if op[0] == "NORM":
                        b = op[1]
                        av = vbank[b % 2][:, 0:H * (DH + 1)].rearrange("p (h d) -> p h d", h=H)
                        dve.wait_ge(av_done, g * 16 + 4 * b + 4)
                        nc.vector.reciprocal(recip[:, b % 2, :], av[:, :, DH]).then_inc(recip_done, 1)
                        dve.wait_ge(recip_done, g * TG + b + 1)
                        nc.vector.tensor_tensor(o[:, b % 2, :].rearrange("p (h d) -> p h d", h=H), av[:, :, 0:DH],
                                                bcast(recip[:, b % 2, :], 2, DH), ALU.mult).then_inc(o_done, 1)
                    if op[0] == "out":
                        b = op[1]
                        dve.wait_ge(job_done, ev.filled(j))
                        dst = cfg["dst"][:, bass.ds(g * TG + b, 1), :].rearrange("p o d -> p (o d)")
                        base = ln[:, par, b, :] if cfg["base"] == "ln" else dst
                        if bo is not None:
                            nc.vector.tensor_tensor(res[:, b % 2, :], jbank[j % 2][:, 0:D], bo[:, :], ALU.add)\
                              .then_inc(res_done, 1)
                            dve.wait_ge(res_done, g * TG + b + 1)
                            nc.vector.tensor_tensor(dst, res[:, b % 2, :], base, ALU.add).then_inc(out_of["V"], 1)
                        else:
                            nc.vector.tensor_tensor(dst, jbank[j % 2][:, 0:D], base, ALU.add).then_inc(out_of["V"], 1)

            run(dve, emit)

        @block.scalar
        def _(act):

            def emit(g0, par0, ops):
                ev = counts(g0, ops)
                n = g0 + 1
                np_ = 1 - par0
                j = -1
                for op in ops:
                    g, par = (g0, par0) if op[3] == 0 else (g0 - 1, 1 - par0)
                    if op[2]:
                        j += 1
                    if op[0] == "lnT":
                        act.wait_ge(job_done, ev.filled(j))
                        dst = lnT[:, op[1], :] if project else qT[:, np_, op[1], :]
                        nc.scalar.activation(dst, jbank[j % 2][:, :], ACT.Identity).then_inc(out_of["A"], 1)
                        if op[1] == 1 and isinstance(g, int) and g < 0:
                            act.wait_ge(w_in, n_weights)
                    if op[0] == "k":
                        act.wait_ge(job_done, ev.filled(j))
                        if not (isinstance(n, int) and n == 0):
                            act.wait_ge(kblk_done[par][op[1]], kblk_count(g, par))
                        bias = bk[:, op[1]:op[1] + 1] if bk is not None else 0.0
                        nc.scalar.activation(kT[:, op[1], :], jbank[j % 2][:, :], ACT.Identity, bias=bias)\
                          .then_inc(out_of["A"], 1)
                    if op[0] == "S":
                        u = op[1]
                        U = g * 16 + u
                        act.wait_ge(sub_done, U + 1)
                        ge(act, t_done, U - 3)
                        if mask is not None:
                            if u == 0:
                                act.wait_ge(mask_done, g + 1 if mask == "full" else 1)
                            scale = expscale[:, par, u // 4:u // 4 + 1]
                        else:
                            scale = cfg["scale"]
                        nc.scalar.activation(e[:, u % 4, :, :], shifted[:, u % 4, :, :], ACT.Exp, scale=scale)\
                          .then_inc(exp_done, 1)
                    if op[0] == "T":
                        u = op[1]
                        U = g * 16 + u
                        act.wait_ge(t_done, U + 1)
                        ge(act, av_done, U - 3)
                        nc.scalar.activation(eT[:, u % 4, :, :].rearrange("p h k -> p (h k)"), tbank[u % 2][:, :],
                                             ACT.Identity).then_inc(eT_done, 1)
                    if op[0] == "oT":
                        act.wait_ge(job_done, ev.filled(j))
                        nc.scalar.activation(oT[:, op[1] % 2, :, :].rearrange("p c t -> p (c t)"), jbank[j % 2][:, 0:D],
                                             ACT.Identity).then_inc(out_of["A"], 1)

            run(act, emit)

        @block.tensor
        def _(pe):

            def emit(g0, par0, ops):
                ev = counts(g0, ops)
                n = g0 + 1
                np_ = 1 - par0
                j = -1
                for op in ops:
                    g, par = (g0, par0) if op[3] == 0 else (g0 - 1, 1 - par0)
                    if op[2]:
                        j += 1
                        bank = jbank[j % 2]
                        bank_free(pe, ev, j)
                    if op[0] == "lnT":
                        pe.wait_ge(ln_done, n + 1)
                        for b in range(TG):
                            last_mm = nc.tensor.transpose(bank[:, b * P:(b + 1) * P], ln[:, np_, b, op[1] * P:(op[1] + 1) * P],
                                                          sh.ident[:, :])
                        last_mm.then_inc(job_done, 1)
                        if op[1] == 1 and isinstance(g, int) and g < 0:
                            pe.wait_ge(w_in, n_weights)
                            pe.wait_ge(zeroed, 2)
                    if op[0] in ("q", "k"):
                        w, x = (wq, lnT) if op[0] == "q" else (wk, ctxT if from_ctx else lnT)
                        if op[0] == "q" and op[1] == 0:
                            who, cnt = ev.emptied(j - 1)
                            pe.wait_ge(out_of[who], cnt)
                        if op[0] == "k" and op[1] == 0 and from_ctx:
                            pe.wait_ge(ctx_in, 16 * C * (n + 1))
                        for c in range(C):
                            last_mm = nc.tensor.matmul(bank[:, :], w[:, c, op[1] * P:(op[1] + 1) * P], x[:, c, :],
                                                       start=(c == 0), stop=(c == C - 1))
                        last_mm.then_inc(job_done, 1)
                    if op[0] == "v":
                        x = ctxT if from_ctx else lnT
                        for i in range(2):
                            b = 2 * op[1] + i
                            for c in range(C):
                                last_mm = nc.tensor.matmul(bank[:, i * D:(i + 1) * D], x[:, c, b * P:(b + 1) * P], wv[:, c, :],
                                                           start=(c == 0), stop=(c == C - 1))
                        last_mm.then_inc(job_done, 1)
                    if op[0] == "S":
                        u = op[1]
                        U = g * 16 + u
                        b, c, h0 = u // 4, (u % 4) // 2, QH * (u % 2)
                        if u == 0:
                            who, cnt = ev.emptied(ev.place_before("q" if project else "lnT"))
                            pe.wait_ge(out_of[who], cnt)
                            pe.wait_ge(kblk_done[par][0], kblk_count(g, par))
                            if mask is not None:
                                pe.wait_ge(mask_done, g + 1 if mask == "full" else 1)
                        if u == 2 and isinstance(g, int) and g == 0:
                            pe.wait_ge(zeroed_1, 1)
                        if u == 2:
                            pe.wait_ge(kblk_done[par][1], kblk_count(g, par))
                        ge(pe, sub_done, U - 1)
                        bank = sbank[u % 2]
                        if mask is not None:
                            nc.tensor.matmul(bank[:, :].rearrange("p (h k) -> p h k", h=QH), sh.ident_bf[:, :],
                                             bcast(mask_add[:, par, b, :], 1, QH), start=True, stop=False)
                        nc.tensor.matmul(bank[:, :].rearrange("p (h k) -> p h k", h=QH), qT[:, par, c, b * P:(b + 1) * P],
                                         kblk[par][:, c, h0:h0 + QH, b * P:(b + 1) * P],
                                         start=(mask is None), stop=True).then_inc(s_done, 1)
                    if op[0] == "T":
                        u = op[1]
                        U = g * 16 + u
                        pe.wait_ge(exp_done, U + 1)
                        ge(pe, eT_done, U - 1)
                        for h in range(QH):
                            last_mm = nc.tensor.transpose(tbank[u % 2][:, h * P:(h + 1) * P], e[:, u % 4, h, :], sh.ident[:, :])
                        last_mm.then_inc(t_done, 1)
                    if op[0] == "AV":
                        u = op[1]
                        U = g * 16 + u
                        b = u // 4
                        if u == 0:
                            if project:
                                who, cnt = ev.emptied(ev.place_before("v"))
                                pe.wait_ge(out_of[who], cnt)
                            else:
                                pe.wait_ge(vaug_done, g + 1)
                        pe.wait_ge(eT_done, U + 1)
                        if u % 4 == 0:
                            ge(pe, o_done, g * TG + b - 1)
                        for h in range(QH):
                            hh = QH * (u % 4) + h
                            last_mm = nc.tensor.matmul(vbank[b % 2][:, hh * (DH + 1):(hh + 1) * (DH + 1)], eT[:, u % 4, h, :],
                                                       vaug[par][:, b, hh, :], start=True, stop=True)
                        last_mm.then_inc(av_done, 1)
                    if op[0] == "oT":
                        b = op[1]
                        pe.wait_ge(o_done, g * TG + b + 1)
                        for c in range(C):
                            last_mm = nc.tensor.transpose(bank[:, c * P:(c + 1) * P], o[:, b % 2, c * P:(c + 1) * P], sh.ident[:, :])
                        last_mm.then_inc(job_done, 1)
                    if op[0] == "out":
                        b = op[1]
                        who, cnt = ev.emptied(ev.place(("oT", b)))
                        pe.wait_ge(out_of[who], cnt)
                        for c in range(C):
                            last_mm = nc.tensor.matmul(bank[:, 0:D], oT[:, b % 2, c, :], wo[:, c, :],
                                                       start=(c == 0), stop=(c == C - 1))
                        last_mm.then_inc(job_done, 1)

            run(pe, emit)


class Chain:

    def __init__(self, eng, sem, start, per):
        self.eng, self.sem, self.start, self.per = eng, sem, start, per

    def group(self, g):
        self.base, self.k = (0 if isinstance(g, int) and g < 0 else self.start + g * self.per), 0

    def link(self, ins):
        self.k += 1
        ins.then_inc(self.sem, 1)
        self.eng.wait_ge(self.sem, self.base + self.k)


def run_groups(eng, emit, G, prologue, middle, last, peeled=0):
    emit(-1, 1, prologue)
    emit(0, 0, middle)
    for t in range(peeled):
        emit(t * 2 + 1, 1, middle)
        emit(t * 2 + 2, 0, middle)
    with eng.Fori(peeled, (G - 2) // 2) as t:
        emit(t * 2 + 1, 1, middle)
        emit(t * 2 + 2, 0, middle)
    emit(G - 1, 1, last)


def tile_of(stream, t):
    return stream[:, bass.ds(t, 1), :].rearrange("p o d -> p (o d)")


def ffn(nc, sh, name, G, cfg):
    with ExitStack() as ctx:
        m = Memory(nc, ctx, name)
        affine, post = cfg["affine"], cfg["post"]
        F = cfg["F"]
        NF = F // P
        resident = cfg.get("resident")
        w1 = resident[0] if resident else m.sb("w1", [P, C, F])
        w2 = resident[1] if resident else m.sb("w2", [P, NF, D])
        b1 = m.sb("b1", [P, NF])
        b2 = m.sb("b2", [P, D])
        vec = {}
        for k, src in (("g", affine and affine[0]), ("b", affine and affine[1]),
                       ("pg", post and post[0]), ("pb", post and post[1])):
            if src is not None:
                vec[k] = (m.sb(k, [P, D]), src)
        stats = m.sb("stats", [P, TG, 6])
        moments = m.sb("moments", [P, TG, 2])
        veps, rstd = m.sb("veps", [P, TG]), m.sb("rstd", [P, TG])
        pmoments = m.sb("pmoments", [P, TG, 2])
        pveps, prstd = m.sb("pveps", [P, TG]), m.sb("prstd", [P, TG])
        ln = m.sb("ln", [P, 2, TG, D])
        lnT = m.sb("lnT", [P, 2, C, GT])
        hT = m.sb("hT", [P, 4, GT])
        y = m.sb("y", [P, TG, D])

        hbank = [m.bank(f"h{i}") for i in range(2)]
        ybank = [m.bank(f"y{i}") for i in range(TG)]
        tbank = [m.bank(f"t{i}") for i in range(C)]

        w_in = m.sem("w_in")
        stats_done, veps_done, rstd_done, ln_done = m.sem("stats"), m.sem("veps"), m.sem("rstd"), m.sem("ln")
        pstats_done, pveps_done, prstd_done = m.sem("pstats"), m.sem("pveps"), m.sem("prstd")
        chain_sem = m.sem("chain")
        t_done, lnT_done = m.sem("t"), m.sem("lnT")
        h_done, act_done, y_done, out_done = m.sem("h"), m.sem("act"), m.sem("y"), m.sem("out")

        def schedule(with_next):
            ops = []
            for s in range(NF + 2):
                if s < NF:
                    ops.append(("H", s))
                if s >= 2:
                    ops.append(("Y", s - 2))
                if with_next:
                    ops += {1: [("STATS",)], 4: [("LN",)], 6: [("lnT", 0), ("lnT", 1)]}.get(s, [])
            return ops + [("OUT",)]

        prologue = [("STATS",), ("LN",), ("lnT", 0), ("lnT", 1)]
        middle, last = schedule(True), schedule(False)
        loads = (0 if resident else 2) + 2 + len(vec)
        block = ctx.enter_context(nc.Block())

        @block.sync
        def _(sp):
            if not resident:
                sp.dma_start(w1[:, :, :], cfg["w1"].rearrange("(c p) n -> p c n", p=P)).then_inc(w_in, 16)
                sp.dma_start(w2[:, :, :], cfg["w2"].rearrange("(c p) n -> p c n", p=P)).then_inc(w_in, 16)
            sp.dma_start(b1[:, :], column(cfg["b1"]), allow_slow_non_contiguous=True).then_inc(w_in, 16)
            sp.dma_start(b2[:, :], rows(cfg["b2"])).then_inc(w_in, 16)
            for dst, src in vec.values():
                sp.dma_start(dst[:, :], rows(src)).then_inc(w_in, 16)

        @block.gpsimd
        def _(pool):
            def emit(g, par, ops):
                n = g + 1
                for op in ops:
                    if op[0] == "STATS":
                        pool.wait_ge(stats_done, n + 1)
                        settle(pool, sh)
                        nc.gpsimd.tensor_scalar(veps[:, :], moments[:, :, 1], cfg["eps"], None, ALU.add)\
                          .then_inc(veps_done, 1)
                        pool.wait_ge(veps_done, n + 1)
                        nc.gpsimd.tensor_tensor(rstd[:, :], veps[:, :], sh.power[:, :], ALU.pow).then_inc(rstd_done, 1)
                    if op[0] == "OUT" and post:
                        pool.wait_ge(pstats_done, g + 1)
                        settle(pool, sh)
                        nc.gpsimd.tensor_scalar(pveps[:, :], pmoments[:, :, 1], post[2], None, ALU.add)\
                          .then_inc(pveps_done, 1)
                        pool.wait_ge(pveps_done, g + 1)
                        nc.gpsimd.tensor_tensor(prstd[:, :], pveps[:, :], sh.power[:, :], ALU.pow).then_inc(prstd_done, 1)

            run_groups(pool, emit, G, prologue, middle, last)

        @block.vector
        def _(dve):
            ln_links = 1 + (2 if affine else 0)
            out_links = 1 + (1 + 1 + 3 if post else 0)
            chain = Chain(dve, chain_sem, ln_links, ln_links + out_links)

            def emit(g, par, ops):
                n = g + 1
                np_ = 1 - par
                chain.group(g)
                for op in ops:
                    if op[0] == "STATS":
                        for b in range(TG):
                            bn = nc.vector.bn_stats(stats[:, b, :], tile_of(cfg["src"], n * TG + b))
                        chain.link(bn)
                        settle(dve, sh)
                        for b in range(TG):
                            bn = nc.vector.bn_aggr(moments[:, b, :], stats[:, b, :])
                        bn.then_inc(stats_done, 1)
                        if isinstance(g, int) and g < 0:
                            dve.wait_ge(w_in, 16 * loads)
                    if op[0] == "LN":
                        dve.wait_ge(rstd_done, n + 1)
                        for b in range(TG):
                            lnop = nc.vector.tensor_scalar(ln[:, np_, b, :], tile_of(cfg["src"], n * TG + b),
                                                           moments[:, b, 0:1], rstd[:, b:b + 1], ALU.subtract, ALU.mult)
                        if affine:
                            chain.link(lnop)
                            x4 = ln[:, np_, :, :]
                            chain.link(nc.vector.tensor_tensor(x4, x4, bcast(vec["g"][0][:, :], 1, TG), ALU.mult))
                            lnop = nc.vector.tensor_tensor(x4, x4, bcast(vec["b"][0][:, :], 1, TG), ALU.add)
                        lnop.then_inc(ln_done, 1)
                    if op[0] == "OUT":
                        dve.wait_ge(y_done, (g + 1) * NF)
                        for b in range(TG):
                            add = nc.vector.tensor_tensor(y[:, b, :], ybank[b][:, 0:D], b2[:, :], ALU.add)
                        add.then_inc(out_done, 1)
                        dve.wait_ge(out_done, g + 1)
                        base = ln[:, par, :, :] if affine else cfg["dst"][:, bass.ds(g * TG, TG), :]
                        if not post:
                            dst = cfg["dst"][:, bass.ds(g * TG, TG), :]
                            chain.link(nc.vector.tensor_tensor(dst, y[:, :, :], base, ALU.add))
                        else:
                            chain.link(nc.vector.tensor_tensor(y[:, :, :], y[:, :, :], base, ALU.add))
                            for b in range(TG):
                                bn = nc.vector.bn_stats(stats[:, b, :], y[:, b, :])
                            chain.link(bn)
                            settle(dve, sh)
                            for b in range(TG):
                                bn = nc.vector.bn_aggr(pmoments[:, b, :], stats[:, b, :])
                            bn.then_inc(pstats_done, 1)
                            dve.wait_ge(prstd_done, g + 1)
                            for b in range(TG):
                                lnop = nc.vector.tensor_scalar(y[:, b, :], y[:, b, :], pmoments[:, b, 0:1],
                                                               prstd[:, b:b + 1], ALU.subtract, ALU.mult)
                            chain.link(lnop)
                            chain.link(nc.vector.tensor_tensor(y[:, :, :], y[:, :, :], bcast(vec["pg"][0][:, :], 1, TG), ALU.mult))
                            chain.link(nc.vector.tensor_tensor(y[:, :, :], y[:, :, :], bcast(vec["pb"][0][:, :], 1, TG), ALU.add))
                            dst = cfg["dst"][:, bass.ds(g * TG, TG), :]
                            chain.link(nc.vector.tensor_tensor(dst, dst, y[:, :, :], ALU.add))

            run_groups(dve, emit, G, prologue, middle, last)

        @block.scalar
        def _(act):

            def emit(g, par, ops):
                n = g + 1
                for op in ops:
                    if op[0] == "lnT":
                        act.wait_ge(t_done, n * C + op[1] + 1)
                        nc.scalar.activation(lnT[:, 1 - par, op[1], :], tbank[op[1]][:, :], ACT.Identity).then_inc(lnT_done, 1)
                        if op[1] == 1 and isinstance(g, int) and g < 0:
                            act.wait_ge(w_in, 16 * loads)
                    if op[0] == "H":
                        U = g * NF + op[1]
                        act.wait_ge(h_done, U + 1)
                        ge(act, y_done, U - 3)
                        nc.scalar.activation(hT[:, op[1] % 4, :], hbank[op[1] % 2][:, :], cfg["act"],
                                             bias=b1[:, op[1]:op[1] + 1]).then_inc(act_done, 1)

            run_groups(act, emit, G, prologue, middle, last)

        @block.tensor
        def _(pe):

            def emit(g, par, ops):
                n = g + 1
                for op in ops:
                    if op[0] == "lnT":
                        c = op[1]
                        pe.wait_ge(ln_done, n + 1)
                        ge(pe, lnT_done, n * C - C + c + 1 if not isinstance(n, int) or n > 0 else 0)
                        for b in range(TG):
                            tr = nc.tensor.transpose(tbank[c][:, b * P:(b + 1) * P], ln[:, 1 - par, b, c * P:(c + 1) * P],
                                                     sh.ident[:, :])
                        tr.then_inc(t_done, 1)
                        if c == 1 and isinstance(g, int) and g < 0:
                            pe.wait_ge(w_in, 16 * loads)
                    if op[0] == "H":
                        f = op[1]
                        U = g * NF + f
                        if f == 0:
                            pe.wait_ge(lnT_done, C * (g + 1))
                        ge(pe, act_done, U - 1)
                        for c in range(C):
                            mm = nc.tensor.matmul(hbank[f % 2][:, :], w1[:, c, f * P:(f + 1) * P], lnT[:, par, c, :],
                                                  start=(c == 0), stop=(c == C - 1))
                        mm.then_inc(h_done, 1)
                    if op[0] == "Y":
                        f = op[1]
                        pe.wait_ge(act_done, g * NF + f + 1)
                        if f == 0:
                            ge(pe, out_done, g)
                        for b in range(TG):
                            mm = nc.tensor.matmul(ybank[b][:, 0:D], hT[:, f % 4, b * P:(b + 1) * P], w2[:, f, :],
                                                  start=(f == 0), stop=(f == NF - 1))
                        mm.then_inc(y_done, 1)

            run_groups(pe, emit, G, prologue, middle, last)


def attention_narrow(nc, sh, name, G, cfg):
    with ExitStack() as ctx:
        m = Memory(nc, ctx, name)
        strided = cfg["kind"] == "strided"
        affine = cfg["affine"]
        KW = P + H if strided else P
        SLOTS = KW // H
        wq, wk, wv, wo = (m.sb(w, [P, C, D]) for w in ("wq", "wk", "wv", "wo"))
        bq, bk = m.sb("bq", [P, C]), m.sb("bk", [P, C])
        bv, bo = m.sb("bv", [P, D]), m.sb("bo", [P, D])
        if affine:
            ga, be = m.sb("ga", [P, D]), m.sb("be", [P, D])
        stats, moments = m.sb("stats", [P, TG, 6]), m.sb("moments", [P, TG, 2])
        veps, rstd = m.sb("veps", [P, TG]), m.sb("rstd", [P, TG])
        ln = m.sb("ln", [P, 2, TG, D])
        lnT = m.sb("lnT", [P, C, GT])
        ctxT = m.sb("ctxT", [P, 2, C, GT])
        qT = m.sb("qT", [P, 2, C, GT])
        k = m.sb("k", [P, 2, C, TG, KW])
        vt = m.sb("vt", [P, TG, D])
        v = m.sb("v", [P, 2, TG, D])
        if strided:
            head_of = m.sb("head_of", [P, C, H])
            key_of = m.sb("key_of", [P, H])
            xt = m.sb("xt", [H, TG, D])
            vx = m.sb("vx", [H, 2, TG, D])
            mask_in = m.sb("mask_in", [P, TG, P], I32)
            keep = m.sb("keep", [P, 2, TG, KW])
            fill = m.sb("fill", [P, 2, TG, KW])
            pxT = m.sb("pxT", [H, TG, P])
        sc = m.sb("sc", [P, TG, KW])
        p = m.sb("p", [P, TG, KW])
        NMAX = H if strided else 1
        best, total, recip = (m.sb(x, [P, TG, NMAX]) for x in ("best", "total", "recip"))
        pT = m.sb("pT", [P, TG, P])
        o = m.sb("o", [P, TG, D])
        oT = m.sb("oT", [P, 2, 2, C, P])
        res = m.sb("res", [P, TG, D])

        jbank = [m.bank(f"j{i}") for i in range(2)]
        sbank = [m.bank(f"s{i}") for i in range(2)]
        vbank = [m.bank(f"v{i}") for i in range(2)]
        tbank = m.bank("t")
        xbank = m.bank("x")

        w_in, ctx_in, mask_in_done = m.sem("w_in"), m.sem("ctx_in"), m.sem("mask_in")
        heads_made, heads_step = m.sem("heads_made"), m.sem("heads_step")
        stats_done, veps_done, rstd_done, ln_done = m.sem("stats"), m.sem("veps"), m.sem("rstd"), m.sem("ln")
        mask_done = m.sem("mask")
        job_done = m.sem("job")
        out_of = {"A": m.sem("act_job"), "V": m.sem("dve_job")}
        s_done, sc_done, exp_done, total_done = m.sem("s"), m.sem("sc"), m.sem("exp"), m.sem("total")
        pt_done, pT_done, av_done, o_done = m.sem("pt"), m.sem("pT"), m.sem("av"), m.sem("o")
        ot_done, oT_done, out_done, res_done = m.sem("ot"), m.sem("oT"), m.sem("out"), m.sem("res")
        chain_sem = m.sem("chain")

        proj = [("k", 0, "V"), ("k", 1, "V"), ("lnT", 0, "A"), ("lnT", 1, "A"), ("q", 0, "A"), ("q", 1, "A"),
                ("v", 0, "V"), ("v", 1, "V")]
        if strided:
            proj += [("x", 0, "V"), ("x", 1, "V")]
        J = dict(((x[0], x[1]), x) for x in proj)
        prologue = [("STATS",), ("LN",)] + proj
        last = [("S",), ("SOFT",), ("TOTAL",), ("PT",), ("AV",), ("NORM",), ("OT",), ("OUT",)]
        middle = [("S",), ("STATS",), J["k", 0], ("LN",), J["k", 1], J["lnT", 0], J["lnT", 1], J["q", 0], J["q", 1], ("SOFT",),
                  ("TOTAL",), J["v", 0], ("PT",), J["v", 1], ("AV",), ("NORM",)]
        middle += [J["x", 0], ("OT",), J["x", 1]] if strided else [("OT",)]
        middle += [("OUT",)]
        jobs_of = lambda ops: [x for x in ops if len(x) == 3]
        per = {w: sum(x[2] == w for x in proj) for w in "AV"}

        def counts(g, ops):
            n = g + 1
            before = [] if isinstance(g, int) and g < 0 else proj
            return Evacuations(jobs_of(ops), before, n * len(proj), {w: n * per[w] for w in "AV"})

        front_links = 1 + (2 if affine else 0)
        next_links = front_links + (4 if strided else 0)
        own_links = 5 if strided else 2
        loads = 8 + (2 if affine else 0)
        block = ctx.enter_context(nc.Block())

        @block.sync
        def _(sp):
            for dst, src in ((wq, "wq"), (wk, "wk"), (wv, "wv"), (wo, "wo")):
                sp.dma_start(dst[:, :, :], cfg[src].rearrange("(c p) n -> p c n", p=P)).then_inc(w_in, 16)
            for dst, src in ((bq, "bq"), (bk, "bk")):
                sp.dma_start(dst[:, :], column(cfg[src]), allow_slow_non_contiguous=True).then_inc(w_in, 16)
            for dst, src in ((bv, cfg["bv"]), (bo, cfg["bo"])) + (((ga, affine[0]), (be, affine[1])) if affine else ()):
                sp.dma_start(dst[:, :], rows(src)).then_inc(w_in, 16)

            def emit(g, par, ops):
                n = g + 1
                for op in ops:
                    if op[0] == "STATS":
                        if not (isinstance(n, int) and n < 2):
                            sp.wait_ge(job_done, (n - 1) * len(proj))
                        if not (isinstance(n, int) and n < 1):
                            sp.wait_ge(ctx_in, 16 * C * n)
                        for c in range(C):
                            sp.dma_start(ctxT[:, 1 - par, c, :], sh.ctxT_dram[c * P:(c + 1) * P, bass.ds(n * GT, GT)])\
                              .then_inc(ctx_in, 16)
                        if strided:
                            ge(sp, mask_done, n)
                            sp.dma_start(mask_in[:, :, :], cfg["mask_dram"][bass.ds(n * TG, TG), :]
                                         .partition_broadcast(P)).then_inc(mask_in_done, 16)

            run_groups(sp, emit, G, prologue, middle, last)

        @block.gpsimd
        def _(pool):
            if strided:
                nc.gpsimd.memset(head_of[:, :, :], 1.0).then_inc(heads_step, 1)
                pool.wait_ge(heads_step, 1)
                nc.gpsimd.affine_select(out=head_of[:, :, :], in_=head_of[:, :, :], compare_op=ALU.is_ge, fill=0.0,
                                        base=0, pattern=[[P, C], [-DH, H]], channel_multiplier=1).then_inc(heads_step, 1)
                pool.wait_ge(heads_step, 2)
                nc.gpsimd.affine_select(out=head_of[:, :, :], in_=head_of[:, :, :], compare_op=ALU.is_ge, fill=0.0,
                                        base=DH - 1, pattern=[[-P, C], [DH, H]], channel_multiplier=-1)\
                  .then_inc(heads_step, 1)
                nc.gpsimd.memset(key_of[:, :], 0.0).then_inc(heads_step, 1)
                for i in range(P // H):
                    pool.wait_ge(heads_step, 4 + i)
                    nc.gpsimd.affine_select(out=key_of[:, :], in_=key_of[:, :], compare_op=ALU.not_equal, fill=1.0,
                                            base=-H * i, pattern=[[-1, H]], channel_multiplier=1).then_inc(heads_step, 1)

            def emit(g, par, ops):
                n = g + 1
                for op in ops:
                    if op[0] == "STATS":
                        pool.wait_ge(stats_done, n + 1)
                        settle(pool, sh)
                        nc.gpsimd.tensor_scalar(veps[:, :], moments[:, :, 1], cfg["eps"], None, ALU.add)\
                          .then_inc(veps_done, 1)
                        pool.wait_ge(veps_done, n + 1)
                        nc.gpsimd.tensor_tensor(rstd[:, :], veps[:, :], sh.power[:, :], ALU.pow).then_inc(rstd_done, 1)

            run_groups(pool, emit, G, prologue, middle, last)

        @block.vector
        def _(dve):
            if cfg.get("src_in"):
                dve.wait_ge(cfg["src_in"], 16)
            if strided:
                dve.wait_ge(heads_step, 4 + P // H)
            chain = Chain(dve, chain_sem, next_links, next_links + own_links)

            def emit(g, par, ops):
                n = g + 1
                np_ = 1 - par
                ev = counts(g, ops)
                j = -1
                chain.group(g)
                for op in ops:
                    if len(op) == 3:
                        j += 1
                        if op[2] == "V":
                            dve.wait_ge(job_done, ev.filled(j))
                    if op[0] == "STATS":
                        for b in range(TG):
                            bn = nc.vector.bn_stats(stats[:, b, :], tile_of(cfg["src"], n * TG + b))
                        chain.link(bn)
                        settle(dve, sh)
                        for b in range(TG):
                            bn = nc.vector.bn_aggr(moments[:, b, :], stats[:, b, :])
                        bn.then_inc(stats_done, 1)
                        if isinstance(g, int) and g < 0:
                            dve.wait_ge(w_in, 16 * loads)
                        if strided:
                            dve.wait_ge(mask_in_done, 16 * (n + 1))
                            last_key = bcast(mask_in[:, :, P - 1], 2, H)
                            nc.vector.tensor_scalar(keep[:, np_, :, 0:P], mask_in[:, :, :], 0, cfg["scale"],
                                                    ALU.not_equal, ALU.mult)
                            nc.vector.tensor_scalar(fill[:, np_, :, 0:P], mask_in[:, :, :], 0, cfg["masked"],
                                                    ALU.is_equal, ALU.mult)
                            nc.vector.tensor_scalar(fill[:, np_, :, P:KW], last_key, 0, cfg["masked"],
                                                    ALU.is_equal, ALU.mult)
                            nc.vector.tensor_scalar(keep[:, np_, :, P:KW], last_key, 0, cfg["scale"],
                                                    ALU.not_equal, ALU.mult).then_inc(mask_done, 1)
                    if op[0] == "LN":
                        dve.wait_ge(rstd_done, n + 1)
                        for b in range(TG):
                            lnop = nc.vector.tensor_scalar(ln[:, np_, b, :], tile_of(cfg["src"], n * TG + b),
                                                           moments[:, b, 0:1], rstd[:, b:b + 1], ALU.subtract, ALU.mult)
                        if affine:
                            chain.link(lnop)
                            x4 = ln[:, np_, :, :]
                            chain.link(nc.vector.tensor_tensor(x4, x4, bcast(ga[:, :], 1, TG), ALU.mult))
                            lnop = nc.vector.tensor_tensor(x4, x4, bcast(be[:, :], 1, TG), ALU.add)
                        lnop.then_inc(ln_done, 1)
                    if op[0] == "k":
                        c = op[1]
                        bank = jbank[j % 2][:, :]
                        if strided:
                            for b in range(TG):
                                nc.vector.scalar_tensor_tensor(
                                    out=k[:, np_, c, b, 0:P].rearrange("p (i h) -> p i h", h=H),
                                    in0=bank[:, b * P:(b + 1) * P].rearrange("p (i h) -> p i h", h=H),
                                    scalar=bk[:, c:c + 1], in1=bcast(head_of[:, c, :], 1, P // H), op0=ALU.add, op1=ALU.mult)
                            nc.vector.scalar_tensor_tensor(
                                out=k[:, np_, c, :, P:KW],
                                in0=bcast(bank.rearrange("p (b k) -> p b k", b=TG)[:, :, P - 1], 2, H),
                                scalar=bk[:, c:c + 1], in1=bcast(head_of[:, c, :], 1, TG), op0=ALU.add, op1=ALU.mult)\
                              .then_inc(out_of["V"], 1)
                        else:
                            nc.vector.tensor_scalar(k[:, np_, c, :, :].rearrange("p b k -> p (b k)"), bank,
                                                    bk[:, c:c + 1], None, ALU.add).then_inc(out_of["V"], 1)
                    if op[0] == "v":
                        b0 = 2 * op[1]
                        bank = jbank[j % 2][:, :].rearrange("p (b d) -> p b d", b=2)
                        if strided:
                            chain.link(nc.vector.tensor_tensor(vt[:, b0:b0 + 2, :], bank, bcast(bv[:, :], 1, 2), ALU.add))
                            nc.vector.tensor_tensor(v[:, np_, b0:b0 + 2, :].rearrange("p b (h d) -> p b h d", h=H),
                                                    vt[:, b0:b0 + 2, :].rearrange("p b (h d) -> p b h d", h=H),
                                                    bcast(bcast(key_of[:, :], 1, 2), 3, DH), ALU.mult)\
                              .then_inc(out_of["V"], 1)
                        else:
                            nc.vector.tensor_tensor(v[:, np_, b0:b0 + 2, :], bank, bcast(bv[:, :], 1, 2), ALU.add)\
                              .then_inc(out_of["V"], 1)
                    if op[0] == "x":
                        b0 = 2 * op[1]
                        bank = jbank[j % 2][0:H, :].rearrange("p (b d) -> p b d", b=2)
                        chain.link(nc.vector.tensor_tensor(xt[:, b0:b0 + 2, :], bank, bcast(bv[0:H, :], 1, 2), ALU.add))
                        nc.vector.tensor_tensor(vx[:, np_, b0:b0 + 2, :].rearrange("p b (h d) -> p b h d", h=H),
                                                xt[:, b0:b0 + 2, :].rearrange("p b (h d) -> p b h d", h=H),
                                                bcast(bcast(key_of[0:H, :], 1, 2), 3, DH), ALU.mult)\
                          .then_inc(out_of["V"], 1)
                    if op[0] == "SOFT":
                        dve.wait_ge(s_done, g + 1)
                        by_head = lambda t: t[:, :, :].rearrange("p b (i h) -> p b h i", h=NMAX) if strided else t[:, :, :]
                        if strided:
                            for i in range(2):
                                mul = nc.vector.tensor_tensor(
                                    sc[:, 2 * i:2 * i + 2, :], sbank[i][:, 0:2 * KW].rearrange("p (b k) -> p b k", b=2),
                                    keep[:, par, 2 * i:2 * i + 2, :], ALU.mult)
                            mul.then_inc(sc_done, 1)
                            dve.wait_ge(sc_done, g + 1)
                            chain.link(nc.vector.tensor_tensor(sc[:, :, :], sc[:, :, :], fill[:, par, :, :], ALU.add))
                            chain.link(nc.vector.tensor_reduce(best[:, :, :], by_head(sc), AX.X, ALU.max))
                            chain.link(nc.vector.tensor_tensor(
                                sc[:, :, :].rearrange("p b (i h) -> p b i h", h=H),
                                sc[:, :, :].rearrange("p b (i h) -> p b i h", h=H),
                                bcast(best[:, :, :], 2, SLOTS), ALU.subtract))
                        else:
                            s4 = sbank[0][:, :].rearrange("p (b k) -> p b k", b=TG)
                            chain.link(nc.vector.tensor_reduce(best[:, :, 0], s4, AX.X, ALU.max))
                            nc.vector.tensor_tensor(sc[:, :, :], s4, bcast(best[:, :, 0], 2, P), ALU.subtract)\
                              .then_inc(sc_done, 1)
                            dve.wait_ge(sc_done, g + 1)
                    if op[0] == "TOTAL":
                        by_head = lambda t: t[:, :, :].rearrange("p b (i h) -> p b h i", h=NMAX) if strided else t[:, :, :]
                        if strided:
                            dve.wait_ge(exp_done, g + 1)
                            chain.link(nc.vector.tensor_scalar(p[:, :, P:KW], p[:, :, P:KW], float(cfg["repeats"]), None,
                                                               ALU.mult))
                            chain.link(nc.vector.tensor_reduce(total[:, :, :], by_head(p), AX.X, ALU.add))
                        else:
                            dve.wait_ge(exp_done, g + 1)
                            chain.link(nc.vector.tensor_reduce(total[:, :, 0], p[:, :, :], AX.X, ALU.add))
                        nc.vector.reciprocal(recip[:, :, :], total[:, :, :]).then_inc(total_done, 1)
                    if op[0] == "NORM":
                        dve.wait_ge(av_done, g + 1)
                        dve.wait_ge(total_done, g + 1)
                        for i in range(2):
                            if strided:
                                for b in range(2):
                                    mul = nc.vector.tensor_tensor(
                                        o[:, 2 * i + b, :].rearrange("p (h d) -> p h d", h=H),
                                        vbank[i][:, b * D:(b + 1) * D].rearrange("p (h d) -> p h d", h=H),
                                        bcast(recip[:, 2 * i + b, :], 2, DH), ALU.mult)
                            else:
                                mul = nc.vector.tensor_tensor(
                                    o[:, 2 * i:2 * i + 2, :], vbank[i][:, :].rearrange("p (b d) -> p b d", b=2),
                                    bcast(recip[:, 2 * i:2 * i + 2, 0], 2, D), ALU.mult)
                        mul.then_inc(o_done, 1)
                    if op[0] == "OUT":
                        dve.wait_ge(out_done, g + 1)
                        for i in range(2):
                            add = nc.vector.tensor_tensor(res[:, 2 * i:2 * i + 2, :],
                                                          vbank[i][:, :].rearrange("p (b d) -> p b d", b=2),
                                                          bcast(bo[:, :], 1, 2), ALU.add)
                        add.then_inc(res_done, 1)
                        dve.wait_ge(res_done, g + 1)
                        dst = cfg["dst"][:, bass.ds(g * TG, TG), :]
                        base = ln[:, par, :, :] if affine else dst
                        nc.vector.tensor_tensor(dst, res[:, :, :], base, ALU.add)

            run_groups(dve, emit, G, prologue, middle, last)

        @block.scalar
        def _(act):
            act.wait_ge(w_in, 16 * loads)

            def emit(g, par, ops):
                n = g + 1
                ev = counts(g, ops)
                j = -1
                for op in ops:
                    if len(op) == 3:
                        j += 1
                        if op[2] == "A":
                            act.wait_ge(job_done, ev.filled(j))
                    if op[0] == "lnT":
                        nc.scalar.activation(lnT[:, op[1], :], jbank[j % 2][:, :], ACT.Identity).then_inc(out_of["A"], 1)
                    if op[0] == "q":
                        nc.scalar.activation(qT[:, 1 - par, op[1], :], jbank[j % 2][:, :], ACT.Identity,
                                             bias=bq[:, op[1]:op[1] + 1]).then_inc(out_of["A"], 1)
                    if op[0] == "SOFT":
                        if strided:
                            in_front = front_links if ("STATS",) in ops else 0
                            act.wait_ge(chain_sem, next_links + g * (next_links + own_links) + in_front + 3)
                            nc.scalar.activation(p[:, :, :], sc[:, :, :], ACT.Exp).then_inc(exp_done, 1)
                        else:
                            act.wait_ge(sc_done, g + 1)
                            nc.scalar.activation(p[:, :, :], sc[:, :, :], ACT.Exp, scale=cfg["scale"]).then_inc(exp_done, 1)
                    if op[0] == "PT":
                        act.wait_ge(pt_done, g + 1)
                        pe_copy = nc.scalar.activation(pT[:, :, :].rearrange("p b q -> p (b q)"), tbank[:, :], ACT.Identity)
                        if strided:
                            pe_copy = nc.scalar.activation(pxT[:, :, :].rearrange("p b q -> p (b q)"), xbank[0:H, :],
                                                           ACT.Identity)
                        pe_copy.then_inc(pT_done, 1)
                    if op[0] == "OT":
                        act.wait_ge(ot_done, g + 1)
                        for i in range(2):
                            cp = nc.scalar.activation(oT[:, i, :, :, :].rearrange("p b c t -> p (b c t)"), sbank[i][:, :],
                                                      ACT.Identity)
                        cp.then_inc(oT_done, 1)

            run_groups(act, emit, G, prologue, middle, last)

        @block.tensor
        def _(pe):
            pe.wait_ge(w_in, 16 * loads)

            def emit(g, par, ops):
                n = g + 1
                np_ = 1 - par
                ev = counts(g, ops)
                j = -1
                for op in ops:
                    if len(op) == 3:
                        j += 1
                        bank = jbank[j % 2]
                        if ev.before or j >= 2:
                            who, cnt = ev.emptied(j - 2)
                            pe.wait_ge(out_of[who], cnt)
                    if op[0] == "lnT":
                        pe.wait_ge(ln_done, n + 1)
                        for b in range(TG):
                            mm = nc.tensor.transpose(bank[:, b * P:(b + 1) * P], ln[:, np_, b, op[1] * P:(op[1] + 1) * P],
                                                     sh.ident[:, :])
                        mm.then_inc(job_done, 1)
                    if op[0] in ("q", "k"):
                        w, x = (wq, lnT) if op[0] == "q" else (wk, ctxT[:, np_, :, :])
                        if op == ("q", 0, "A"):
                            who, cnt = ev.emptied(ev.place(("lnT", 1)))
                            pe.wait_ge(out_of[who], cnt)
                        if op[0] == "k" and op[1] == 0:
                            pe.wait_ge(ctx_in, 16 * C * (n + 1))
                        for c in range(C):
                            mm = nc.tensor.matmul(bank[:, :], w[:, c, op[1] * P:(op[1] + 1) * P], x[:, c, :],
                                                  start=(c == 0), stop=(c == C - 1))
                        mm.then_inc(job_done, 1)
                    if op[0] == "v":
                        for i in range(2):
                            b = 2 * op[1] + i
                            for c in range(C):
                                mm = nc.tensor.matmul(bank[:, i * D:(i + 1) * D], ctxT[:, np_, c, b * P:(b + 1) * P],
                                                      wv[:, c, :], start=(c == 0), stop=(c == C - 1))
                        mm.then_inc(job_done, 1)
                    if op[0] == "x":
                        for i in range(2):
                            b = 2 * op[1] + i
                            for c in range(C):
                                last_key = ctxT[:, np_, c, (b + 1) * P - 1:(b + 1) * P].broadcast_to([P, H])
                                mm = nc.tensor.matmul(bank[0:H, i * D:(i + 1) * D], last_key, wv[:, c, :],
                                                      start=(c == 0), stop=(c == C - 1))
                        mm.then_inc(job_done, 1)
                    if op[0] == "S":
                        for who in ("A", "V"):
                            pe.wait_ge(out_of[who], (g + 1) * per[who])
                        ge(pe, oT_done, g)
                        for b in range(TG):
                            out = sbank[b // 2][:, (b % 2) * KW:(b % 2 + 1) * KW] if strided else sbank[0][:, b * P:(b + 1) * P]
                            for c in range(C):
                                mm = nc.tensor.matmul(out, qT[:, par, c, b * P:(b + 1) * P], k[:, par, c, b, :],
                                                      start=(c == 0), stop=(c == C - 1))
                        mm.then_inc(s_done, 1)
                    if op[0] == "PT":
                        pe.wait_ge(total_done, g + 1)
                        ge(pe, pT_done, g)
                        for b in range(TG):
                            mm = nc.tensor.transpose(tbank[:, b * P:(b + 1) * P], p[:, b, 0:P], sh.ident[:, :])
                            if strided:
                                mm = nc.tensor.transpose(xbank[0:H, b * P:(b + 1) * P], p[:, b, P:KW], sh.ident[:, :])
                        mm.then_inc(pt_done, 1)
                    if op[0] == "AV":
                        pe.wait_ge(pT_done, g + 1)
                        ge(pe, res_done, g)
                        for b in range(TG):
                            out = vbank[b // 2][:, (b % 2) * D:(b % 2 + 1) * D]
                            mm = nc.tensor.matmul(out, pT[:, b, :], v[:, par, b, :], start=True, stop=not strided)
                            if strided:
                                mm = nc.tensor.matmul(out, pxT[:, b, :], vx[:, par, b, :], start=False, stop=True)
                        mm.then_inc(av_done, 1)
                    if op[0] == "OT":
                        pe.wait_ge(o_done, g + 1)
                        for b in range(TG):
                            for c in range(C):
                                at = ((b % 2) * C + c) * P
                                mm = nc.tensor.transpose(sbank[b // 2][:, at:at + P], o[:, b, c * P:(c + 1) * P], sh.ident[:, :])
                        mm.then_inc(ot_done, 1)
                    if op[0] == "OUT":
                        pe.wait_ge(oT_done, g + 1)
                        for b in range(TG):
                            for c in range(C):
                                mm = nc.tensor.matmul(vbank[b // 2][:, (b % 2) * D:(b % 2 + 1) * D], oT[:, b // 2, b % 2, c, :],
                                                      wo[:, c, :], start=(c == 0), stop=(c == C - 1))
                        mm.then_inc(out_done, 1)

            run_groups(pe, emit, G, prologue, middle, last)


def quantised_weights(nc, name, weights, steps):
    QMAX, SCALING = steps
    ROUND = 1.5 * 2.0 ** 23
    with ExitStack() as ctx:
        m = Memory(nc, ctx, name)
        N = len(weights)
        rank = weights[0][2].shape[0]
        w = [m.sb(f"w{i}", list(x[0].shape)) for i, x in enumerate(weights)]
        t = [m.sb(f"t{i}", list(x[0].shape)) for i, x in enumerate(weights)]
        a = [m.sb(f"a{i}", [rank, x[2].shape[1]]) for i, x in enumerate(weights)]
        b = [m.sb(f"b{i}", [rank, x[3].shape[1]]) for i, x in enumerate(weights)]
        most, most_all, scale, inverse = (m.sb(x, [P, N]) for x in ("most", "most_all", "scale", "inverse"))
        banks = [m.bank(f"bank{i}") for i in range(8)]
        w_in, most_done, all_done, low_done = m.sem("w_in"), m.sem("most"), m.sem("all"), m.sem("low")
        chain_sem = m.sem("chain")
        flat = lambda x: x[:, :, :].rearrange("p c n -> p (c n)")

        def low_rank_pieces():
            at = 0
            for i, x in enumerate(weights):
                _, chunks, cols = x[0].shape
                for c in range(chunks):
                    for n0 in range(0, cols, 512):
                        width = min(512, cols - n0)
                        yield i, c, n0, width, at // 512, at % 512
                        at += width

        block = ctx.enter_context(nc.Block())

        @block.sync
        def _(sp):
            for i, (_, wT, A, BT) in enumerate(weights):
                sp.dma_start(w[i][:, :, :], wT.rearrange("(c p) n -> p c n", p=P)).then_inc(w_in, 16)
                sp.dma_start(a[i][:, :], A).then_inc(w_in, 16)
                sp.dma_start(b[i][:, :], BT).then_inc(w_in, 16)

        @block.gpsimd
        def _(pool):
            pool.wait_ge(most_done, 1)
            nc.gpsimd.partition_all_reduce(most_all[:, :], most[:, :], P, bass.bass_isa.ReduceOp.max).then_inc(all_done, 1)

        @block.tensor
        def _(pe):
            pe.wait_ge(w_in, 48 * N)
            for i, c, n0, width, bank, at in low_rank_pieces():
                mm = nc.tensor.matmul(banks[bank][:, at:at + width], a[i][:, c * P:(c + 1) * P], b[i][:, n0:n0 + width],
                                      start=True, stop=True)
            mm.then_inc(low_done, 1)

        @block.vector
        def _(dve):
            chain = Chain(dve, chain_sem, 0, 0)
            chain.group(-1)
            dve.wait_ge(w_in, 48 * N)
            for i in range(N):
                red = nc.vector.tensor_reduce(most[:, i:i + 1], w[i][:, :, :], AX.XY, ALU.max, apply_absolute_value=True)
            red.then_inc(most_done, 1)
            dve.wait_ge(all_done, 1)
            chain.link(nc.vector.tensor_scalar(scale[:, :], most_all[:, :], 1.0 / QMAX, None, ALU.mult))
            chain.link(nc.vector.reciprocal(inverse[:, :], scale[:, :]))
            for i in range(N):
                chain.link(nc.vector.tensor_scalar(flat(t[i]), flat(w[i]), inverse[:, i:i + 1], None, ALU.mult))
                chain.link(nc.vector.tensor_scalar(flat(t[i]), flat(t[i]), ROUND, ROUND, ALU.add, ALU.subtract))
                chain.link(nc.vector.tensor_scalar(flat(t[i]), flat(t[i]), -QMAX - 1, QMAX, ALU.max, ALU.min))
                chain.link(nc.vector.scalar_tensor_tensor(out=flat(t[i]), in0=flat(t[i]), scalar=scale[:, i:i + 1],
                                                          in1=flat(w[i]), op0=ALU.mult, op1=ALU.subtract))
                chain.link(nc.vector.tensor_tensor(flat(t[i]), flat(t[i]), flat(w[i]), ALU.add))
            dve.wait_ge(low_done, 1)
            for i, c, n0, width, bank, at in low_rank_pieces():
                nc.vector.scalar_tensor_tensor(out=weights[i][0][:, c, n0:n0 + width], in0=banks[bank][:, at:at + width],
                                               scalar=SCALING, in1=t[i][:, c, n0:n0 + width], op0=ALU.mult, op1=ALU.add)


def ffn_quantised(nc, sh, name, G, cfg):
    F = cfg["F"]
    with ExitStack() as ctx:
        m = Memory(nc, ctx, name + "_w")
        w1, w2 = m.sb("w1", [P, C, F]), m.sb("w2", [P, F // P, D])
        quantised_weights(nc, name + "_quant", [(w1, cfg["w1T"], cfg["A1"], cfg["B1T"]), (w2, cfg["w2T"], cfg["A2"], cfg["B2T"])],
                          (127.0, 2.0))
        ffn(nc, sh, name, G, dict(cfg, resident=(w1, w2), affine=None, post=None))


class SharedExpert:

    NF = 4

    def __init__(self, nc, sh, m, cfg, lnT, lnT_done):
        self.nc, self.sh, self.cfg, self.lnT, self.lnT_done = nc, sh, cfg, lnT, lnT_done
        self.FW = cfg["F"] // self.NF
        self.w13 = [m.sb(x, [P, C, cfg["F"]]) for x in ("shared_w1", "shared_w3")]
        self.w2 = m.sb("shared_w2", [self.FW, self.NF, D])
        self.sil = m.sb("sil", [self.FW, 2, GT])
        self.hT = m.sb("hT", [self.FW, self.NF, GT])
        self.hbank = [[m.bank(f"h{i}_{j}") for j in range(2)] for i in range(2)]
        self.ybank = [m.bank(f"y{i}") for i in range(2)]
        self.loaded, self.stored = m.sem("shared_in"), m.sem("stored")
        self.h_done, self.sil_done, self.gate_done = m.sem("h"), m.sem("sil"), m.sem("gate")
        self.y_done, self.out_done = m.sem("y"), m.sem("out")

    def load(self, sp):
        for dst, src in zip(self.w13, (self.cfg["w1T"], self.cfg["w3T"])):
            sp.dma_start(dst[:, :, :], src.rearrange("(c p) n -> p c n", p=P)).then_inc(self.loaded, 16)
        sp.dma_start(self.w2[:, :, :], self.cfg["w2T"].rearrange("(c p) n -> p c n", p=self.FW)).then_inc(self.loaded, 16)

    def store(self, sp, g):
        sp.wait_ge(self.out_done, g + 1)
        sp.dma_start(self.sh.sum_rows[bass.ds(g * GT, GT), :].rearrange("(b t) d -> t b d", t=P),
                     self.cfg["dst"][:, bass.ds(g * TG, TG), :]).then_inc(self.stored, 16)

    def hidden(self, pe, g, par, f):
        U = g * self.NF + f
        if isinstance(g, int) and g == 0 and f == 0:
            pe.wait_ge(self.loaded, 48)
        if f == 0:
            pe.wait_ge(self.lnT_done, C * (g + 1))
        ge(pe, self.gate_done, U - 1)
        for j in range(2):
            for c in range(C):
                mm = self.nc.tensor.matmul(self.hbank[f % 2][j][0:self.FW, :],
                                           self.w13[j][:, c, f * self.FW:(f + 1) * self.FW],
                                           self.lnT[:, par, c, :], start=(c == 0), stop=(c == C - 1))
        mm.then_inc(self.h_done, 1)

    def activate(self, act, g, f):
        U = g * self.NF + f
        act.wait_ge(self.h_done, U + 1)
        ge(act, self.gate_done, U - 1)
        self.nc.scalar.activation(self.sil[:, f % 2, :], self.hbank[f % 2][0][0:self.FW, :], self.cfg["act"])\
            .then_inc(self.sil_done, 1)

    def gate(self, dve, g, f):
        dve.wait_ge(self.sil_done, g * self.NF + f + 1)
        ge(dve, self.y_done, g)
        self.nc.vector.tensor_tensor(self.hT[:, f, :], self.sil[:, f % 2, :], self.hbank[f % 2][1][0:self.FW, :],
                                     ALU.mult).then_inc(self.gate_done, 1)

    def second(self, pe, g):
        pe.wait_ge(self.gate_done, (g + 1) * self.NF)
        ge(pe, self.out_done, g)
        for b in range(TG):
            for f in range(self.NF):
                mm = self.nc.tensor.matmul(self.ybank[b // 2][:, (b % 2) * D:(b % 2 + 1) * D],
                                           self.hT[:, f, b * P:(b + 1) * P], self.w2[:, f, :],
                                           start=(f == 0), stop=(f == self.NF - 1))
        mm.then_inc(self.y_done, 1)

    def add(self, dve, g):
        dve.wait_ge(self.y_done, g + 1)
        for i in range(2):
            dst = self.cfg["dst"][:, bass.ds(g * TG + 2 * i, 2), :]
            add = self.nc.vector.tensor_tensor(dst, self.ybank[i][:, :].rearrange("p (b d) -> p b d", b=2), dst, ALU.add)
        add.then_inc(self.out_done, 1)

FAR = 1.0e6


class Steps:

    def __init__(self, eng, sem, per):
        self.eng, self.sem, self.per, self.k = eng, sem, per, per

    def at(self, index):
        assert self.k == self.per, (self.k, self.per)
        self.base, self.k = index * self.per, 0

    def link(self, ins):
        self.k += 1
        ins.then_inc(self.sem, 1)
        self.eng.wait_ge(self.sem, self.base + self.k)


def zero_rows(nc, sh, ctx):
    spare = sh.token_rows.shape[0] - sh.NT * P
    m = Memory(nc, ctx, "rows")
    zero = m.sb("zero", [P, D])
    set_, done = m.sem("set"), m.sem("done")
    with nc.Block() as block:
        @block.vector
        def _(dve):
            nc.vector.memset(zero[:, :], 0.0).then_inc(set_, 1)

        @block.sync
        def _(sp):
            sp.wait_ge(set_, 1)
            for table in (sh.token_rows, sh.sum_rows):
                sp.dma_start(table[sh.NT * P:, :].rearrange("(r p) d -> p r d", p=P), bcast(zero[:, :], 1, spare // P))\
                  .then_inc(done, 16)
            sp.wait_ge(done, 32)


def route(nc, sh, name, G, cfg):
    E, K, CAP = cfg["E"], cfg["K"], cfg["CAP"]
    table = cfg["table"]
    NS = table.shape[0]
    with ExitStack() as ctx:
        m = Memory(nc, ctx, name)
        wg = m.sb("wg", [P, C, E])
        bias = m.sb("bias", [P, E]) if cfg["bg"] is not None else None
        sbias = m.sb("sbias", [P, E]) if cfg["sb"] is not None else None
        b2 = m.sb("b2", [E, D]) if cfg["b2"] is not None else None
        expert_no = m.sb("expert_no", [P, E])
        token_no = m.sb("token_no", [P, G * TG], I32)
        before = m.sb("before", [P, P], BF16)
        ones = m.sb("ones", [P, P], BF16)
        initial = m.sb("initial", [P, NS // P, 2], I32)
        stats, moments = m.sb("stats", [P, TG, 6]), m.sb("moments", [P, TG, 2])
        veps, rstd = m.sb("veps", [P, TG]), m.sb("rstd", [P, TG])
        ln = m.sb("ln", [P, 2, TG, D])
        lnT = m.sb("lnT", [P, 2, C, GT])
        logit, prob = m.sb("logit", [P, TG, E]), m.sb("prob", [P, TG, E])
        choice = m.sb("choice", [P, TG, E]) if sbias is not None else prob
        top, total, inv = m.sb("top", [P, TG]), m.sb("total", [P, TG]), m.sb("inv", [P, TG])
        best = m.sb("best", [P, TG, 8])
        best_at = m.sb("best_at", [P, TG, 8], U32)
        at_f = m.sb("at_f", [P, TG, K])
        hot = m.sb("hot", [P, TG * K, E])
        work = m.sb("work", [P, TG * K, E])
        taken = m.sb("taken", [P, 2, TG, E], BF16)
        taken_sum = m.sb("taken_sum", [P, E])
        so_far = m.sb("so_far", [P, 2, E], BF16)
        place = m.sb("place", [P, TG, K])
        weight = m.sb("weight", [P, TG, K])
        slot_f, over = m.sb("slot_f", [P, TG, K]), m.sb("over", [P, TG, K])
        slot = m.sb("slot", [P, 2, TG * K], U32)
        pay = m.sb("pay", [P, 2, TG * K, 2], I32)
        kept = m.sb("kept", [P, TG, K])
        wsum, wT = m.sb("wsum", [P, TG, E]), m.sb("wT", [E, TG, P])

        shared = cfg.get("shared")
        tb = [m.bank(f"t{i}") for i in range(1 if shared else C)]
        lbank = m.bank("l")
        pbank = lbank[:, 256:512] if shared else m.bank("p")[:, 0:256]
        if b2 is not None:
            wbank = m.bank("w")
            bbank = [m.bank(f"b{i}") for i in range(2)]

        w_in, const, const_step = m.sem("w_in"), m.sem("const"), m.sem("const_step")
        table_set = m.sem("table_set")
        pay_out = [sh.pool_dma_sems.pop() for _ in range(2)]
        rows_out = [m.sem(f"rows_out{i}") for i in range(2)]
        stats_done, veps_done, rstd_done, ln_done = m.sem("stats"), m.sem("veps"), m.sem("rstd"), m.sem("ln")
        t_done, lnT_done, l_done = m.sem("t"), m.sem("lnT"), m.sem("l")
        logit_done, exp_done, taken_done, p_done = m.sem("logit"), m.sem("exp"), m.sem("taken"), m.sem("p")
        slot_done, wsum_done, wt_done, wT_done = m.sem("slot"), m.sem("wsum"), m.sem("wt"), m.sem("wT")
        b_done, x_done, x_out = m.sem("b"), m.sem("x"), m.sem("x_out")
        front_sem, back_sem, so_far_done = m.sem("front"), m.sem("back"), m.sem("so_far")

        if shared:
            shared = SharedExpert(nc, sh, m, shared, lnT, lnT_done)
        prologue = [("STATS",), ("LN",), ("T",), ("LG",)]
        bias2 = b2 is not None
        if shared:
            middle = [("SOFT",), ("PICK",), ("H", 0), ("H", 1), ("ADD", -1), ("STATS",), ("PLACE",), ("H", 2), ("LN",), ("H", 3),
                      ("T",), ("LG",), ("Y",)]
            last = [x for x in middle if x not in prologue] + [("ADD", 0)]
        else:
            middle = [("SOFT",), ("PICK",), ("STATS",), ("BIAS2", -1), ("PLACE",), ("LN",), ("T",), ("LG",)]
            last = [("SOFT",), ("PICK",), ("BIAS2", -1), ("PLACE",), ("BIAS2", 0)]
        loads = 1 + sum(x is not None for x in (bias, sbias, b2))
        trash0 = sh.NT * P
        block_context = ExitStack()
        block = block_context.enter_context(nc.Block())

        @block.sync
        def _(sp):
            sp.dma_start(wg[:, :, :], cfg["wg"].rearrange("(c p) e -> p c e", p=P)).then_inc(w_in, 16)
            for dst, src in ((bias, cfg["bg"]), (sbias, cfg["sb"])):
                if dst is not None:
                    sp.dma_start(dst[:, :], rows(src)).then_inc(w_in, 16)
            if bias2:
                sp.dma_start(b2[:, :], cfg["b2"]).then_inc(w_in, 16)
            if cfg.get("weights"):
                cfg["weights"].first(sp)
            if shared:
                shared.load(sp)
            sp.wait_ge(const, 2)
            sp.dma_start(table.rearrange("(p r) c -> p r c", p=P), initial[:, :, :]).then_inc(table_set, 16)

            def emit(g0, par, ops):
                n = g0 + 1
                for op in ops:
                    g = g0 + op[1] if op[0] == "BIAS2" else g0
                    if isinstance(g, int) and op[0] == "BIAS2" and g < 0:
                        continue
                    if op[0] == "T":
                        sp.wait_ge(ln_done, n + 1)
                        sp.dma_start(sh.token_rows[bass.ds(n * GT, GT), :].rearrange("(b t) d -> t b d", t=P),
                                     ln[:, 1 - par, :, :]).then_inc(rows_out[1 - par], 16)
                    if op[0] == "SOFT" and cfg.get("weights"):
                        cfg["weights"].load(sp, g)
                    if op[0] == "ADD" and not (isinstance(g, int) and g + op[1] < 0):
                        shared.store(sp, g + op[1])
                    if op[0] == "BIAS2":
                        sp.wait_ge(x_done, g + 1)
                        sp.dma_start(sh.sum_rows[bass.ds(g * GT, GT), :].rearrange("(b t) d -> t b d", t=P),
                                     cfg["src"][:, bass.ds(g * TG, TG), :]).then_inc(x_out, 16)

            run_groups(sp, emit, G, prologue, middle, last)
            for sem in rows_out:
                sp.wait_ge(sem, 16 * (G // 2))
            ge(sp, x_out, 16 * G * bias2)
            if shared:
                sp.wait_ge(shared.stored, 16 * G)

        @block.gpsimd
        def _(pool):
            nc.gpsimd.iota(expert_no[:, :], [[1, E]], base=0, channel_multiplier=0,
                           allow_small_or_imprecise_dtypes=True)
            nc.gpsimd.iota(token_no[:, :], [[P, G * TG]], base=0, channel_multiplier=1)
            nc.gpsimd.memset(ones[:, :], 1.0)
            nc.gpsimd.memset(before[:, :], 1.0).then_inc(const_step, 1)
            pool.wait_ge(const_step, 1)
            nc.gpsimd.affine_select(out=before[:, :], in_=before[:, :], compare_op=ALU.is_gt, fill=0.0, base=0,
                                    pattern=[[1, P]], channel_multiplier=-1).then_inc(const, 1)
            nc.gpsimd.memset(initial[:, :, 1], 0).then_inc(const_step, 1)
            pool.wait_ge(const_step, 2)
            nc.gpsimd.iota(initial[:, :, 0], cfg["trash"][0], base=trash0, channel_multiplier=cfg["trash"][1])\
              .then_inc(const, 1)

            def emit(g0, par, ops):
                n = g0 + 1
                for op in ops:
                    g = g0 + op[1] if op[0] == "BIAS2" else g0
                    if isinstance(g, int) and op[0] == "BIAS2" and g < 0:
                        continue
                    if op[0] == "STATS":
                        pool.wait_ge(stats_done, n + 1)
                        settle(pool, sh)
                        nc.gpsimd.tensor_scalar(veps[:, :], moments[:, :, 1], cfg["eps"], None, ALU.add)\
                          .then_inc(veps_done, 1)
                        pool.wait_ge(veps_done, n + 1)
                        nc.gpsimd.tensor_tensor(rstd[:, :], veps[:, :], sh.power[:, :], ALU.pow).then_inc(rstd_done, 1)
                    if op[0] == "PLACE":
                        pool.wait_ge(slot_done, g + 1)
                        settle(pool, sh)
                        if isinstance(g, int) and g == 0:
                            pool.wait_ge(table_set, 16)
                        for i in range(TG * K):
                            nc.gpsimd.indirect_dma_start(
                                table, bass.IndirectOffsetOnAxis(ap=slot[:, par, i:i + 1], axis=0), pay[:, par, i, :], None,
                                bounds_check=NS - 1, oob_is_err=False).then_inc(pay_out[par], 16)

            run_groups(pool, emit, G, prologue, middle, last)
            for sem in pay_out:
                pool.wait_ge(sem, 8 * G * TG * K)

        @block.vector
        def _(dve):
            nc.vector.memset(pay[:, :, :, :], 0)
            nc.vector.memset(so_far[:, 0, :], 0.0).then_inc(so_far_done, 1)
            front = Steps(dve, front_sem, 1)
            per = 11 + (bias is not None) + (sbias is not None) + 2 * (cfg["weight"] == "score")
            per += (1 if CAP is None else 3) + 2 * (bias2 and cfg["weight"] != "one")
            back = Steps(dve, back_sem, per)

            def emit(g0, par, ops):
                n = g0 + 1
                by_k = lambda t: t[:, :, :].rearrange("p (b k) e -> p b k e", b=TG)
                for op in ops:
                    g = g0 + op[1] if op[0] == "BIAS2" else g0
                    if isinstance(g, int) and op[0] == "BIAS2" and g < 0:
                        continue
                    if op[0] == "STATS":
                        front.at(n)
                        for b in range(TG):
                            bn = nc.vector.bn_stats(stats[:, b, :], tile_of(cfg["src"], n * TG + b))
                        front.link(bn)
                        settle(dve, sh)
                        for b in range(TG):
                            bn = nc.vector.bn_aggr(moments[:, b, :], stats[:, b, :])
                        bn.then_inc(stats_done, 1)
                        if isinstance(g, int) and g < 0:
                            dve.wait_ge(w_in, 16 * loads)
                            dve.wait_ge(const, 2)
                    if op[0] == "LN":
                        dve.wait_ge(rstd_done, n + 1)
                        ge(dve, rows_out[1 - par], 8 * n if par == 1 else 8 * (n - 1))
                        for b in range(TG):
                            lnop = nc.vector.tensor_scalar(ln[:, 1 - par, b, :], tile_of(cfg["src"], n * TG + b),
                                                           moments[:, b, 0:1], rstd[:, b:b + 1], ALU.subtract, ALU.mult)
                        lnop.then_inc(ln_done, 1)
                    if op[0] == "SOFT":
                        back.at(g)
                        dve.wait_ge(l_done, g + 1)
                        logits = lbank[:, 0:TG * E].rearrange("p (b e) -> p b e", b=TG)
                        if bias is not None:
                            back.link(nc.vector.tensor_tensor(logit[:, :, :], logits, bcast(bias[:, :], 1, TG), ALU.add))
                            logits = logit[:, :, :]
                        back.link(nc.vector.tensor_reduce(top[:, :], logits, AX.X, ALU.max))
                        nc.vector.tensor_tensor(logit[:, :, :], logits, bcast(top[:, :], 2, E), ALU.subtract)\
                          .then_inc(logit_done, 1)
                    if op[0] == "PICK":
                        dve.wait_ge(exp_done, g + 1)
                        back.link(nc.vector.tensor_reduce(total[:, :], prob[:, :, :], AX.X, ALU.add))
                        back.link(nc.vector.reciprocal(inv[:, :], total[:, :]))
                        back.link(nc.vector.tensor_tensor(prob[:, :, :], prob[:, :, :], bcast(inv[:, :], 2, E), ALU.mult))
                        if sbias is not None:
                            back.link(nc.vector.tensor_tensor(choice[:, :, :], prob[:, :, :], bcast(sbias[:, :], 1, TG),
                                                              ALU.add))
                        settle(dve, sh)
                        for b in range(TG):
                            mx = nc.vector.max(best[:, b, :], choice[:, b, :])
                        back.link(mx)
                        settle(dve, sh)
                        for b in range(TG):
                            mx = nc.vector.max_index(best_at[:, b, :], best[:, b, :], choice[:, b, :])
                        back.link(mx)
                        settle(dve, sh)
                        back.link(nc.vector.tensor_copy(at_f[:, :, :], best_at[:, :, 0:K]))
                        back.link(nc.vector.tensor_tensor(hot[:, :, :], bcast(expert_no[:, :], 1, TG * K),
                                                          bcast(at_f[:, :, :].rearrange("p b k -> p (b k)"), 2, E),
                                                          ALU.is_equal))
                        with nc.allow_low_precision(reason="zeroes and ones"):
                            nc.vector.tensor_reduce(taken[:, par, :, :], by_k(hot).rearrange("p b k e -> p b e k"), AX.X,
                                                    ALU.add).then_inc(taken_done, 1)
                        dve.wait_ge(taken_done, g + 1)
                        back.link(nc.vector.tensor_reduce(taken_sum[:, :], taken[:, par, :, :].rearrange("p b e -> p e b"),
                                                          AX.X, ALU.add))
                        dve.wait_ge(so_far_done, g + 1)
                        nc.vector.tensor_tensor(so_far[:, 1 - par, :], so_far[:, par, :], taken_sum[:, :], ALU.add)\
                          .then_inc(so_far_done, 1)
                        if cfg["weight"] == "score":
                            back.link(nc.vector.tensor_tensor(by_k(work), by_k(hot), bcast(prob[:, :, :], 2, K), ALU.mult))
                            back.link(nc.vector.tensor_reduce(weight[:, :, :], by_k(work), AX.X, ALU.add))
                    if op[0] == "PLACE":
                        dve.wait_ge(p_done, g + 1)
                        places = pbank[:, 0:TG * E].rearrange("p (b e) -> p b e", b=TG)
                        back.link(nc.vector.tensor_tensor(by_k(work), by_k(hot), bcast(places, 2, K), ALU.mult))
                        back.link(nc.vector.tensor_reduce(place[:, :, :], by_k(work), AX.X, ALU.add))
                        if CAP is None:
                            back.link(nc.vector.scalar_tensor_tensor(out=slot_f[:, :, :], in0=at_f[:, :, :],
                                                                     scalar=float(sh.NT * P), in1=place[:, :, :],
                                                                     op0=ALU.mult, op1=ALU.add))
                        else:
                            back.link(nc.vector.tensor_scalar(over[:, :, :], place[:, :, :], float(CAP), FAR, ALU.is_ge,
                                                              ALU.mult))
                            back.link(nc.vector.tensor_scalar(slot_f[:, :, :], place[:, :, :], float(E), None, ALU.mult))
                            back.link(nc.vector.tensor_tensor(slot_f[:, :, :], slot_f[:, :, :], at_f[:, :, :], ALU.add))
                        ge(dve, pay_out[par], 8 * TG * K * (g if par == 0 else g - 1))
                        slots = slot[:, par, :].rearrange("p (b k) -> p b k", b=TG)
                        if CAP is None:
                            nc.vector.tensor_copy(slots, slot_f[:, :, :])
                        else:
                            nc.vector.tensor_tensor(slots, slot_f[:, :, :], over[:, :, :], ALU.add)
                        pay4 = pay[:, par, :, :].rearrange("p (b k) c -> p b k c", b=TG)
                        payop = nc.vector.tensor_copy(pay4[:, :, :, 0], bcast(token_no[:, bass.ds(g * TG, TG)], 2, K))
                        if cfg["weight"] != "one":
                            w = best[:, :, 0:K] if cfg["weight"] == "best" else weight[:, :, :]
                            payop = nc.vector.tensor_copy(pay4[:, :, :, 1].bitcast(F32), w)
                        payop.then_inc(slot_done, 1)
                        if bias2 and cfg["weight"] == "one":
                            nc.vector.tensor_copy(wsum[:, :, :], taken[:, par, :, :]).then_inc(wsum_done, 1)
                        if bias2 and cfg["weight"] == "best":
                            back.link(nc.vector.tensor_scalar(kept[:, :, :], place[:, :, :], float(CAP), None, ALU.is_lt))
                            back.link(nc.vector.tensor_tensor(kept[:, :, :], kept[:, :, :], best[:, :, 0:K], ALU.mult))
                            nc.vector.tensor_tensor(wsum[:, :, :], hot[:, :, :], bcast(kept[:, :, 0], 2, E), ALU.mult)\
                              .then_inc(wsum_done, 1)
                    if op[0] == "H":
                        shared.gate(dve, g, op[1])
                    if op[0] == "ADD" and not (isinstance(g, int) and g + op[1] < 0):
                        shared.add(dve, g + op[1])
                    if op[0] == "BIAS2":
                        dve.wait_ge(b_done, g + 1)
                        for i in range(2):
                            dst = cfg["src"][:, bass.ds(g * TG + 2 * i, 2), :]
                            add = nc.vector.tensor_tensor(dst, bbank[i][:, :].rearrange("p (b d) -> p b d", b=2), dst, ALU.add)
                        add.then_inc(x_done, 1)

            run_groups(dve, emit, G, prologue, middle, last, peeled=1)

        @block.scalar
        def _(act):
            def emit(g0, par, ops):
                n = g0 + 1
                for op in ops:
                    g = g0 + op[1] if op[0] == "BIAS2" else g0
                    if isinstance(g, int) and op[0] == "BIAS2" and g < 0:
                        continue
                    if op[0] == "T":
                        for c in range(C):
                            act.wait_ge(t_done, n * C + c + 1)
                            nc.scalar.activation(lnT[:, 1 - par, c, :], tb[c % len(tb)][:, :], ACT.Identity)\
                              .then_inc(lnT_done, 1)
                    if op[0] == "H":
                        shared.activate(act, g, op[1])
                    if op[0] == "SOFT":
                        act.wait_ge(logit_done, g + 1)
                        nc.scalar.activation(prob[:, :, :], logit[:, :, :], ACT.Exp).then_inc(exp_done, 1)
                    if op[0] == "BIAS2":
                        act.wait_ge(wt_done, g + 1)
                        nc.scalar.activation(wT[:, :, :].rearrange("e b t -> e (b t)"), wbank[0:E, :], ACT.Identity)\
                          .then_inc(wT_done, 1)

            run_groups(act, emit, G, prologue, middle, last)

        @block.tensor
        def _(pe):
            pe.wait_ge(w_in, 16 * loads)
            pe.wait_ge(const, 2)

            def emit(g0, par, ops):
                n = g0 + 1
                for op in ops:
                    g = g0 + op[1] if op[0] == "BIAS2" else g0
                    if isinstance(g, int) and op[0] == "BIAS2" and g < 0:
                        continue
                    if op[0] == "T":
                        pe.wait_ge(ln_done, n + 1)
                        for c in range(C):
                            ge(pe, lnT_done, n * C + (c if shared else 0))
                            for b in range(TG):
                                mm = nc.tensor.transpose(tb[c % len(tb)][:, b * P:(b + 1) * P], ln[:, 1 - par, b, c * P:(c + 1) * P],
                                                         sh.ident[:, :])
                            mm.then_inc(t_done, 1)
                    if op[0] == "LG":
                        pe.wait_ge(lnT_done, (n + 1) * C)
                        ge(pe, logit_done, n)
                        if shared:
                            ge(pe, slot_done, n)
                        for b in range(TG):
                            for c in range(C):
                                mm = nc.tensor.matmul(lbank[:, b * E:(b + 1) * E], lnT[:, 1 - par, c, b * P:(b + 1) * P], wg[:, c, :],
                                                      start=(c == 0), stop=(c == C - 1))
                        mm.then_inc(l_done, 1)
                    if op[0] == "PLACE":
                        pe.wait_ge(taken_done, g + 1)
                        pe.wait_ge(so_far_done, g + 1)
                        for b in range(TG):
                            out = pbank[:, b * E:(b + 1) * E]
                            nc.tensor.matmul(out, before[:, :], taken[:, par, b, :], start=True, stop=False)
                            for a in range(b):
                                nc.tensor.matmul(out, ones[:, :], taken[:, par, a, :], start=False, stop=False)
                            mm = nc.tensor.matmul(out, ones[:, :], so_far[:, par, :], start=False, stop=True)
                        mm.then_inc(p_done, 1)
                    if op[0] == "H":
                        shared.hidden(pe, g, par, op[1])
                    if op[0] == "Y":
                        shared.second(pe, g)
                    if op[0] == "BIAS2":
                        pe.wait_ge(wsum_done, g + 1)
                        ge(pe, wT_done, g)
                        for b in range(TG):
                            mm = nc.tensor.transpose(wbank[0:E, b * P:(b + 1) * P], wsum[:, b, :], sh.ident[:, :])
                        mm.then_inc(wt_done, 1)
                        pe.wait_ge(wT_done, g + 1)
                        ge(pe, x_done, g)
                        for b in range(TG):
                            mm = nc.tensor.matmul(bbank[b // 2][:, (b % 2) * D:(b % 2 + 1) * D], wT[:, b, :], b2[:, :],
                                                  start=True, stop=True)
                        mm.then_inc(b_done, 1)

            run_groups(pe, emit, G, prologue, middle, last)

        block_context.close()
        if CAP is None:
            number_tiles(nc, sh, m, cfg, so_far, ones)


def number_tiles(nc, sh, m, cfg, so_far, ones):
    E, tile_expert, tile_row = cfg["E"], cfg["tile_expert"], cfg["tile_row"]
    TILES = tile_expert.shape[1]
    WHOLE = 1.5 * 2.0 ** 23
    DOWN = 0.5 - 1.0 / (2 * P)
    filled, ends = m.sb("filled", [P, E]), m.sb("ends", [P, E + 1])
    tile_no = m.sb("tile_no", [P, TILES])
    after = m.sb("after", [P, TILES, E])
    lengths = m.sb("lengths", [P, TILES, E - 1])
    expert, row, past = m.sb("expert", [P, TILES]), m.sb("row", [P, TILES]), m.sb("past", [P, TILES])
    bank = m.bank("count")
    count_done, no_done, step = m.sem("count"), m.sem("tile_no"), m.sem("number_step")
    with nc.Block() as block:
        @block.tensor
        def _(pe):
            nc.tensor.matmul(bank[:, 0:E], ones[:, :], so_far[:, 0, :], start=True, stop=True).then_inc(count_done, 1)

        @block.gpsimd
        def _(pool):
            nc.gpsimd.iota(tile_no[:, :], [[1, TILES]], base=0, channel_multiplier=0, allow_small_or_imprecise_dtypes=True)\
              .then_inc(no_done, 1)

        @block.vector
        def _(dve):
            steps = Steps(dve, step, 12 + E)
            steps.at(0)
            dve.wait_ge(count_done, 1)
            steps.link(nc.vector.tensor_scalar(filled[:, :], bank[:, 0:E], P - 1.0, 1.0 / P, ALU.add, ALU.mult))
            steps.link(nc.vector.tensor_scalar(filled[:, :], filled[:, :], -DOWN, WHOLE, ALU.add, ALU.add))
            steps.link(nc.vector.tensor_scalar(filled[:, :], filled[:, :], WHOLE, None, ALU.subtract))
            steps.link(nc.vector.memset(ends[:, 0:1], 0.0))
            for e in range(E):
                steps.link(nc.vector.tensor_tensor(ends[:, e + 1:e + 2], ends[:, e:e + 1], filled[:, e:e + 1], ALU.add))
            dve.wait_ge(no_done, 1)
            steps.link(nc.vector.tensor_tensor(after[:, :, :], bcast(tile_no[:, :], 2, E), bcast(ends[:, 1:E + 1], 1, TILES),
                                               ALU.is_ge))
            steps.link(nc.vector.tensor_reduce(expert[:, :], after[:, :, 0:E - 1], AX.X, ALU.add))
            steps.link(nc.vector.tensor_copy(tile_expert[:, :], expert[:, :]))
            steps.link(nc.vector.tensor_tensor(lengths[:, :, :], after[:, :, 0:E - 1], bcast(filled[:, 0:E - 1], 1, TILES),
                                               ALU.mult))
            steps.link(nc.vector.tensor_reduce(row[:, :], lengths[:, :, :], AX.X, ALU.add))
            steps.link(nc.vector.tensor_tensor(row[:, :], tile_no[:, :], row[:, :], ALU.subtract))
            steps.link(nc.vector.scalar_tensor_tensor(out=row[:, :], in0=expert[:, :], scalar=float(sh.NT), in1=row[:, :],
                                                      op0=ALU.mult, op1=ALU.add))
            steps.link(nc.vector.scalar_tensor_tensor(out=past[:, :], in0=after[:, :, E - 1], scalar=FAR, in1=row[:, :],
                                                      op0=ALU.mult, op1=ALU.add))
            nc.vector.tensor_scalar(tile_row[:, :], past[:, :], float(E * sh.NT), None, ALU.min)


def experts(nc, sh, name, cfg):
    T, S, U, F = cfg["TILES"], cfg["S"], cfg["unroll"], cfg["F"]
    gated = cfg.get("w3T") is not None
    FW = F // 2 if gated else P
    NF = F // FW
    WIDTH = 2 * F if gated else F
    SLOTS = 4
    with ExitStack() as ctx:
        m = Memory(nc, ctx, name)
        if gated:
            w1 = m.sb("w1", [P, SLOTS, C, WIDTH])
            w2 = m.sb("w2", [FW, SLOTS, NF, D])
            sil = m.sb("sil", [S, 2, F])
        else:
            w1, w2, b1 = cfg["w1"], cfg["w2"], cfg["b1"]
        tab = m.sb("tab", [S, T, 2], I32)
        gather_at = m.sb("gather_at", [S, 2], U32)
        scatter_at = m.sb("scatter_at", [S, 2], U32)
        xg = m.sb("xg", [S, 2, D])
        xT = m.sb("xT", [P, 2, C, S])
        g = m.sb("g", [S, 2, F])
        hT = m.sb("hT", [FW, NF, S])
        y = m.sb("y", [S, 2, D])

        HB = -(-WIDTH // 512)
        hbank = [[m.bank(f"h{i}_{j}") for j in range(HB)] for i in range(2)]
        thbank = [m.bank(f"th{j}") for j in range(-(-NF * S // 512))]
        per_th = 512 // S if not gated else NF
        txbank, ybank = m.bank("txbank"), m.bank("ybank")

        tab_in = m.sem("tab_in")
        rows_in = [m.sem(f"rows_in{i}") for i in range(2)]
        w_in = [m.sem(f"w_in{i}") for i in range(SLOTS)] if gated else None
        gather_at_done = m.sem("gather_at")
        gather_done = [sh.pool_dma_sems.pop() for _ in range(2)]
        scatter_done = sh.pool_dma_sems.pop()
        tx_done, xT_done, h_done, sil_done, g_done = m.sem("tx"), m.sem("xT"), m.sem("h"), m.sem("sil"), m.sem("g")
        th_done, hT_done, y_done, out_done = m.sem("th"), m.sem("hT"), m.sem("y"), m.sem("out")

        def run_tiles(emit, eng):
            ends = -(-3 // U)
            for s in range(ends * U):
                emit(s, s % U)
            with eng.Fori(ends, T // U - ends) as t:
                for u in range(U):
                    emit(t * U + u, u)
            for s in range(T - ends * U, T):
                emit(s, s % U)
            emit(T, 0)

        def exists(i):
            return not isinstance(i, (int, np.integer)) or 0 <= i < T

        def gathered(i, par):
            return 8 * i + 16 if par == 0 else 8 * i + 8

        block = ctx.enter_context(nc.Block())

        @block.sync
        def _(sp):
            for src, part in cfg["table"] or []:
                sp.dma_start(tab[:, part, :], src).then_inc(tab_in, 16)

            def table_rows(i, par):
                if exists(i):
                    ge(sp, gather_at_done, i - 1)
                    settle(sp, sh)
                    row = sp.value_load(cfg["tile_row"][0:1, bass.ds(i, 1)], min_val=0, max_val=cfg["rows"].shape[1] - 1)
                    sp.dma_start(tab[:, bass.ds(i, 1), :], cfg["rows"][:, bass.ds(row, 1), :]).then_inc(rows_in[par], 16)

            if cfg["table"] is None:
                run_tiles(lambda i, u: table_rows(i, u % 2), sp)

            def load(i, u):
                if gated and exists(i):
                    ge(sp, y_done, i - SLOTS + 1)
                    for half, src in ((0, cfg["w1T"]), (1, cfg["w3T"])):
                        sp.dma_start(w1[:, u % SLOTS, :, half * F:(half + 1) * F],
                                     src[bass.ds(i, 1), :, :].rearrange("o (c p) n -> p (o c) n", p=P))\
                          .then_inc(w_in[u % SLOTS], 16)
                    sp.dma_start(w2[:, u % SLOTS, :, :],
                                 cfg["w2T"][bass.ds(i, 1), :, :].rearrange("o (c p) n -> p (o c) n", p=FW))\
                      .then_inc(w_in[u % SLOTS], 16)

            if gated:
                run_tiles(load, sp)

        @block.gpsimd
        def _(pool):
            def gather(i, par):
                if exists(i):
                    pool.wait_ge(gather_at_done, i + 1)
                    ge(pool, tx_done, i - 1)
                    settle(pool, sh)
                    nc.gpsimd.indirect_dma_start(xg[:, par, :], None, sh.token_rows,
                                                 bass.IndirectOffsetOnAxis(ap=gather_at[:, par:par + 1], axis=0))\
                      .then_inc(gather_done[par], 16)

            def step(s, u):
                gather(s + 2, u % 2)
                if exists(s - 1):
                    pool.wait_ge(out_done, s)
                    ge(pool, scatter_done, 16 * (s - 1))
                    settle(pool, sh)
                    par = (u + 1) % 2
                    nc.gpsimd.indirect_dma_start(sh.sum_rows, bass.IndirectOffsetOnAxis(ap=scatter_at[:, par:par + 1], axis=0),
                                                 y[:, par, :], None, compute_op=ALU.add).then_inc(scatter_done, 16)

            gather(0, 0)
            gather(1, 1)
            run_tiles(step, pool)
            pool.wait_ge(scatter_done, 16 * T)

        @block.vector
        def _(dve):
            if cfg["table"]:
                dve.wait_ge(tab_in, 16 * len(cfg["table"]))

            def indices(i, par):
                if exists(i):
                    if not cfg["table"]:
                        dve.wait_ge(rows_in[par], gathered(i, par))
                    ge(dve, gather_done[par], gathered(i - 2, par))
                    nc.vector.tensor_copy(gather_at[:, par:par + 1], tab[:, bass.ds(i, 1), 0]).then_inc(gather_at_done, 1)

            def step(s, u):
                par = u % 2
                if exists(s):
                    dve.wait_ge(sil_done if gated else h_done, s + 1)
                    ge(dve, th_done, s - 1)
                    if gated:
                        gop = nc.vector.tensor_tensor(g[:, par, :], sil[:, par, :], hbank[par][0][0:S, F:2 * F], ALU.mult)
                    else:
                        for j in range(HB):
                            gop = nc.vector.tensor_copy(g[:, par, j * 512:(j + 1) * 512], hbank[par][j][0:S, :])
                    gop.then_inc(g_done, 1)
                if exists(s - 1):
                    i, ipar = s - 1, 1 - par
                    dve.wait_ge(y_done, i + 1)
                    ge(dve, scatter_done, 16 * (i - 1))
                    nc.vector.tensor_copy(scatter_at[:, ipar:ipar + 1], tab[:, bass.ds(i, 1), 0])
                    if cfg["weighted"]:
                        yop = nc.vector.tensor_scalar(y[:, ipar, :], ybank[0:S, 0:D],
                                                      tab[:, bass.ds(i, 1), 1].bitcast(F32), None, ALU.mult)
                    else:
                        yop = nc.vector.tensor_copy(y[:, ipar, :], ybank[0:S, 0:D])
                    yop.then_inc(out_done, 1)
                indices(s + 3, 1 - par)

            indices(0, 0)
            indices(1, 1)
            indices(2, 0)
            run_tiles(step, dve)

        @block.scalar
        def _(act):
            if not gated:
                act.wait_ge(*cfg["w_in"])

            def xT_out(i, par):
                if exists(i):
                    act.wait_ge(tx_done, i + 1)
                    ge(act, h_done, i - 1)
                    nc.scalar.activation(xT[:, par, :, :].rearrange("p c s -> p (c s)"), txbank[:, 0:C * S], ACT.Identity)\
                      .then_inc(xT_done, 1)

            def step(s, u):
                par = u % 2
                if exists(s - 1):
                    i = s - 1
                    act.wait_ge(th_done, i + 1)
                    ge(act, y_done, i)
                    if gated:
                        nc.scalar.activation(hT[:, :, :].rearrange("p f s -> p (f s)"), thbank[0][0:FW, 0:NF * S], ACT.Identity)\
                          .then_inc(hT_done, 1)
                    else:
                        e = cfg["expert"](act, i)
                        for f in range(NF):
                            at = (f % per_th) * S
                            nc.scalar.activation(hT[:, f, :], thbank[f // per_th][:, at:at + S], cfg["act"],
                                                 bias=b1[:, bass.ds(e * NF + f, 1)]).then_inc(hT_done, 1)
                xT_out(s + 1, 1 - par)
                if gated and exists(s):
                    act.wait_ge(h_done, s + 1)
                    ge(act, g_done, s - 1)
                    nc.scalar.activation(sil[:, par, :], hbank[par][0][0:S, 0:F], cfg["act"]).then_inc(sil_done, 1)

            xT_out(0, 0)
            run_tiles(step, act)

        @block.tensor
        def _(pe):
            if not gated:
                pe.wait_ge(*cfg["w_in"])

            def transpose_x(i, par):
                if exists(i):
                    pe.wait_ge(gather_done[par], gathered(i, par))
                    ge(pe, xT_done, i)
                    for c in range(C):
                        tr = nc.tensor.transpose(txbank[:, c * S:(c + 1) * S], xg[:, par, c * P:(c + 1) * P], sh.ident[0:S, 0:S])
                    tr.then_inc(tx_done, 1)

            def step(s, u):
                par = u % 2
                if exists(s - 1):
                    pe.wait_ge(g_done, s)
                    ge(pe, hT_done, (s - 1) * (1 if gated else NF))
                    for f in range(NF):
                        at = (f % per_th) * S
                        tr = nc.tensor.transpose(thbank[f // per_th][0:FW, at:at + S], g[:, 1 - par, f * FW:(f + 1) * FW],
                                                 sh.ident[0:S, 0:S])
                    tr.then_inc(th_done, 1)
                transpose_x(s + 1, 1 - par)
                if exists(s):
                    pe.wait_ge(xT_done, s + 1)
                    ge(pe, g_done, s - 1)
                    if gated:
                        k = u % SLOTS
                        pe.wait_ge(w_in[k], (s - k) * (48 // SLOTS) + 48)
                        for c in range(C):
                            mm = nc.tensor.matmul(hbank[par][0][0:S, 0:WIDTH], xT[:, par, c, :], w1[:, k, c, :],
                                                  start=(c == 0), stop=(c == C - 1))
                    else:
                        e = cfg["expert"](pe, s)
                        for j in range(HB):
                            for c in range(C):
                                mm = nc.tensor.matmul(hbank[par][j][0:S, :], xT[:, par, c, :],
                                                      w1[:, c, bass.ds(e * F + j * 512, 512)], start=(c == 0), stop=(c == C - 1))
                    mm.then_inc(h_done, 1)
                if exists(s - 1):
                    i = s - 1
                    ge(pe, out_done, i)
                    if not gated:
                        e = cfg["expert"](pe, i)
                    for f in range(NF):
                        if gated:
                            if f == 0:
                                pe.wait_ge(hT_done, i + 1)
                            rhs = w2[:, (u - 1) % SLOTS, f, :]
                        else:
                            pe.wait_ge(hT_done, i * NF + f + 1)
                            rhs = w2[:, f, bass.ds(e * D, D)]
                        mm = nc.tensor.matmul(ybank[0:S, 0:D], hT[:, f, :], rhs, start=(f == 0), stop=(f == NF - 1))
                    mm.then_inc(y_done, 1)

            transpose_x(0, 0)
            run_tiles(step, pe)


class ResidentExperts:

    def __init__(self, m, E, F, w1_dram, w2_dram, b1_dram):
        self.E, self.F, self.w1_dram, self.w2_dram, self.b1_dram = E, F, w1_dram, w2_dram, b1_dram
        self.w1 = m.sb("w1", [P, C, E * F])
        self.w2 = m.sb("w2", [P, F // P, E * D])
        self.b1 = m.sb("b1", [P, E * (F // P)])
        self.sem = m.sem("w_in")
        self.loaded = (self.sem, 16 * (2 * E + 1))

    def first(self, eng):
        eng.dma_start(self.b1[:, :], self.b1_dram.rearrange("e (f p) -> p (e f)", p=P), allow_slow_non_contiguous=True)\
           .then_inc(self.sem, 16)

    def load(self, eng, e):
        F = self.F
        eng.dma_start(self.w1[:, :, bass.ds(e * F, F)],
                      self.w1_dram[bass.ds(e, 1), :, :].rearrange("o (c p) f -> p (o c) f", p=P)).then_inc(self.sem, 16)
        eng.dma_start(self.w2[:, :, bass.ds(e * D, D)],
                      self.w2_dram[bass.ds(e, 1), :, :].rearrange("o (f p) d -> p (o f) d", p=P)).then_inc(self.sem, 16)


def ffn_all_resident_routed(nc, sh, name, G, cfg):
    with ExitStack() as ctx:
        m = Memory(nc, ctx, name)
        T, S, F, E = cfg["TILES"], cfg["S"], cfg["F"], cfg["E"]
        tile_expert, tile_row = m.sb("tile_expert", [P, T], I32), m.sb("tile_row", [P, T], I32)
        assert E == G
        weights = ResidentExperts(m, E, F, cfg["w1"], cfg["w2"], cfg["b1"])
        route(nc, sh, name + "_route", G, dict(cfg, tile_expert=tile_expert, tile_row=tile_row, weights=weights))
        views = rows_view = None
        if cfg["CAP"] is None:
            rows_view = cfg["table"].rearrange("(t r) c -> r t c", r=S)
        else:
            HALVES = T // E
            parts = cfg["table"].rearrange("(h r e) c -> h r e c", r=S, e=E)
            views = [(parts[h], slice(h, T, HALVES)) for h in range(HALVES)]
            numbered = m.sem("numbered")
            with nc.Block() as block:
                @block.gpsimd
                def _(pool):
                    nc.gpsimd.iota(tile_expert[:, :].rearrange("p (e h) -> p e h", h=HALVES), [[1, E], [0, HALVES]], base=0,
                                   channel_multiplier=0).then_inc(numbered, 1)
                    pool.wait_ge(numbered, 1)

        def expert(eng, i):
            settle(eng, sh)
            return eng.value_load(tile_expert[0:1, bass.ds(i, 1)], min_val=0, max_val=E - 1)

        experts(nc, sh, name + "_tiles", dict(
            TILES=T, S=S, table=views, rows=rows_view, tile_row=tile_row, unroll=cfg["unroll"], weighted=cfg["weight"] != "one",
            F=F, w1=weights.w1, w2=weights.w2, b1=weights.b1, w_in=weights.loaded, act=cfg["act"], expert=expert))
        with nc.Block() as block:
            @block.sync
            def _(sp):
                sp.dma_start(sh.X[:, :, :], sh.sum_rows[0:sh.NT * P, :].rearrange("(b t) d -> t b d", t=P))\
                  .then_inc(cfg["x_in"], 16)


def blocks_kernel(nc, a, out):
    B = a["x"].shape[0]
    G = B // TG
    F = a["L0_xattn_ffn_w1"].shape[1]
    EPS, EPS_L0 = 1e-5, 1e-6

    E0, K0 = a["L0_ffn_Wg"].shape[1], 2
    T0 = B * K0 + E0
    E2, CAP2, S2 = a["L2_ffn_gate_w"].shape[1], 160, 80
    E3, K3, CAP3 = a["L3_ffn_gate_wT"].shape[1], 6, 128
    spare = E2 * CAP2

    def part(prefix, *names):
        return {n.split("_")[-1].lower(): a[prefix + n] for n in names}

    with ExitStack() as ctx:
        sh = Shared()
        sh.NT = B
        sh.X = ctx.enter_context(nc.sbuf_tensor("X", [P, B, D], F32))
        sh.x_dram, sh.ctx_dram, sh.ctxT_dram = a["x"], a["ctx_1024"], a["ctxT"]
        sh.token_rows = nc.dram_tensor("token_rows", [B * P + spare, D], F32, kind="Internal").ap()
        sh.sum_rows = nc.dram_tensor("sum_rows", [B * P + spare, D], F32, kind="Internal").ap()
        table = lambda i, slots: nc.dram_tensor(f"table{i}", [slots, 2], I32, kind="Internal").ap()
        Memory.used.clear()
        build_constants(nc, sh, ctx)
        zero_rows(nc, sh, ctx)

        with ExitStack() as inner:
            Y = inner.enter_context(nc.sbuf_tensor("Y", [P, B, D], F32))
            attention_heads(nc, sh, "l0sa", G, dict(
                part("L0_xattn_", "sa_wq", "sa_wk", "sa_wv", "sa_wo", "sa_bq", "sa_bk", "sa_bv", "sa_bo"),
                src=sh.X, src_in=sh.x_in[0], dst=Y, base="ln", eps=EPS, ctx=False, mask="full",
                mask_dram=a["mask_Bx1xSxS_ik0"].rearrange("b o q k -> b (o q) k"), scale=DH ** -0.5))
            attention_narrow(nc, sh, "l0ca", G, dict(
                part("L0_xattn_", "ca_wq", "ca_wk", "ca_wv", "ca_wo", "ca_bq", "ca_bk", "ca_bv", "ca_bo"),
                kind="strided", src=Y, dst=Y, eps=EPS_L0, affine=(a["L0_xattn_ln1_g"], a["L0_xattn_ln1_b"]),
                repeats=P - P // H, masked=-1e9, mask_dram=a["mask_Bx1x1xS2_if1"].rearrange("b o q k -> b (o q k)"),
                scale=DH ** -0.5))
            ffn(nc, sh, "l0ff", G, dict(
                part("L0_xattn_", "ffn_w1", "ffn_w2", "ffn_b1", "ffn_b2"),
                src=Y, dst=sh.X, eps=EPS_L0, affine=(a["L0_xattn_ln2_g"], a["L0_xattn_ln2_b"]), F=F, act=ACT.Relu,
                post=(a["L0_xattn_ln3_g"], a["L0_xattn_ln3_b"], EPS_L0)))

        clear_semaphores(nc, Memory.used)

        ffn_all_resident_routed(nc, sh, "l0moe", G, dict(
            part("L0_ffn_", "Wg", "bg", "W1", "b1", "W2", "b2"),
            src=sh.X, eps=EPS, E=E0, K=K0, CAP=None, sb=None, weight="one", table=table(0, (E0 * B + 1) * P),
            trash=([[1, E0 * B + 1]], 0),
            TILES=T0, S=P, F=F, act=ACT.Relu, unroll=2, x_in=sh.x_in[1]))
        clear_semaphores(nc, Memory.used)

        attention_narrow(nc, sh, "l1att", G, dict(
            part("L1_xattn_", "Wq", "Wk", "Wv", "Wo", "bq", "bk", "bv", "bo"),
            kind="single", src=sh.X, src_in=sh.x_in[1], dst=sh.X, eps=EPS, affine=None, scale=D ** -0.5))
        ffn_quantised(nc, sh, "l1ff", G, dict(
            src=sh.X, dst=sh.X, eps=EPS, F=F, act=ACT.Gelu, w1T=a["L1_ffn_W_fcT"], w2T=a["L1_ffn_W_projT"],
            A1=a["L1_ffn_A_fc"], A2=a["L1_ffn_A_proj"], B1T=a["L1_ffn_B_fcT"], B2T=a["L1_ffn_B_projT"],
            b1=a["L1_ffn_b_fc"], b2=a["L1_ffn_b_proj"]))

        clear_semaphores(nc, Memory.used)

        attention_heads(nc, sh, "l2att", G, dict(
            wq=a["L2_xattn_W_qT"], wk=a["L2_xattn_W_kT"], wv=a["L2_xattn_W_vT"], wo=a["L2_xattn_W_oT"],
            bq=None, bk=None, bv=None, bo=None, src=sh.X, dst=sh.X, base="dst", eps=EPS, ctx=True, mask="shared",
            mask_dram=a["mask_shared"], scale=DH ** -0.5))
        ffn_all_resident_routed(nc, sh, "l2moe", G, dict(
            part("L2_ffn_", "w1", "b1", "w2", "b2"), wg=a["L2_ffn_gate_w"], bg=a["L2_ffn_gate_b"],
            src=sh.X, eps=EPS, E=E2, K=1, CAP=CAP2, sb=None, weight="best", table=table(2, E2 * CAP2),
            trash=([[1, E2 * CAP2 // P]], E2 * CAP2 // P), TILES=E2 * CAP2 // S2, S=S2, F=F, act=ACT.Gelu_apprx_tanh,
            unroll=2, x_in=sh.x_in[2]))
        clear_semaphores(nc, Memory.used)

        attention_heads(nc, sh, "l3att", G, dict(
            wq=None, wk=None, wv=None, wo=a["L3_xattn_W_outT"], bq=None, bk=None, bv=None, bo=a["L3_xattn_b_out"],
            src=sh.X, src_in=sh.x_in[2], dst=sh.X, base="dst", eps=EPS, ctx=True, mask=None, scale=D ** -0.5))
        clear_semaphores(nc, Memory.used)
        table3 = table(3, E3 * CAP3)
        route(nc, sh, "l3route", G, dict(
            src=sh.X, eps=EPS, E=E3, K=K3, CAP=CAP3, wg=a["L3_ffn_gate_wT"], bg=None, sb=a["L3_ffn_gate_b"],
            weight="score", b2=None, table=table3, trash=([[0, E3 * CAP3 // P]], 1),
            shared=dict(dst=sh.X, F=a["L3_ffn_ws1T"].shape[1], w1T=a["L3_ffn_ws1T"], w3T=a["L3_ffn_ws3T"],
                        w2T=a["L3_ffn_ws2T"], act=ACT.Silu)))
        experts(nc, sh, "l3moe", dict(
            TILES=E3, S=CAP3, table=[(table3.rearrange("(r e) c -> r e c", e=E3), slice(0, E3))], unroll=4, weighted=True,
            F=a["L3_ffn_w1T"].shape[2], w1T=a["L3_ffn_w1T"], w2T=a["L3_ffn_w2T"], w3T=a["L3_ffn_w3T"], act=ACT.Silu))
        out_stored = Memory(nc, ctx, "out").sem("stored")
        with nc.Block() as block:
            @block.sync
            def _(sp):
                sp.dma_start(out.rearrange("b t d -> (b t) d"), sh.sum_rows[0:B * P, :]).then_inc(out_stored, 16)
                sp.wait_ge(out_stored, 16)


_TRANSPOSED = ["L1_ffn_W_fc", "L1_ffn_W_proj", "L1_ffn_B_fc", "L1_ffn_B_proj", "L2_xattn_W_q", "L2_xattn_W_k",
               "L2_xattn_W_v", "L2_xattn_W_o", "L3_xattn_W_out", "L3_ffn_gate_w", "L3_ffn_w1", "L3_ffn_w2",
               "L3_ffn_w3", "L3_ffn_ws1", "L3_ffn_ws2", "L3_ffn_ws3"]
_OUTS = [((32, 128, 256), "float32")]


def kernel(**inputs):
    import numpy as _np
    import concourse.bacc as _bacc
    from concourse import mybir as _mybir
    from concourse.bass_utils import run_bass_kernel_spmd as _run

    nc = _bacc.Bacc("TRN2", target_bir_lowering=False, num_devices=1)
    laid_out = {}
    for name, value in inputs.items():
        value = _np.asarray(value)
        if name == "mask_1x1xSxS2_bk0":
            laid_out["mask_shared"] = _np.ascontiguousarray(value).reshape(value.shape[2:])
        elif name in _TRANSPOSED:
            laid_out[name + "T"] = _np.swapaxes(value, -1, -2)
        else:
            laid_out[name] = value
    ctx = laid_out["ctx_1024"]
    laid_out["ctxT"] = ctx.transpose(2, 0, 1).reshape(ctx.shape[2], -1)
    arrays, args = {}, {}
    for name, value in laid_out.items():
        arrays[f"in_{name}_dram"] = _np.ascontiguousarray(value)
        args[name] = nc.dram_tensor(f"in_{name}_dram", value.shape, _mybir.dt.from_np(value.dtype), kind="ExternalInput").ap()
    outs = []
    for i, (shape, dtype) in enumerate(_OUTS):
        dt = _mybir.dt.from_np(_np.dtype(dtype))
        outs.append(nc.dram_tensor(f"out_{i}_dram", shape, dt, kind="ExternalOutput").ap())
    blocks_kernel(nc, args, *outs)
    r = _run(nc, [arrays], core_ids=[0])
    return r.results[0]["out_0_dram"]
```
